# Optimizing a Trainium2 kernel written in Bass

```python
import numpy as np
import jax
import jax.numpy as jnp

def _softmax(x, axis=-1):
    return jax.nn.softmax(x, axis=axis)
def _gelu(x):
    return jax.nn.gelu(x, approximate=True)
def _silu(x):
    return jax.nn.silu(x)
def _sigmoid(x):
    return jax.nn.sigmoid(x)
def _layernorm(x, axis=-1, eps=1e-5):
    m = jnp.mean(x, axis=axis, keepdims=True)
    v = jnp.var(x, axis=axis, keepdims=True)
    return (x - m) / jnp.sqrt(v + eps)
def _scatter_add(tgt, idx, src, axis=0):
    return tgt.at[idx].add(src)
def _segment_sum(src, seg, n):
    return jax.ops.segment_sum(src, seg, n)

kernel_name = 'mk_metaformer_d1_conv_nhwc128_d72e9c'

def setup_inputs(seed: int = 0):
    np.random.seed(seed)
    _w = jnp.asarray
    def _rec_inputs():
        import jax
        import jax.numpy as jnp
        _gk = jax.random.key(seed)
        x = 7.22e-05 + 1 * jax.random.normal(jax.random.fold_in(_gk, 1), (4, 128, 128, 128), jnp.float32)
        return x
    x = _rec_inputs()
    def _L0_conv_setup():
        import jax, jax.numpy as jnp
        import numpy as np
        EPS = 1e-06

        def kernel_to_freq_2d(kernel, H, W):
            C, kh, kw = kernel.shape
            th = (jnp.arange(kh) - kh // 2) % H
            tw = (jnp.arange(kw) - kw // 2) % W
            TH, TW = jnp.meshgrid(th, tw, indexing='ij')
            padded = jnp.zeros((C, H, W), dtype=kernel.dtype).at[:, TH, TW].set(kernel)
            return jnp.fft.fft2(padded, axes=(1, 2))

        def heinsen_scan_log(log_coeffs, log_values):

            def op(left, right):
                la, lb = left
                ra, rb = right
                return (la + ra, jnp.logaddexp(ra + lb, rb))
            _, log_h = jax.lax.associative_scan(op, (log_coeffs, log_values), axis=0)
            return log_h
        key = jax.random.key(seed)
        ks = jax.random.split(key, 7)
        B, H, W, C, k = (4, 128, 128, 128, 7)
        fan_in = k * k
        x = jax.random.normal(ks[0], (B, H, W, C), dtype=jnp.float32)
        A_kernel = jax.random.normal(ks[1], (C, k, k), dtype=jnp.float32) / np.sqrt(fan_in)
        B_kernel = jax.random.normal(ks[2], (C, k, k), dtype=jnp.float32) / np.sqrt(fan_in)
        gate_A_kernel = jax.random.normal(ks[3], (C, k, k), dtype=jnp.float32) * 0.02
        gate_B_kernel = jax.random.normal(ks[4], (C, k, k), dtype=jnp.float32) * 0.02
        W_out = jax.random.normal(ks[5], (C, C), dtype=jnp.float32) / np.sqrt(C)
        b_out = jnp.zeros((C,), dtype=jnp.float32)
        return dict(x=x, A_kernel=A_kernel, B_kernel=B_kernel, gate_A_kernel=gate_A_kernel, gate_B_kernel=gate_B_kernel, W_out=W_out, b_out=b_out, T=8)
    _L0_conv_all = _L0_conv_setup()
    _L0_conv_in = {k: v for k, v in _L0_conv_all.items() if k in ('A_kernel', 'B_kernel', 'gate_A_kernel', 'gate_B_kernel', 'W_out', 'b_out', )}
    del _L0_conv_all

    def _L0_ffn_setup():
        import jax, jax.numpy as jnp
        import numpy as np
        B, N, D, C, E, K = (8, 8192, 128, 128, 8, 2)
        key = jax.random.key(seed)
        k0, k1, k2 = jax.random.split(key, 3)
        x = jax.random.normal(k0, (B, N, D), dtype=jnp.float32)
        router_w = jax.random.normal(k1, (D, E), dtype=jnp.float32) * 0.05
        router_b = jnp.zeros((E,), dtype=jnp.float32)
        expert_w = jax.random.normal(k2, (E, D, C), dtype=jnp.float32) * (1.0 / np.sqrt(D))
        expert_b = jnp.zeros((E, C), dtype=jnp.float32)
        return {'x': x, 'router_w': router_w, 'router_b': router_b, 'expert_w': expert_w, 'expert_b': expert_b}
    _L0_ffn_all = _L0_ffn_setup()
    _L0_ffn_in = {k: v for k, v in _L0_ffn_all.items() if k in ('router_w', 'router_b', 'expert_w', 'expert_b', )}
    del _L0_ffn_all

    return {
        "x": x,
        "L0_conv_A_kernel": _L0_conv_in["A_kernel"],
        "L0_conv_B_kernel": _L0_conv_in["B_kernel"],
        "L0_conv_gate_A_kernel": _L0_conv_in["gate_A_kernel"],
        "L0_conv_gate_B_kernel": _L0_conv_in["gate_B_kernel"],
        "L0_conv_W_out": _L0_conv_in["W_out"],
        "L0_conv_b_out": _L0_conv_in["b_out"],
        "L0_ffn_router_w": _L0_ffn_in["router_w"],
        "L0_ffn_router_b": _L0_ffn_in["router_b"],
        "L0_ffn_expert_w": _L0_ffn_in["expert_w"],
        "L0_ffn_expert_b": _L0_ffn_in["expert_b"],
    }

def reference(x, L0_conv_A_kernel, L0_conv_B_kernel, L0_conv_gate_A_kernel, L0_conv_gate_B_kernel, L0_conv_W_out, L0_conv_b_out, L0_ffn_router_w, L0_ffn_router_b, L0_ffn_expert_w, L0_ffn_expert_b):
    import jax
    import jax.numpy as jnp
    def _L0_conv_ref(x, A_kernel, B_kernel, gate_A_kernel, gate_B_kernel, W_out, b_out, T):
        import jax, jax.numpy as jnp
        import numpy as np
        EPS = 1e-06

        def kernel_to_freq_2d(kernel, H, W):
            C, kh, kw = kernel.shape
            th = (jnp.arange(kh) - kh // 2) % H
            tw = (jnp.arange(kw) - kw // 2) % W
            TH, TW = jnp.meshgrid(th, tw, indexing='ij')
            padded = jnp.zeros((C, H, W), dtype=kernel.dtype).at[:, TH, TW].set(kernel)
            return jnp.fft.fft2(padded, axes=(1, 2))

        def heinsen_scan_log(log_coeffs, log_values):

            def op(left, right):
                la, lb = left
                ra, rb = right
                return (la + ra, jnp.logaddexp(ra + lb, rb))
            _, log_h = jax.lax.associative_scan(op, (log_coeffs, log_values), axis=0)
            return log_h
        B, H, W, C = x.shape

        def ifft_real(z_bhwc):
            return jnp.fft.ifft2(z_bhwc.transpose(0, 3, 1, 2), axes=(2, 3)).real.transpose(0, 2, 3, 1)
        A_f = kernel_to_freq_2d(A_kernel, H, W).transpose(1, 2, 0)
        B_f = kernel_to_freq_2d(B_kernel, H, W).transpose(1, 2, 0)
        gA_f = kernel_to_freq_2d(gate_A_kernel, H, W).transpose(1, 2, 0)
        gB_f = kernel_to_freq_2d(gate_B_kernel, H, W).transpose(1, 2, 0)
        x_f = jnp.fft.fft2(x.transpose(0, 3, 1, 2), axes=(2, 3)).transpose(0, 2, 3, 1)
        gate_A = jax.nn.sigmoid(ifft_real(gA_f[None] * x_f))
        gate_B = jax.nn.sigmoid(ifft_real(gB_f[None] * x_f))
        a_spatial = ifft_real(jnp.broadcast_to(A_f[None], (B, H, W, C)))
        b_spatial = ifft_real(B_f[None] * x_f)
        a_t = a_spatial * gate_A
        b_t = b_spatial * gate_B
        gate_seq = jnp.tile(a_t[None], (T, 1, 1, 1, 1))
        h_tilde_seq = jnp.tile(b_t[None], (T, 1, 1, 1, 1))
        log_z = -jax.nn.softplus(-gate_seq)
        log_coeffs = -jax.nn.softplus(gate_seq)
        log_values = log_z + jnp.log(jax.nn.softplus(h_tilde_seq) + EPS)
        log_h = heinsen_scan_log(log_coeffs, log_values)
        h_final = jnp.exp(log_h[-1])
        return h_final @ W_out + b_out

    def _L0_ffn_ref(x, router_w, router_b, expert_w, expert_b):
        import jax, jax.numpy as jnp
        import numpy as np
        B, N, D, C, E, K = (8, 8192, 128, 128, 8, 2)
        router_probs = jax.nn.softmax(x @ router_w + router_b, axis=-1)
        top_p, top_i = jax.lax.top_k(router_probs, K)
        top_p = top_p / jnp.sum(top_p, axis=-1, keepdims=True)
        expert_out = jnp.einsum('bnd,edc->bnec', x, expert_w) + expert_b
        gathered = jnp.take_along_axis(expert_out, top_i[..., None], axis=2)
        return jnp.einsum('bnk,bnkc->bnc', top_p, gathered)

    def _gn(v, G=32, eps=1e-5):
        B_, H_, W_, C_ = v.shape
        g = v.reshape(B_, H_, W_, G, C_ // G)
        m = jnp.mean(g, axis=(1, 2, 4), keepdims=True)
        s = jnp.var(g, axis=(1, 2, 4), keepdims=True)
        return ((g - m) / jnp.sqrt(s + eps)).reshape(v.shape)

    def _ln_c(v, eps=1e-6):
        m = jnp.mean(v, axis=-1, keepdims=True)
        s = jnp.var(v, axis=-1, keepdims=True)
        return (v - m) / jnp.sqrt(s + eps)

    def _ln_t(v, eps=1e-5):
        m = jnp.mean(v, axis=-1, keepdims=True)
        s = jnp.var(v, axis=-1, keepdims=True)
        return (v - m) / jnp.sqrt(s + eps)

    def _to_tokens(v):
        B_, H_, W_, C_ = v.shape
        return v.reshape(B_, H_ * W_, C_)
    def _from_tokens(t, like):
        return t.reshape(like.shape)

    x = x + _L0_conv_ref(_ln_c(x), L0_conv_A_kernel, L0_conv_B_kernel, L0_conv_gate_A_kernel, L0_conv_gate_B_kernel, L0_conv_W_out, L0_conv_b_out, 8)
    t = _to_tokens(x)
    t = t + _L0_ffn_ref(_ln_t(t), L0_ffn_router_w, L0_ffn_router_b, L0_ffn_expert_w, L0_ffn_expert_b)
    x = _from_tokens(t, x)
    return x


_drawn_inputs = setup_inputs


def setup_inputs(seed=0):
    import zlib

    import numpy as np

    out = dict(_drawn_inputs(seed))
    spreads = {'L0_conv_b_out': (0.0, 0.1), 'L0_ffn_router_b': (0.0, 0.1), 'L0_ffn_expert_b': (0.0, 0.1)}
    factors = {}
    for name, (base, spread) in spreads.items():
        noise = np.random.default_rng([zlib.crc32(name.encode()), seed]).standard_normal(out[name].shape)
        drawn = base * np.exp(spread * noise) if base else spread * noise
        out[name] = jnp.asarray(drawn.astype(out[name].dtype))
    for name, factor in factors.items():
        out[name] = (out[name] * factor).astype(out[name].dtype)
    return out
```

```python
import concourse.bass as bass
from concourse import mybir
from contextlib import ExitStack


def metaformer_layer(nc, x, A_kernel, B_kernel, gate_A_kernel, gate_B_kernel, W_out, b_out,
                     router_w, router_b, expert_w, expert_b, out):
    f32, f16, bf16 = mybir.dt.float32, mybir.dt.float16, mybir.dt.bfloat16
    i32, u32 = mybir.dt.int32, mybir.dt.uint32
    ALU = mybir.AluOpType
    ACT = mybir.ActivationFunctionType
    AX = mybir.AxisListType.X

    NB, H, W, C = x.shape
    E = router_w.shape[1]
    KS = A_kernel.shape[1]
    RAD = KS // 2
    STEPS = 8
    PAIR = 2
    PAIRS = NB // PAIR
    R = 4
    QI = H // R
    Q = PAIR * QI
    HP = H + 2 * RAD
    NT = 2 * KS * 2
    SPAN = 16
    DIAG = 2 * (SPAN - 1 + RAD) + 1
    MID = SPAN - 1 + RAD
    GRP = 2
    KSC = 256.0
    EPS_SCAN, EPS1, EPS2 = 1e-6, 1e-6, 1e-5
    F0 = 1.0 - 2.0 ** -STEPS
    CW = 2 * KS - 1
    CR = NB * CW
    HALF = E // 2

    xt = x.rearrange("b h w c -> w (b h) c")
    ot = out.rearrange("b h w c -> w (b h) c")

    ctx = ExitStack()
    with ctx:
        def sb(name, shape, dt):
            return ctx.enter_context(nc.sbuf_tensor(name, shape, dt))

        def pb(name, shape, dt):
            return ctx.enter_context(nc.psum_tensor(name, shape, dt))

        def sem(name):
            return ctx.enter_context(nc.semaphore(name))

        XN = sb("XN", [128, C, PAIR * HP, 2], f16)
        circ = sb("circ", [128, 2 * GRP, W, NT], f16)
        xin = sb("xin", [128, 4, R, C], f32)
        xc = sb("xc", [128, 2, R, C], f32)
        hT = sb("hT", [128, R, W], f32)
        x1 = xin
        xTh = sb("xTh", [128, 2, R, W], f16)
        xTl = sb("xTl", [128, 2, R, W], f16)
        ys = sb("ys", [128, 12 * 256], f32)
        acc = sb("acc", [128, R, C], f32)
        outs = sb("outs", [128, 2, R, C], f32)
        weh = sb("weh", [128, E, C], f16)
        wel = sb("wel", [128, E, C], f16)
        wf = sb("wf", [128, C], f32)
        identf = sb("identf", [128, 128], f32)
        ident = sb("ident", [128, 128], f16)
        mirror = sb("mirror", [128, 128], f16)
        rwh = sb("rwh", [128, E], f16)
        rwl = sb("rwl", [128, E], f16)
        ones3 = sb("ones3", [128, 128], bf16)
        brow = sb("brow", [128, C], bf16)
        bblk = sb("bblk", [96, R, C], f16)
        rb4 = sb("rb4", [128, R, E], f32)
        iota8 = sb("iota8", [128, R, E], f32)
        mhalf = sb("mhalf", [128, 16], f32)
        epst = sb("epst", [128, 2, R], f32)
        NSC = 5
        GB, BB, EW, RW, EB = range(NSC)
        pw2 = sb("pw2", [128, NSC], f32)
        inv = sb("inv", [128, NSC], f32)
        sc = sb("sc", [128, 12], f32)
        KAP, IKAP, NSG, SBV, ISE, SR, SEB, KWE = range(8)
        stats = sb("stats", [128, 2, R, 6], f32)
        mv = sb("mv", [128, 2, R, 2], f32)
        ve = sb("ve", [128, 2, R], f32)
        rstd = sb("rstd", [128, 2, R], f32)
        lg = sb("lg", [128, R, E], f32)
        mx = sb("mx", [128, R, 8], f32)
        mi = sb("mi", [128, R, 8], u32)
        oh1 = sb("oh1", [128, R, E], f32)
        oh2 = sb("oh2", [128, R, E], f32)
        gap = sb("gap", [128, R], f32)
        eg2 = sb("eg2", [128, R], f32)
        wden = sb("wden", [128, R], f32)
        w1 = sb("w1", [128, R], f32)
        w2 = sb("w2", [128, R], f32)
        wt1 = sb("wt1", [128, R, E], f32)
        wt2 = sb("wt2", [128, R, E], f32)
        wsel = sb("wsel", [128, 2, R, E], f32)
        wcat = sb("wcat", [128, 3, R * E], f16)
        wTs = sb("wTs", [96, 128], f16)

        def ytmp(n):
            return ys[:, n * 512:(n + 1) * 512].rearrange("p (s n) -> p s n", s=2)

        t_eg, t_rs, t_v, t_relu, t_l, t_hp = [ytmp(n) for n in range(6)]

        xnf = XN[:, :, :, :].rearrange("p c r l -> p (c r l)").bitcast(f32)
        used = [0]

        def tmp(n):
            used[0] += n
            return xnf[:, used[0] - n:used[0]]

        kraw = tmp(4 * KS * KS).rearrange("p (k i j) -> p k i j", k=4, i=KS)
        ksc = tmp(2 * KS * KS).rearrange("p (k i j) -> p k i j", k=2, i=KS)
        table = tmp(DIAG * NT // 2).bitcast(f16).rearrange("p (d n) -> p d n", n=NT)
        we_raw = tmp(E * C).rearrange("p (e c) -> p e c", e=E)
        we_sc = tmp(E * C).rearrange("p (e c) -> p e c", e=E)
        rw_raw = tmp(E)
        rw_sc = tmp(E)
        w_raw = tmp(C)
        w_abs = tmp(NSC)
        eb_raw = tmp(R * C).rearrange("p (r c) -> p r c", r=R)
        eb_sc = tmp(R * C).rearrange("p (r c) -> p r c", r=R)
        eb_hi = tmp(R * C // 2).bitcast(f16).rearrange("p (r c) -> p r c", r=R)
        diag5 = tmp(NSC)
        colmax = tmp(1)
        onesf = tmp(128)
        brf = tmp(C)
        brd = tmp(2 * C)
        b3 = tmp(3 * C // 2).bitcast(bf16).rearrange("p (k c) -> p k c", k=3)
        cx = tmp(CW * C).rearrange("p (w c) -> p w c", w=CW)
        cxn = tmp(CW * C).rearrange("p (w c) -> p w c", w=CW)
        cst = tmp(CW * 6).rearrange("p (w s) -> p w s", w=CW)
        cmv = tmp(CW * 2).rearrange("p (w s) -> p w s", w=CW)
        cve = tmp(CW)
        crs = tmp(CW)
        cxT = tmp(CW * CR).rearrange("p (w r) -> p w r", w=CW)
        NCV = 3
        ccv = tmp(NCV * KS * CR).rearrange("p (k w r) -> p k w r", k=NCV, w=KS)
        ctm = [tmp(KS * CR) for _ in range(8)]
        cfix = tmp(KS * C).rearrange("p (w c) -> p w c", w=KS)

        PT = pb("PT", [128, R, W], f32)
        PX = pb("PX", [128, R, W], f32)
        PW = pb("PW", [128, R, C], f32)
        PM = pb("PM", [128, 512], f32)
        PY = [pb(f"PY{i}", [128, 512], f32) for i in range(4)]
        PR = PM[:, 0:R * E]
        PWT = PM[0:96, 256:256 + 64].bitcast(f16)

        tbl = nc.dram_tensor("circulant_table", [C, DIAG, NT], f16).ap()
        fixed = nc.dram_tensor("corner_rows", [CR, KS, C], f32).ap()

        weights_in = sem("weights_in")
        corner_in = sem("corner_in")
        zeroed = sem("zeroed")
        consts = sem("consts")
        setup_v = sem("setup_v")
        setup_a = sem("setup_a")
        setup_p = sem("setup_p")
        setup_g = sem("setup_g")
        table_out = sem("table_out")
        brow_in = sem("brow_in")
        fixed_out = sem("fixed_out")
        x_in = [sem(f"x_in{i}") for i in range(4)]
        circ_in = [sem(f"circ_in{i}") for i in range(2)]
        ln_stats = sem("ln_stats")
        ln_aggr = sem("ln_aggr")
        ln_ve = sem("ln_ve")
        ln_rstd = sem("ln_rstd")
        ln_xc = sem("ln_xc")
        ln_hi = sem("ln_hi")
        ln_lo = sem("ln_lo")
        halo = sem("halo")
        conv_done = sem("conv_done")
        gate_exp = sem("gate_exp")
        gate_den = sem("gate_den")
        gate_rec = sem("gate_rec")
        val = sem("val")
        relu = sem("relu")
        absv = sem("absv")
        expn = sem("expn")
        logp = sem("logp")
        h_sum = sem("h_sum")
        h_hi = sem("h_hi")
        h_lo = sem("h_lo")
        x2_in = [sem(f"x2_in{i}") for i in range(4)]
        x2_part = sem("x2_part")
        t1_done = sem("t1_done")
        hT_ready = sem("hT_ready")
        wout_done = sem("wout_done")
        x1_ready = sem("x1_ready")
        st2 = sem("st2")
        ag2 = sem("ag2")
        ve2 = sem("ve2")
        rstd2 = sem("rstd2")
        xc2_ready = sem("xc2_ready")
        t2_done = sem("t2_done")
        xTh_ready = sem("xTh_ready")
        xTl_ready = sem("xTl_ready")
        router_done = sem("router_done")
        lg_ready = sem("lg_ready")
        mx_ready = sem("mx_ready")
        mi_ready = sem("mi_ready")
        oh_ready = sem("oh_ready")
        gap_ready = sem("gap_ready")
        e_ready = sem("e_ready")
        wden_ready = sem("wden_ready")
        w1_ready = sem("w1_ready")
        w2_ready = sem("w2_ready")
        wt_ready = sem("wt_ready")
        w_ready = sem("w_ready")
        wh_ready = sem("wh_ready")
        wcat_ready = sem("wcat_ready")
        wT_done = sem("wT_done")
        wTs_ready = sem("wTs_ready")
        pb_done = sem("pb_done")
        moe_done = sem("moe_done")
        dve_part = sem("dve_part")
        act_part = sem("act_part")
        sum_a = sem("sum_a")
        sum_b = sem("sum_b")
        acc_ready = sem("acc_ready")
        out_ready = sem("out_ready")
        out_sent = [sem(f"out_sent{i}") for i in range(2)]

        block = ctx.enter_context(nc.Block())

        def loop(eng, a, b, step, body, peel=False):
            if peel or b - a <= step:
                for k in range(min(step, b - a)):
                    body(a, k)
                a += step
            if a >= b:
                return
            assert (b - a) % step == 0
            with eng.Fori(0, (b - a) // step, 1) as turn:
                for k in range(step):
                    body(turn * step + a, k)

        def wait_pos(eng, s, value, at_least_one):
            if at_least_one:
                eng.wait_ge(s, value)

        NW_IN = 4 + 3 + 12 + 1 + 1
        PARTS = ((0, CW // 2, H - CW // 2), (CW // 2, CW - CW // 2, 0))

        @block.sync
        def _(sp):
            for k, src in enumerate((gate_B_kernel, B_kernel, gate_A_kernel, A_kernel)):
                sp.dma_start(kraw[:, k], src).then_inc(weights_in, 16)
            sp.dma_start(we_raw, expert_w.rearrange("e d c -> d e c")).then_inc(weights_in, 16)
            sp.dma_start(rw_raw, router_w).then_inc(weights_in, 16)
            sp.dma_start(w_raw, W_out).then_inc(weights_in, 16)
            sp.wait_ge(zeroed, 1)
            for part in range(3):
                for r in range(R):
                    at = (part * R + r) * E
                    sp.dma_start(eb_raw[at:at + E, r], expert_b).then_inc(weights_in, 16)
            sp.dma_start(brf[0:1, :], b_out.rearrange("(o c) -> o c", o=1)).then_inc(weights_in, 16)
            rb_src = bass.AP(tensor=router_b.tensor, offset=0, ap=[[0, 128], [0, R], [1, E]])
            sp.dma_start(rb4[:, :, :], rb_src).then_inc(weights_in, 16)
            for b in range(NB):
                for ph, nh, h0 in PARTS:
                    for pw, nw, w0 in PARTS:
                        at = b * CW + ph
                        sp.dma_start(cx[at:at + nh, pw:pw + nw],
                                     x[b, h0:h0 + nh, w0:w0 + nw, :]).then_inc(corner_in, 16)
            sp.wait_ge(setup_v, S_TABLE)
            sp.dma_start(tbl, table).then_inc(table_out, 16)
            sp.wait_ge(setup_v, S_B3)
            for k in range(3):
                sp.dma_start(brow[k:k + 1, :], b3[0:1, k]).then_inc(brow_in, 16)
            sp.wait_ge(setup_v, S_CFIX)
            sp.dma_start(fixed, cfix[0:CR]).then_inc(fixed_out, 16)
            sp.wait_ge(table_out, 16)
            sp.wait_ge(fixed_out, 16)
            sp.wait_ge(zeroed, 3)

            parts = [0]
            for pair in range(PAIRS):
                n0, m0 = pair * Q, pair * C

                def ln_load(q, k):
                    if not (pair == 0 and isinstance(q, int) and q + k < 4):
                        sp.wait_ge(ln_xc, q + (n0 + k - 3))
                    sp.dma_start(xin[:, k % 4], xt[:, bass.ds((q + (n0 + k)) * R, R), :])\
                      .then_inc(x_in[k % 4], 16)

                if pair:
                    sp.wait_ge(acc_ready, n0)
                loop(sp, 0, 4, 4, ln_load)
                loop(sp, 4, Q, 4, ln_load)

                def circ_load(c, k):
                    slot, g = GRP * k, GRP * k
                    if not (pair == 0 and isinstance(c, int)):
                        sp.wait_ge(conv_done, c + (m0 + g - GRP))

                    def band(p0, w0, w1, wrap=0):
                        v0, v1 = W - w1, W - w0
                        diag = v0 + p0 - (W - 1) + wrap
                        src = bass.AP(tensor=tbl.tensor, offset=(c + g) * (DIAG * NT) + (MID + diag) * NT,
                                      ap=[[NT, SPAN], [DIAG * NT, GRP], [1, (v1 - v0) * NT]])
                        dst = circ[p0:p0 + SPAN, slot:slot + GRP, v0:v1, :].rearrange("p c w n -> p c (w n)")
                        sp.dma_start(dst, src).then_inc(circ_in[k], 16)

                    for p0 in range(0, W, SPAN):
                        band(p0, max(p0 - RAD, 0), min(p0 + SPAN + RAD, W))
                    band(0, W - RAD, W, W)
                    band(W - SPAN, 0, RAD, -W)

                circ_load(0, 0)
                circ_load(0, 1)
                with sp.Fori(1, C // 4, 1) as turn:
                    circ_load(turn * 4, 0)
                    circ_load(turn * 4, 1)

                def x2_load(q, k, first, last):
                    n = q + (n0 + k)
                    slot = k % 4
                    dst = xin[:, slot]
                    src = xt[:, bass.ds(n * R, R), :]
                    if not (first or last):
                        sp.dma_start(dst, src).then_inc(x2_in[slot], 16)
                        return
                    sp.dma_start(dst, src).then_inc(x2_part, 16)
                    parts[0] += 1
                    sp.wait_ge(x2_part, 16 * parts[0])
                    b = (n0 + q + k) // QI
                    rows = (0, R, b * CW + 2 * RAD) if first else (R - RAD, R, b * CW + RAD)
                    r0, r1, f0 = rows
                    sp.dma_start(xin[0:RAD + 1, slot, r0:r1],
                                 fixed[f0:f0 + r1 - r0, RAD:KS].rearrange("r w c -> w r c"))\
                      .then_inc(x2_part, 16)
                    parts[0] += 1
                    sp.wait_ge(x2_part, 16 * parts[0])
                    sp.dma_start(xin[W - RAD:W, slot, r0:r1],
                                 fixed[f0:f0 + r1 - r0, 0:RAD].rearrange("r w c -> w r c"))\
                      .then_inc(x2_in[slot], 16)

                def ahead(q, k, first=False, last=False):
                    sp.wait_ge(acc_ready, q + (n0 + k + 1))
                    x2_load(q, k + 4, first, last)

                def store(q, k):
                    n = q + (n0 + k)
                    sp.wait_ge(out_ready, n + 1)
                    sp.dma_start(ot[:, bass.ds(n * R, R), :], outs[:, k % 2]).then_inc(out_sent[k % 2], 16)

                def both(q, k):
                    ahead(q, k)
                    store(q, k)

                sp.wait_ge(ln_xc, n0 + Q)
                for q in range(4):
                    x2_load(0, q, q == 0, False)
                loop(sp, 0, QI - 8, 4, both)
                for q in range(QI - 8, QI):
                    ahead(0, q, q + 4 == QI, q + 4 == QI - 1)
                    store(0, q)
                loop(sp, QI, Q - 8, 4, both)
                for q in range(Q - 8, Q):
                    if q + 4 < Q:
                        ahead(0, q, False, q + 4 == Q - 1)
                    store(0, q)
            for k in range(2):
                sp.wait_ge(out_sent[k], 16 * PAIRS * Q // 2)

        @block.gpsimd
        def _(g):
            g.memset(eb_raw, 0.0).then_inc(zeroed, 1)
            g.memset(table, 0.0).then_inc(zeroed, 1)
            g.memset(circ[:, :, :, :], 0.0).then_inc(zeroed, 1)
            g.memset(brow[:, :], 0.0).then_inc(zeroed, 1)
            g.memset(ones3[:, :], 1.0)
            g.memset(onesf, 1.0)
            g.memset(mhalf[:, :], -0.5)
            g.memset(epst[:, 0], EPS1)
            g.memset(epst[:, 1], EPS2)
            for e in range(E):
                g.memset(iota8[:, :, e:e + 1], float(e))
            g.memset(w_abs, 0.0)
            g.memset(identf[:, :], 0.0)
            g.memset(mirror[:, :], 0.0)
            g.memset(ident[:, :], 0.0).then_inc(consts, 1)
            g.wait_ge(consts, 1)
            g.affine_select(out=mirror[:, :], in_=mirror[:, :], compare_op=ALU.not_equal, fill=1.0,
                            base=-127, pattern=[[1, 128]], channel_multiplier=1).then_inc(consts, 1)
            for m in (identf, ident):
                g.affine_select(out=m[:, :], in_=m[:, :], compare_op=ALU.not_equal, fill=1.0,
                                base=0, pattern=[[-1, 128]], channel_multiplier=1).then_inc(consts, 1)
            g.wait_ge(setup_v, S_CVE)
            g.tensor_tensor(crs[0:CR], cve[0:CR], mhalf[0:CR, 0:CW], ALU.pow).then_inc(setup_g, 1)

            for pair in range(PAIRS):
                n0, m0 = pair * Q, pair * C

                def ln_root(q, k):
                    n = q + (n0 + k)
                    g.wait_ge(ln_aggr, n + 1)
                    g.tensor_tensor(ve[:, k % 2], mv[:, k % 2, :, 1], epst[:, 0], ALU.add)\
                     .then_inc(ln_ve, 1)
                    g.wait_ge(ln_ve, n + 1)
                    g.tensor_tensor(rstd[:, k % 2], ve[:, k % 2], mhalf[:, 0:R], ALU.pow).then_inc(ln_rstd, 1)

                def ln_low(q, k):
                    n = q + (n0 + k)
                    g.wait_ge(ln_hi, n + 1)
                    at = (q + k) * R + ((q + k) // QI) * (2 * RAD) + RAD
                    view = XN[:, :, bass.ds(at, R), :]
                    g.tensor_tensor(view[:, :, :, 1], xc[:, k % 2].rearrange("p r c -> p c r"),
                                    view[:, :, :, 0], ALU.subtract).then_inc(ln_lo, 1)

                def ln_both(q, k):
                    ln_root(q, k + 1)
                    ln_low(q, k)

                if pair:
                    g.wait_ge(xc2_ready, n0)
                ln_root(0, 0)
                loop(g, 0, Q - 2, 2, ln_both)
                ln_both(0, Q - 2)
                ln_low(0, Q - 1)
                g.wait_ge(ln_lo, n0 + Q)
                xi = XN[:, :, :, :].rearrange("p c (b r) l -> p c b (r l)", b=PAIR).bitcast(i32)
                for b in range(PAIR):
                    g.tensor_copy(xi[:, :, b, 0:RAD], xi[:, :, b, H:H + RAD]).then_inc(halo, 1)
                    g.tensor_copy(xi[:, :, b, H + RAD:HP], xi[:, :, b, RAD:2 * RAD]).then_inc(halo, 1)

                def h_low(c, k):
                    m = c + (m0 + k)
                    g.wait_ge(h_hi, m + 1)
                    view = XN[:, bass.ds(c + k, 1), :, :].rearrange("p o (b r) l -> p (o b) r l", b=PAIR)
                    g.tensor_tensor(view[:, :, RAD:RAD + H, 1],
                                    t_hp[:, k % 2].rearrange("p (b r) -> p b r", b=PAIR),
                                    view[:, :, RAD:RAD + H, 0], ALU.subtract).then_inc(h_lo, 1)

                loop(g, 0, C, 2, h_low)

                def root2(q, k):
                    n = q + (n0 + k)
                    g.wait_ge(ag2, n + 1)
                    g.tensor_tensor(ve[:, k % 2], mv[:, k % 2, :, 1], epst[:, 1], ALU.add)\
                     .then_inc(ve2, 1)
                    g.wait_ge(ve2, n + 1)
                    g.tensor_tensor(rstd[:, k % 2], ve[:, k % 2], mhalf[:, 0:R], ALU.pow).then_inc(rstd2, 1)

                def spread(q, k):
                    n = q + (n0 + k)
                    g.wait_ge(w2_ready, n + 1)
                    s = k % 2
                    g.tensor_tensor(wt1[:, :, :], oh1[:, :, :],
                                    w1[:, :].unsqueeze(2).broadcast_to([128, R, E]), ALU.mult).then_inc(wt_ready, 1)
                    g.tensor_tensor(wt2[:, :, :], oh2[:, :, :],
                                    w2[:, :].unsqueeze(2).broadcast_to([128, R, E]), ALU.mult).then_inc(wt_ready, 1)
                    g.wait_ge(wt_ready, 2 * n + 2)
                    wait_pos(g, acc_ready, n - 1, not (isinstance(q, int) and n < 2))
                    g.tensor_tensor(wsel[:, s], wt1[:, :, :], wt2[:, :, :], ALU.add).then_inc(w_ready, 1)
                    g.wait_ge(w_ready, n + 1)
                    wait_pos(g, wT_done, n, not (isinstance(q, int) and n < 1))
                    wv = wsel[:, s].rearrange("p r e -> p (r e)")
                    kwe = sc[:, KWE:KWE + 1].broadcast_to([128, R * E])
                    for to in (wcat[:, 0], wcat[:, 2], wt1[:, :, :].rearrange("p r e -> p (r e)")):
                        g.tensor_tensor(to, wv, kwe, ALU.mult).then_inc(wh_ready, 1)
                    g.wait_ge(wh_ready, 3 * n + 3)
                    g.tensor_tensor(wcat[:, 1], wt1[:, :, :].rearrange("p r e -> p (r e)"), wcat[:, 0],
                                    ALU.subtract).then_inc(wcat_ready, 1)

                def sum_row(q, k, r):
                    n4 = (q + (n0 + k)) * R + r
                    yr = ys[:, r * 512:(r + 1) * 512]
                    g.wait_ge(act_part, n4 + 1)
                    g.tensor_tensor(yr[:, 0:256], yr[:, 0:256], yr[:, 256:512], ALU.add).then_inc(sum_a, 1)
                    g.wait_ge(sum_a, n4 + 1)
                    g.tensor_tensor(yr[:, 0:128], yr[:, 0:128], yr[:, 128:256], ALU.add).then_inc(sum_b, 1)

                def final(q, k):
                    n = q + (n0 + k)
                    g.wait_ge(sum_b, R * n + R)
                    g.wait_ge(acc_ready, n + 1)
                    if not (isinstance(q, int) and n < 2):
                        g.wait_ge(out_sent[k % 2], ((n - k % 2) // 2) * 16)
                    yv = ys[:, 0:R * 512].rearrange("p (r n) -> p r n", r=R)
                    g.tensor_tensor(outs[:, k % 2], acc[:, :, :], yv[:, :, 0:C], ALU.add).then_inc(out_ready, 1)

                def step(t, k, a2, a1, a0):
                    if a2:
                        root2(t, k + 2)
                    for r in range(R):
                        if a0:
                            sum_row(t, k, r)
                    if a1:
                        spread(t, k + 1)
                    if a0:
                        final(t, k)

                step(0, -2, True, False, False)
                step(0, -1, True, True, False)
                loop(g, 0, Q - 4, 4, lambda t, k: step(t, k, True, True, True),
                     pair == 0)
                for k in range(Q - 4, Q):
                    step(0, k, k + 2 < Q, k + 1 < Q, True)

        @block.scalar
        def _(a):
            def corner(src, dst, func, **kw):
                a.activation(dst, src, func, **kw).then_inc(setup_a, 1)

            a.wait_ge(setup_p, P_CXT)
            corner(PT[:, :, :].rearrange("p r w -> p (r w)")[:, 0:7 * CR],
                   cxT[:, 0:7].rearrange("p w r -> p (w r)"), ACT.Copy)
            corner(PX[:, :, :].rearrange("p r w -> p (r w)")[:, 0:6 * CR],
                   cxT[:, 7:13].rearrange("p w r -> p (w r)"), ACT.Copy)
            flat = [ccv[:, k].rearrange("p w r -> p (w r)") for k in range(NCV)]
            a.wait_ge(setup_v, S_CCONV)
            corner(flat[0], ctm[0], ACT.Exp, scale=-1.0)
            corner(flat[1], ctm[1], ACT.Exp, scale=-1.0)
            a.wait_ge(setup_v, S_CVAL)
            corner(ctm[2], ctm[4], ACT.Abs)
            corner(ctm[3], ctm[6], ACT.Exp)
            a.wait_ge(setup_a, A_ABS)
            corner(ctm[4], ctm[5], ACT.Exp, scale=-1.0)
            a.wait_ge(setup_a, A_EXPN)
            corner(ctm[5], ctm[7], ACT.Ln, bias=1.0)

            for pair in range(PAIRS):
                n0, m0 = pair * Q, pair * C

                def ln_high(q, k):
                    n = q + (n0 + k)
                    a.wait_ge(ln_xc, n + 1)
                    at = (q + k) * R + ((q + k) // QI) * (2 * RAD) + RAD
                    a.activation(XN[:, :, bass.ds(at, R), 0], xc[:, k % 2].rearrange("p r c -> p c r"),
                                 ACT.Copy).then_inc(ln_hi, 1)

                loop(a, 0, Q, 2, ln_high)

                def gate(c, k):
                    m = c + (m0 + k)
                    a.wait_ge(conv_done, m + 1)
                    wait_pos(a, gate_rec, m - 1, not (isinstance(c, int) and m < 2))
                    a.activation(t_eg[:, k % 2], PY[k % 4][:, 0:256], ACT.Exp,
                                 scale=sc[:, NSG:NSG + 1]).then_inc(gate_exp, 1)

                def softplus_log(c, k):
                    m = c + (m0 + k)
                    s = k % 2
                    a.wait_ge(val, m + 1)
                    wait_pos(a, h_sum, m - 1, not (isinstance(c, int) and m < 2))
                    a.activation(t_l[:, s], t_v[:, s], ACT.Abs).then_inc(absv, 1)
                    a.wait_ge(absv, m + 1)
                    a.activation(t_l[:, s], t_l[:, s], ACT.Exp, scale=-1.0).then_inc(expn, 1)
                    a.wait_ge(expn, m + 1)
                    a.activation(t_l[:, s], t_l[:, s], ACT.Ln, bias=1.0).then_inc(logp, 1)

                def conv_end(c, k):
                    gate(c, k + 1)
                    softplus_log(c, k)

                gate(0, 0)
                loop(a, 0, C - 4, 4, conv_end, pair == 0)
                for k in range(C - 4, C - 1):
                    conv_end(0, k)
                softplus_log(0, C - 1)

                def h_copy(q, k):
                    n = q + (n0 + k)
                    a.wait_ge(t1_done, n + 1)
                    wait_pos(a, wout_done, n, not (isinstance(q, int) and n < 1))
                    a.activation(hT[:, :, :], PT[:, :, :], ACT.Copy).then_inc(hT_ready, 1)

                def x_high(q, k):
                    n = q + (n0 + k)
                    a.wait_ge(t2_done, n + 1)
                    wait_pos(a, moe_done, (n - 1) * R, not (isinstance(q, int) and n < 2))
                    a.activation(xTh[:, k % 2], PX[:, :, :], ACT.Copy).then_inc(xTh_ready, 1)

                def w_copy(q, k):
                    n = q + (n0 + k)
                    a.wait_ge(wT_done, n + 1)
                    wait_pos(a, pb_done, n, not (isinstance(q, int) and n < 1))
                    a.activation(wTs[:, :], PWT, ACT.Copy).then_inc(wTs_ready, 1)

                def weigh(q, k, r):
                    n = q + (n0 + k)
                    a.wait_ge(moe_done, n * R + r + 1)
                    a.wait_ge(w_ready, n + 1)
                    wait_pos(a, out_ready, n, not (isinstance(q, int) and n < 1))
                    py = PY[2 * (r % 2) + 1]
                    for e in range(HALF):
                        ins = a.activation(ys[:, r * 512 + e * C:r * 512 + (e + 1) * C],
                                           py[:, e * C:(e + 1) * C], ACT.Copy,
                                           scale=wsel[:, k % 2, r, HALF + e:HALF + e + 1])
                    ins.then_inc(act_part, 1)

                def gap_exp(q, k):
                    n = q + (n0 + k)
                    a.wait_ge(gap_ready, n + 1)
                    a.activation(eg2[:, :], gap[:, :], ACT.Exp).then_inc(e_ready, 1)

                def step(t, k, a2, a1, a0):
                    if a2:
                        h_copy(t, k + 2)
                    if a0:
                        weigh(t, k, 0)
                        w_copy(t, k)
                    if a1:
                        x_high(t, k + 1)
                    if a0:
                        weigh(t, k, 1)
                        weigh(t, k, 2)
                    if a1:
                        gap_exp(t, k + 1)
                    if a0:
                        weigh(t, k, 3)

                step(0, -2, True, False, False)
                step(0, -1, True, True, False)
                loop(a, 0, Q - 4, 4, lambda t, k: step(t, k, True, True, True),
                     pair == 0)
                for k in range(Q - 4, Q):
                    step(0, k, k + 2 < Q, k + 1 < Q, True)

        @block.vector
        def _(v):
            done = [0]

            def setup(ins):
                done[0] += 1
                ins.then_inc(setup_v, 1)
                v.wait_ge(setup_v, done[0])

            def after(name):
                assert done[0] == SETUP[name], (name, done[0])

            v.wait_ge(weights_in, 16 * NW_IN)
            v.wait_ge(consts, 4)
            v.wait_ge(zeroed, 4)
            for col, src in ((GB, kraw[:, 0]), (BB, kraw[:, 1])):
                setup(v.tensor_reduce(w_abs[:, col:col + 1], src.rearrange("p i j -> p (i j)"), AX, ALU.max,
                                      apply_absolute_value=True))
            setup(v.tensor_reduce(w_abs[:, EW:EW + 1], we_raw.rearrange("p e c -> p (e c)"), AX, ALU.max,
                                  apply_absolute_value=True))
            setup(v.tensor_reduce(w_abs[:, RW:RW + 1], rw_raw, AX, ALU.max, apply_absolute_value=True))
            setup(v.tensor_reduce(w_abs[0:96, EB:EB + 1], eb_raw[0:96].rearrange("p r c -> p (r c)"), AX,
                                  ALU.max, apply_absolute_value=True))
            after("ABS")
            v.wait_ge(setup_p, P_ABST)
            setup(v.tensor_reduce(colmax[0:NSC], PM[0:NSC, 0:128], AX, ALU.max))
            setup(v.tensor_scalar(diag5[0:NSC], identf[0:NSC, 0:NSC], colmax[0:NSC, 0:1], None, ALU.mult))
            after("DIAG")
            v.wait_ge(setup_p, P_MAX)
            setup(v.tensor_scalar(pw2[:, :], PM[:, 128:128 + NSC], 2.0 ** -60, None, ALU.max))
            setup(v.tensor_scalar(pw2[:, :].bitcast(i32), pw2[:, :].bitcast(i32), 0x7F800000, None,
                                  ALU.bitwise_and))
            setup(v.reciprocal(inv[:, :], pw2[:, :]))

            def scale(dst, src, *ops):
                (o1, v1), (o2, v2) = ops if len(ops) == 2 else (ops[0], (None, None))
                if o2 is None:
                    setup(v.tensor_scalar(sc[:, dst:dst + 1], src, v1, None, o1))
                else:
                    setup(v.tensor_scalar(sc[:, dst:dst + 1], src, v1, v2, o1, o2))

            WS = 1.0 / KSC
            scale(IKAP, pw2[:, BB:BB + 1], (ALU.mult, 1.0 / 32), (ALU.max, 1.0))
            setup(v.reciprocal(sc[:, KAP:KAP + 1], sc[:, IKAP:IKAP + 1]))
            scale(NSG, pw2[:, GB:GB + 1], (ALU.mult, -WS))
            scale(SBV, pw2[:, BB:BB + 1], (ALU.mult, WS))
            scale(ISE, inv[:, EW:EW + 1], (ALU.mult, 1.0 / WS))
            scale(SR, pw2[:, RW:RW + 1], (ALU.mult, WS))
            scale(SEB, pw2[:, EB:EB + 1], (ALU.mult, KSC ** -2))
            scale(KWE, sc[:, ISE:ISE + 1], (ALU.mult, KSC))
            for k, col in ((0, GB), (1, BB)):
                setup(v.tensor_scalar(ksc[:, k], kraw[:, k], inv[:, col:col + 1], KSC, ALU.mult, ALU.mult))
            for k in range(2):
                cell = table[:, MID - RAD:MID + RAD + 1, k * 2 * KS:(k + 1) * 2 * KS]
                cell = cell.rearrange("p j (i l) -> p i j l", l=2)
                setup(v.tensor_copy(cell[:, :, :, 0], ksc[:, k, :, ::-1]))
                setup(v.tensor_tensor(cell[:, :, :, 1], ksc[:, k, :, ::-1], cell[:, :, :, 0], ALU.subtract))
            after("TABLE")
            setup(v.tensor_scalar(we_sc, we_raw, inv[:, EW:EW + 1], KSC, ALU.mult, ALU.mult))
            setup(v.tensor_copy(weh[:, :, :], we_sc))
            setup(v.tensor_tensor(wel[:, :, :], we_sc, weh[:, :, :], ALU.subtract))
            setup(v.tensor_scalar(rw_sc, rw_raw, inv[:, RW:RW + 1], KSC, ALU.mult, ALU.mult))
            setup(v.tensor_copy(rwh[:, :], rw_sc))
            setup(v.tensor_tensor(rwl[:, :], rw_sc, rwh[:, :], ALU.subtract))
            setup(v.tensor_scalar(eb_sc[0:96], eb_raw[0:96], inv[0:96, EB:EB + 1], KSC, ALU.mult, ALU.mult))
            setup(v.tensor_copy(eb_hi[0:96], eb_sc[0:96]))
            setup(v.tensor_copy(bblk[0:64], eb_hi[0:64]))
            setup(v.tensor_tensor(bblk[64:96], eb_sc[64:96], eb_hi[64:96], ALU.subtract))
            setup(v.tensor_scalar(wf[:, :], w_raw, F0, None, ALU.mult))
            v.wait_ge(setup_p, P_COLSUM)
            setup(v.scalar_tensor_tensor(out=brd[0:1, 0:C], in0=PM[0:1, 256:256 + C], scalar=F0 * EPS_SCAN,
                                         in1=brf[0:1, :], op0=ALU.mult, op1=ALU.add))
            setup(v.tensor_scalar(brd[0:1, 0:C], brd[0:1, 0:C], sc[0:1, KAP:KAP + 1], None, ALU.mult))
            for k in range(3):
                setup(v.tensor_copy(b3[0:1, k], brd[0:1, 0:C]))
                if k < 2:
                    setup(v.tensor_tensor(brd[0:1, 0:C], brd[0:1, 0:C], b3[0:1, k], ALU.subtract))
            after("B3")

            v.wait_ge(corner_in, 16 * 4 * NB)
            for w in range(CW):
                ins = v.bn_stats(cst[0:CR, w], cx[0:CR, w])
            setup(ins)
            for w in range(CW):
                ins = v.bn_aggr(cmv[0:CR, w], cst[0:CR, w])
            setup(ins)
            setup(v.tensor_scalar(cve[0:CR], cmv[0:CR, :, 1], EPS1, None, ALU.add))
            after("CVE")
            v.wait_ge(setup_g, 1)
            for w in range(CW):
                ins = v.tensor_scalar(cxn[0:CR, w], cx[0:CR, w], cmv[0:CR, w, 0:1], crs[0:CR, w:w + 1],
                                      ALU.subtract, ALU.mult)
            setup(ins)
            after("CXN")
            v.wait_ge(setup_a, A_CXT)
            L = CR - 2 * RAD
            setup(v.memset(ccv, 0.0))
            for j in range(KS):
                for i in range(KS):
                    for k, kern in enumerate((0, 2, 1)):
                        into = ccv[:, k, :, RAD:RAD + L]
                        ins = v.scalar_tensor_tensor(
                            out=into, in0=cxT[:, 2 * RAD - j:2 * RAD - j + KS, 2 * RAD - i:2 * RAD - i + L],
                            scalar=kraw[:, kern, i, j:j + 1], in1=into, op0=ALU.mult, op1=ALU.add)
                        if k == NCV - 1:
                            setup(ins)
            after("CCONV")
            v.wait_ge(setup_a, A_GATES)
            for k in range(2):
                setup(v.tensor_scalar(ctm[k], ctm[k], 1.0, None, ALU.add))
                setup(v.reciprocal(ctm[k], ctm[k]))
            setup(v.tensor_tensor(ctm[2], ccv[:, 2].rearrange("p w r -> p (w r)"), ctm[0], ALU.mult))
            setup(v.memset(ctm[3], 0.0))
            ta = ctm[3].rearrange("p (w b r) -> p w b r", w=KS, b=NB)
            tg = ctm[1].rearrange("p (w b r) -> p w b r", w=KS, b=NB)
            for b in range(NB):
                ins = v.tensor_tensor(ta[:, :, b, RAD:RAD + KS], tg[:, :, b, RAD:RAD + KS],
                                      kraw[:, 3].rearrange("p i j -> p j i"), ALU.mult)
            setup(ins)
            after("CVAL")
            v.wait_ge(setup_a, A_LN)
            setup(v.scalar_tensor_tensor(out=ctm[0], in0=ctm[2], scalar=0.0, in1=ctm[7], op0=ALU.max,
                                         op1=ALU.add))
            setup(v.tensor_scalar(ctm[6], ctm[6], 1.0, None, ALU.add))
            setup(v.reciprocal(ctm[1], ctm[6]))
            setup(v.tensor_scalar(ctm[2], ctm[1], -1.0, 1.0, ALU.mult, ALU.add))
            power = ctm[1]
            free = [ctm[4], ctm[5]]
            terms = 1
            while terms < STEPS:
                setup(v.scalar_tensor_tensor(out=ctm[2], in0=power, scalar=1.0, in1=ctm[2], op0=ALU.add,
                                             op1=ALU.mult))
                terms *= 2
                if terms < STEPS:
                    nxt = free.pop(0)
                    setup(v.tensor_tensor(nxt, power, power, ALU.mult))
                    power = nxt
            setup(v.tensor_scalar(ctm[2], ctm[2], -F0, None, ALU.add))
            setup(v.scalar_tensor_tensor(out=ctm[3], in0=ctm[0], scalar=EPS_SCAN, in1=ctm[2], op0=ALU.add,
                                         op1=ALU.mult))
            after("CDELTA")
            v.wait_ge(setup_p, P_CW)
            for half, bank in ((0, PY[0]), (1, PY[1])):
                lo, hi = (0, 4) if half == 0 else (4, KS)
                setup(v.tensor_tensor(cfix[0:CR, lo:hi], cx[0:CR, RAD + lo:RAD + hi],
                                      bank[0:CR, 0:(hi - lo) * C].rearrange("p (w c) -> p w c", c=C), ALU.add))
            after("CFIX")

            for pair in range(PAIRS):
                n0, m0 = pair * Q, pair * C

                def ln_stat(q, k):
                    n = q + (n0 + k)
                    nd = n // 4 if isinstance(n, int) else (q + n0) // 4 + k // 4
                    v.wait_ge(x_in[k % 4], nd * 16 + 16)
                    for r in range(R):
                        ins = v.bn_stats(stats[:, k % 2, r], xin[:, k % 4, r])
                    ins.then_inc(ln_stats, 1)

                def ln_moments(q, k):
                    for r in range(R):
                        ins = v.bn_aggr(mv[:, k % 2, r], stats[:, k % 2, r])
                    ins.then_inc(ln_aggr, 1)

                def ln_apply(q, k):
                    n = q + (n0 + k)
                    v.wait_ge(ln_rstd, n + 1)
                    wait_pos(v, ln_lo, n - 1, not (isinstance(q, int) and n < 2))
                    for r in range(R):
                        ins = v.tensor_scalar(xc[:, k % 2, r], xin[:, k % 4, r], mv[:, k % 2, r, 0:1],
                                              rstd[:, k % 2, r:r + 1], ALU.subtract, ALU.mult)
                    ins.then_inc(ln_xc, 1)

                def ln_both(q, k):
                    ln_stat(q, k + 1)
                    v.wait_ge(ln_stats, q + (n0 + k + 2))
                    ln_apply(q, k)
                    ln_moments(q, k + 1)

                if pair == 0:
                    v.wait_ge(fixed_out, 16)
                    v.wait_ge(brow_in, 48)
                    v.wait_ge(table_out, 16)
                ln_stat(0, 0)
                v.wait_ge(ln_stats, n0 + 1)
                ln_moments(0, 0)
                loop(v, 0, Q - 4, 4, ln_both, pair == 0)
                for k in range(Q - 4, Q - 1):
                    ln_both(0, k)
                ln_apply(0, Q - 1)

                def value(c, k):
                    m = c + (m0 + k)
                    s = k % 2
                    v.wait_ge(gate_exp, m + 1)
                    v.tensor_scalar(t_eg[:, s], t_eg[:, s], 1.0, None, ALU.add).then_inc(gate_den, 1)
                    v.wait_ge(gate_den, m + 1)
                    v.reciprocal(t_rs[:, s], t_eg[:, s]).then_inc(gate_rec, 1)
                    v.wait_ge(gate_rec, m + 1)
                    wait_pos(v, absv, m - 1, not (isinstance(c, int) and m < 2))
                    v.scalar_tensor_tensor(out=t_v[:, s], in0=PY[k % 4][:, 256:512], scalar=sc[:, SBV:SBV + 1],
                                           in1=t_rs[:, s], op0=ALU.mult, op1=ALU.mult).then_inc(val, 1)
                    v.wait_ge(val, m + 1)
                    v.tensor_scalar(t_relu[:, s], t_v[:, s], sc[:, KAP:KAP + 1], 0.0, ALU.mult, ALU.max)\
                     .then_inc(relu, 1)

                def finish(c, k):
                    m = c + (m0 + k)
                    s = k % 2
                    v.wait_ge(logp, m + 1)
                    v.wait_ge(relu, m + 1)
                    wait_pos(v, h_lo, m - 1, not (isinstance(c, int) and m < 2))
                    v.scalar_tensor_tensor(out=t_hp[:, s], in0=t_l[:, s], scalar=sc[:, KAP:KAP + 1],
                                           in1=t_relu[:, s], op0=ALU.mult, op1=ALU.add).then_inc(h_sum, 1)
                    v.wait_ge(h_sum, m + 1)
                    view = XN[:, bass.ds(c + k, 1), :, :].rearrange("p o (b r) l -> p (o b) r l", b=PAIR)
                    v.tensor_copy(view[:, :, RAD:RAD + H, 0],
                                  t_hp[:, s].rearrange("p (b r) -> p b r", b=PAIR)).then_inc(h_hi, 1)

                def conv_end(c, k):
                    value(c, k + 1)
                    finish(c, k)

                value(0, 0)
                loop(v, 0, C - 4, 4, conv_end, pair == 0)
                for k in range(C - 4, C - 1):
                    conv_end(0, k)
                finish(0, C - 1)

                def residual(q, k):
                    n = q + (n0 + k)
                    nd = n // 4 if isinstance(n, int) else (q + n0) // 4 + k // 4
                    v.wait_ge(wout_done, n + 1)
                    v.wait_ge(x2_in[k % 4], nd * 16 + 16)
                    v.scalar_tensor_tensor(out=x1[:, k % 4], in0=PW[:, :, :], scalar=sc[:, IKAP:IKAP + 1],
                                           in1=xin[:, k % 4], op0=ALU.mult, op1=ALU.add).then_inc(x1_ready, 1)
                    v.wait_ge(x1_ready, n + 1)
                    for r in range(R):
                        ins = v.bn_stats(stats[:, k % 2, r], x1[:, k % 4, r])
                    ins.then_inc(st2, 1)

                def moments(q, k):
                    for r in range(R):
                        ins = v.bn_aggr(mv[:, k % 2, r], stats[:, k % 2, r])
                    ins.then_inc(ag2, 1)

                def apply2(q, k):
                    n = q + (n0 + k)
                    v.wait_ge(rstd2, n + 1)
                    wait_pos(v, t2_done, n - 1, not (isinstance(q, int) and n < 2))
                    for r in range(R):
                        ins = v.tensor_scalar(xc[:, k % 2, r], x1[:, k % 4, r], mv[:, k % 2, r, 0:1],
                                              rstd[:, k % 2, r:r + 1], ALU.subtract, ALU.mult)
                    ins.then_inc(xc2_ready, 1)

                def x_low(q, k):
                    n = q + (n0 + k)
                    v.wait_ge(xTh_ready, n + 1)
                    v.tensor_tensor(xTl[:, k % 2], PX[:, :, :], xTh[:, k % 2], ALU.subtract)\
                     .then_inc(xTl_ready, 1)

                def route(q, k):
                    n = q + (n0 + k)
                    v.wait_ge(router_done, n + 1)
                    v.scalar_tensor_tensor(out=lg[:, :, :].rearrange("p r e -> p (r e)"), in0=PR,
                                           scalar=sc[:, SR:SR + 1],
                                           in1=rb4[:, :, :].rearrange("p r e -> p (r e)"),
                                           op0=ALU.mult, op1=ALU.add).then_inc(lg_ready, 1)

                def choose(q, k):
                    n = q + (n0 + k)
                    for r in range(R):
                        ins = v.max(mx[:, r], lg[:, r])
                    ins.then_inc(mx_ready, 1)
                    v.wait_ge(mx_ready, n + 1)
                    v.tensor_tensor(gap[:, :], mx[:, :, 1], mx[:, :, 0], ALU.subtract).then_inc(gap_ready, 1)
                    for r in range(R):
                        ins = v.max_index(mi[:, r], mx[:, r], lg[:, r])
                    ins.then_inc(mi_ready, 1)
                    v.wait_ge(mi_ready, n + 1)
                    wait_pos(v, wt_ready, 2 * n, not (isinstance(q, int) and n < 1))
                    for o, j in ((oh1, 0), (oh2, 1)):
                        ins = v.tensor_tensor(o[:, :, :], iota8[:, :, :],
                                              mi[:, :, j:j + 1].broadcast_to([128, R, E]), ALU.is_equal)
                    ins.then_inc(oh_ready, 1)

                def shares(q, k):
                    n = q + (n0 + k)
                    v.wait_ge(e_ready, n + 1)
                    v.tensor_scalar(wden[:, :], eg2[:, :], 1.0, sc[:, ISE:ISE + 1], ALU.add, ALU.mult)\
                     .then_inc(wden_ready, 1)
                    v.wait_ge(wden_ready, n + 1)
                    v.reciprocal(w1[:, :], wden[:, :]).then_inc(w1_ready, 1)
                    v.wait_ge(w1_ready, n + 1)
                    v.tensor_tensor(w2[:, :], eg2[:, :], w1[:, :], ALU.mult).then_inc(w2_ready, 1)

                def weigh(q, k, r):
                    n = q + (n0 + k)
                    v.wait_ge(moe_done, n * R + r + 1)
                    v.wait_ge(w_ready, n + 1)
                    wait_pos(v, out_ready, n, not (isinstance(q, int) and n < 1))
                    py = PY[2 * (r % 2)]
                    for e in range(HALF):
                        if e:
                            v.wait_ge(dve_part, (n * R + r) * HALF + e)
                        v.scalar_tensor_tensor(out=acc[:, r], in0=py[:, e * C:(e + 1) * C],
                                               scalar=wsel[:, k % 2, r, e:e + 1],
                                               in1=acc[:, r] if e else x1[:, k % 4, r],
                                               op0=ALU.mult, op1=ALU.add).then_inc(dve_part, 1)

                def bias(q, k):
                    n = q + (n0 + k)
                    v.wait_ge(pb_done, n + 1)
                    v.wait_ge(dve_part, (n + 1) * R * HALF)
                    v.scalar_tensor_tensor(out=acc[:, :, :], in0=PW[:, :, :], scalar=sc[:, SEB:SEB + 1],
                                           in1=acc[:, :, :], op0=ALU.mult, op1=ALU.add).then_inc(acc_ready, 1)

                def step(t, k, a2, a1, a0):
                    if a2:
                        residual(t, k + 2)
                        v.wait_ge(st2, t + (n0 + k + 3))
                    if a0:
                        weigh(t, k, 0)
                    if a2:
                        moments(t, k + 2)
                    if a1:
                        x_low(t, k + 1)
                    if a0:
                        weigh(t, k, 1)
                    if a2:
                        apply2(t, k + 2)
                    if a1:
                        route(t, k + 1)
                        v.wait_ge(lg_ready, t + (n0 + k + 2))
                    if a0:
                        weigh(t, k, 2)
                    if a1:
                        choose(t, k + 1)
                    if a0:
                        weigh(t, k, 3)
                    if a1:
                        shares(t, k + 1)
                    if a0:
                        bias(t, k)

                step(0, -2, True, False, False)
                step(0, -1, True, True, False)
                loop(v, 0, Q - 4, 4, lambda t, k: step(t, k, True, True, True),
                     pair == 0)
                for k in range(Q - 4, Q):
                    step(0, k, k + 2 < Q, k + 1 < Q, True)

        @block.tensor
        def _(p):
            p.wait_ge(consts, 4)
            p.wait_ge(setup_v, S_ABS)
            p.transpose(PM[0:NSC, 0:128], w_abs, identf[:, :]).then_inc(setup_p, 1)
            p.wait_ge(setup_v, S_DIAG)
            p.matmul(PM[:, 128:128 + NSC], onesf[0:NSC, :], diag5[0:NSC], start=True, stop=True)\
             .then_inc(setup_p, 1)
            p.wait_ge(setup_v, S_DIAG + 1)
            p.matmul(PM[0:1, 256:256 + C], onesf[:, 0:1], w_raw, start=True, stop=True).then_inc(setup_p, 1)
            p.wait_ge(setup_v, S_CXN)
            for w in range(CW):
                bank, at = (PT, w) if w < 7 else (PX, w - 7)
                ins = p.transpose(bank[:, :, :].rearrange("p r w -> p (r w)")[:, at * CR:(at + 1) * CR],
                                  cxn[0:CR, w], identf[0:CR, 0:CR])
            ins.then_inc(setup_p, 1)
            p.wait_ge(setup_v, S_CDELTA)
            dh = ctm[3].rearrange("p (w r) -> p w r", w=KS)
            for w in range(KS):
                ins = p.matmul(PY[w // 4][0:CR, (w % 4) * C:(w % 4 + 1) * C], dh[:, w], w_raw, start=True,
                               stop=True)
            ins.then_inc(setup_p, 1)

            for pair in range(PAIRS):
                n0, m0 = pair * Q, pair * C

                def conv(c, k):
                    m = c + (m0 + k)
                    cg = (c + m0) // 4
                    p.wait_ge(circ_in[(k % 4) // GRP], (cg + (k // 4 + 1)) * (16 * 10))
                    wait_pos(p, val, m - 3, not (isinstance(c, int) and m < 4))
                    view = XN[:, bass.ds(c + k, 1), :, :].rearrange("p o (b r) l -> p (o b) r l", b=PAIR)
                    for cv in range(2):
                        into = PY[k % 4][:, cv * 256:(cv + 1) * 256].rearrange("p (b r) -> p b r", b=PAIR)
                        for i in range(KS):
                            for part, (wl, xl) in enumerate(((0, 0), (0, 1), (1, 0))):
                                ins = p.matmul(into, circ[:, k % 4, :, (cv * KS + i) * 2 + wl],
                                               view[:, :, 2 * RAD - i:2 * RAD - i + H, xl],
                                               start=(i == 0 and part == 0), stop=(i == KS - 1 and part == 2))
                    ins.then_inc(conv_done, 1)

                p.wait_ge(halo, 2 * PAIR * (pair + 1))
                if pair == 0:
                    p.wait_ge(setup_v, S_CFIX)
                else:
                    p.wait_ge(act_part, n0 * R)
                    p.wait_ge(dve_part, n0 * R * HALF)
                loop(p, 0, C, 4, conv, pair == 0)

                def turn_h(q, k):
                    n = q + (n0 + k)
                    wait_pos(p, hT_ready, n, not (isinstance(q, int) and n < 1))
                    at = (q + k) * R + ((q + k) // QI) * (2 * RAD) + RAD
                    for r in range(R):
                        for part in range(2):
                            src = XN[:, :, bass.ds(at + r, 1), part].rearrange("p c o -> p (c o)")
                            ins = p.matmul(PT[:, r], src, mirror[:, :], start=part == 0, stop=part == 1)
                    ins.then_inc(t1_done, 1)

                def project(q, k):
                    n = q + (n0 + k)
                    p.wait_ge(hT_ready, n + 1)
                    wait_pos(p, x1_ready, n, not (isinstance(q, int) and n < 1))
                    wait_pos(p, acc_ready, n - 2, not (isinstance(q, int) and n < 3))
                    for r in range(R):
                        p.matmul(PW[:, r], ones3[:, :], brow[:, :], start=True, stop=False)
                        ins = p.matmul(PW[:, r], hT[:, r], wf[:, :], start=False, stop=True)
                    ins.then_inc(wout_done, 1)

                def turn_x(q, k):
                    n = q + (n0 + k)
                    p.wait_ge(xc2_ready, n + 1)
                    wait_pos(p, xTl_ready, n, not (isinstance(q, int) and n < 1))
                    for r in range(R):
                        ins = p.transpose(PX[:, r], xc[:, k % 2, r], identf[:, :])
                    ins.then_inc(t2_done, 1)

                def router(q, k):
                    n = q + (n0 + k)
                    p.wait_ge(xTl_ready, n + 1)
                    wait_pos(p, wTs_ready, n, not (isinstance(q, int) and n < 1))
                    for r in range(R):
                        into = PR[:, r * E:(r + 1) * E]
                        p.matmul(into, xTh[:, k % 2, r], rwh[:, :], start=True, stop=False)
                        p.matmul(into, xTh[:, k % 2, r], rwl[:, :], start=False, stop=False)
                        ins = p.matmul(into, xTl[:, k % 2, r], rwh[:, :], start=False, stop=True)
                    ins.then_inc(router_done, 1)

                def turn_w(q, k):
                    n = q + (n0 + k)
                    p.wait_ge(wcat_ready, n + 1)
                    p.transpose(PWT, wcat[:, :, :].rearrange("p k e -> p (k e)"), ident[:, :]).then_inc(wT_done, 1)

                def bias(q, k, ahead):
                    n = q + (n0 + k)
                    p.wait_ge(wTs_ready, n + 1)
                    p.wait_ge(x1_ready, n + 1 + ahead)
                    p.matmul(PW[:, :, :], wTs[:, :], bblk[:, :, :], start=True, stop=True).then_inc(pb_done, 1)

                def experts(q, k, r):
                    n4 = (q + (n0 + k)) * R + r
                    if not (isinstance(q, int) and n4 < 2):
                        p.wait_ge(act_part, n4 - 1)
                        p.wait_ge(dve_part, (n4 - 1) * HALF)
                    b0, b1 = PY[2 * (r % 2)], PY[2 * (r % 2) + 1]
                    wh = [weh[:, s * HALF:(s + 1) * HALF].rearrange("p e c -> p (e c)") for s in range(2)]
                    wl = [wel[:, s * HALF:(s + 1) * HALF].rearrange("p e c -> p (e c)") for s in range(2)]
                    hi, lo = xTh[:, k % 2, r], xTl[:, k % 2, r]
                    for s, bank in ((0, b0), (1, b1)):
                        p.matmul(bank[:, :], hi, wh[s], start=True, stop=False)
                        p.matmul(bank[:, :], hi, wl[s], start=False, stop=False)
                        ins = p.matmul(bank[:, :], lo, wh[s], start=False, stop=True)
                    ins.then_inc(moe_done, 1)

                def step(t, k, a2, a1, a0):
                    if a2:
                        turn_h(t, k + 2)
                    if a0:
                        experts(t, k, 0)
                        turn_w(t, k)
                    if a2:
                        project(t, k + 2)
                    if a1:
                        turn_x(t, k + 1)
                    if a0:
                        experts(t, k, 1)
                    if a1:
                        router(t, k + 1)
                    if a0:
                        experts(t, k, 2)
                        bias(t, k, 2 if a2 else 1 if a1 else 0)
                        experts(t, k, 3)

                p.wait_ge(h_lo, m0 + C)
                step(0, -2, True, False, False)
                step(0, -1, True, True, False)
                loop(p, 0, Q - 4, 4, lambda t, k: step(t, k, True, True, True),
                     pair == 0)
                for k in range(Q - 4, Q):
                    step(0, k, k + 2 < Q, k + 1 < Q, True)


SETUP = {"ABS": 5, "DIAG": 7, "TABLE": 24, "B3": 42, "CVE": 45, "CXN": 46, "CCONV": 96, "CVAL": 103,
         "CDELTA": 114, "CFIX": 116}
S_ABS, S_DIAG, S_TABLE, S_B3, S_CVE, S_CXN, S_CCONV, S_CVAL, S_CDELTA, S_CFIX = SETUP.values()
P_ABST, P_MAX, P_COLSUM, P_CXT, P_CW = 1, 2, 3, 4, 5
A_CXT, A_GATES, A_ABS, A_EXPN, A_LN = 2, 4, 6, 7, 8

_INS = ["x", "L0_conv_A_kernel", "L0_conv_B_kernel", "L0_conv_gate_A_kernel", "L0_conv_gate_B_kernel",
        "L0_conv_W_out", "L0_conv_b_out", "L0_ffn_router_w", "L0_ffn_router_b", "L0_ffn_expert_w",
        "L0_ffn_expert_b"]


def kernel(**inputs):
    import numpy as _np
    import concourse.bacc as _bacc
    from concourse import mybir as _mybir
    from concourse.bass_utils import run_bass_kernel_spmd as _run

    nc = _bacc.Bacc("TRN2", target_bir_lowering=False, num_devices=1)
    arrays, args = {}, []
    for name in _INS:
        a = _np.ascontiguousarray(inputs[name])
        arrays[f"in_{name}_dram"] = a
        args.append(nc.dram_tensor(f"in_{name}_dram", a.shape, _mybir.dt.from_np(a.dtype),
                                   kind="ExternalInput").ap())
    args.append(nc.dram_tensor("out_dram", inputs["x"].shape, _mybir.dt.float32, kind="ExternalOutput").ap())
    metaformer_layer(nc, *args)
    r = _run(nc, [arrays], core_ids=[0])
    return r.results[0]["out_dram"]
```

```python
import concourse.bass as bass
from concourse import mybir
from contextlib import ExitStack


def metaformer_layer(nc, x, A_kernel, B_kernel, gate_A_kernel, gate_B_kernel, W_out, b_out,
                     router_w, router_b, expert_w, expert_b, out):
    f32, f16, bf16 = mybir.dt.float32, mybir.dt.float16, mybir.dt.bfloat16
    i32, u32 = mybir.dt.int32, mybir.dt.uint32
    ALU = mybir.AluOpType
    ACT = mybir.ActivationFunctionType
    AX = mybir.AxisListType.X

    NB, H, W, C = x.shape
    E = router_w.shape[1]
    KS = A_kernel.shape[1]
    RAD = KS // 2
    STEPS = 8
    PAIR = 2
    PAIRS = NB // PAIR
    R = 4
    QI = H // R
    Q = PAIR * QI
    HP = H + 2 * RAD
    NT = 2 * KS * 2
    SPAN = 16
    DIAG = 2 * (SPAN - 1 + RAD) + 1
    MID = SPAN - 1 + RAD
    GRP = 2
    KSC = 256.0
    EPS_SCAN, EPS1, EPS2 = 1e-6, 1e-6, 1e-5
    F0 = 1.0 - 2.0 ** -STEPS
    CW = 2 * KS - 1
    CR = NB * CW
    HALF = E // 2
    LN_EXP_SET = 6
    DVE_LN = 2

    def dve_rows(k):
        return R - 1 if k % 2 == 0 else R

    xt = x.rearrange("b h w c -> w (b h) c")
    ot = out.rearrange("b h w c -> w (b h) c")

    ctx = ExitStack()
    with ctx:
        def sb(name, shape, dt):
            return ctx.enter_context(nc.sbuf_tensor(name, shape, dt))

        def pb(name, shape, dt):
            return ctx.enter_context(nc.psum_tensor(name, shape, dt))

        def sem(name):
            return ctx.enter_context(nc.semaphore(name))

        XN = sb("XN", [128, C, PAIR * HP, 2], f16)
        circ = sb("circ", [128, 2 * GRP, W, NT], f16)
        xin = sb("xin", [128, 4, R, C], f32)
        xc = sb("xc", [128, 2, R, C], f32)
        hT = sb("hT", [128, R, W], f32)
        x1 = xin
        xTh = sb("xTh", [128, 2, R, W], f16)
        xTl = sb("xTl", [128, 2, R, W], f16)
        ys = sb("ys", [128, 12 * 256], f32)
        ysum = sb("ysum", [128, R, C], f32)
        outs = sb("outs", [128, 2, R, C], f32)
        acc = outs
        weh = sb("weh", [128, E, C], f16)
        wel = sb("wel", [128, E, C], f16)
        wf = sb("wf", [128, C], f32)
        identf = sb("identf", [128, 128], f32)
        ident = sb("ident", [128, 128], f16)
        mirror = sb("mirror", [128, 128], f16)
        rwh = sb("rwh", [128, E], f16)
        rwl = sb("rwl", [128, E], f16)
        ones3 = sb("ones3", [128, 128], bf16)
        brow = sb("brow", [128, C], bf16)
        bblk = sb("bblk", [96, R, C], f16)
        rb4 = sb("rb4", [128, R, E], f32)
        iota8 = sb("iota8", [128, R, E], f32)
        mhalf = sb("mhalf", [128, 16], f32)
        epst = sb("epst", [128, 2, R], f32)
        NSC = 5
        GB, BB, EW, RW, EB = range(NSC)
        pw2 = sb("pw2", [128, NSC], f32)
        inv = sb("inv", [128, NSC], f32)
        sc = sb("sc", [128, 12], f32)
        KAP, IKAP, NSG, SBV, ISE, SR, SEB, KWE = range(8)
        stats = sb("stats", [128, 2, R, 6], f32)
        mv = sb("mv", [128, 2, R, 2], f32)
        ve = sb("ve", [128, 2, R], f32)
        rstd = sb("rstd", [128, 2, R], f32)
        lg = sb("lg", [128, R, E], f32)
        mx = sb("mx", [128, R, 8], f32)
        mi = sb("mi", [128, R, 8], u32)
        oh1 = sb("oh1", [128, R, E], f32)
        oh2 = sb("oh2", [128, R, E], f32)
        gap = sb("gap", [128, R], f32)
        eg2 = sb("eg2", [128, R], f32)
        wden = sb("wden", [128, R], f32)
        w1 = sb("w1", [128, R], f32)
        w2 = sb("w2", [128, R], f32)
        wt1 = sb("wt1", [128, R, E], f32)
        wt2 = sb("wt2", [128, R, E], f32)
        wsel = sb("wsel", [128, 2, R, E], f32)
        nmr = sb("nmr", [128, 2, R], f32)
        wscl = sb("wscl", [128, R * E], f32)
        wcat = sb("wcat", [128, 3, R * E], f16)
        wTs = sb("wTs", [96, 128], f16)

        def ytmp(n):
            return ys[:, n * 512:(n + 1) * 512].rearrange("p (s n) -> p s n", s=2)

        t_eg, t_rs, t_v, t_relu, t_l, t_hp = [ytmp(n) for n in range(6)]

        xnf = XN[:, :, :, :].rearrange("p c r l -> p (c r l)").bitcast(f32)
        used = [0]

        def tmp(n):
            used[0] += n
            return xnf[:, used[0] - n:used[0]]

        kraw = tmp(4 * KS * KS).rearrange("p (k i j) -> p k i j", k=4, i=KS)
        ksc = tmp(2 * KS * KS).rearrange("p (k i j) -> p k i j", k=2, i=KS)
        table = tmp(DIAG * NT // 2).bitcast(f16).rearrange("p (d n) -> p d n", n=NT)
        we_raw = tmp(E * C).rearrange("p (e c) -> p e c", e=E)
        we_sc = tmp(E * C).rearrange("p (e c) -> p e c", e=E)
        rw_raw = tmp(E)
        rw_sc = tmp(E)
        w_raw = tmp(C)
        w_abs = tmp(NSC)
        eb_raw = tmp(R * C).rearrange("p (r c) -> p r c", r=R)
        eb_sc = tmp(R * C).rearrange("p (r c) -> p r c", r=R)
        eb_hi = tmp(R * C // 2).bitcast(f16).rearrange("p (r c) -> p r c", r=R)
        diag5 = tmp(NSC)
        colmax = tmp(1)
        onesf = tmp(128)
        brf = tmp(C)
        brd = tmp(2 * C)
        b3 = tmp(3 * C // 2).bitcast(bf16).rearrange("p (k c) -> p k c", k=3)
        cx = tmp(CW * C).rearrange("p (w c) -> p w c", w=CW)
        cxn = tmp(CW * C).rearrange("p (w c) -> p w c", w=CW)
        cst = tmp(CW * 6).rearrange("p (w s) -> p w s", w=CW)
        cmv = tmp(CW * 2).rearrange("p (w s) -> p w s", w=CW)
        cve = tmp(CW)
        crs = tmp(CW)
        cxT = tmp(CW * CR).rearrange("p (w r) -> p w r", w=CW)
        NCV = 3
        ccv = tmp(NCV * KS * CR).rearrange("p (k w r) -> p k w r", k=NCV, w=KS)
        ctm = [tmp(KS * CR) for _ in range(8)]
        cfix = tmp(KS * C).rearrange("p (w c) -> p w c", w=KS)

        PT = pb("PT", [128, R, W], f32)
        PX = pb("PX", [128, R, W], f32)
        PW = pb("PW", [128, R, C], f32)
        PM = pb("PM", [128, 512], f32)
        PY = [pb(f"PY{i}", [128, 512], f32) for i in range(4)]
        PR = PM[:, 0:R * E]
        PWT = PM[0:96, 256:256 + 64].bitcast(f16)

        tbl = nc.dram_tensor("circulant_table", [C, DIAG, NT], f16).ap()
        fixed = nc.dram_tensor("corner_rows", [CR, KS, C], f32).ap()

        weights_in = sem("weights_in")
        corner_in = sem("corner_in")
        zeroed = sem("zeroed")
        consts = sem("consts")
        setup_v = sem("setup_v")
        setup_a = sem("setup_a")
        setup_p = sem("setup_p")
        setup_g = sem("setup_g")
        table_out = sem("table_out")
        brow_in = sem("brow_in")
        fixed_out = sem("fixed_out")
        x_in = [sem(f"x_in{i}") for i in range(4)]
        circ_in = [sem(f"circ_in{i}") for i in range(2)]
        ln_stats = sem("ln_stats")
        ln_aggr = sem("ln_aggr")
        ln_ve = sem("ln_ve")
        ln_rstd = sem("ln_rstd")
        ln_xc = sem("ln_xc")
        ln_hi = sem("ln_hi")
        ln_lo = sem("ln_lo")
        halo = sem("halo")
        nmr_ready = sem("nmr_ready")
        ln_xa = sem("ln_xa")
        conv_done = sem("conv_done")
        gate_exp = sem("gate_exp")
        gate_den = sem("gate_den")
        gate_rec = sem("gate_rec")
        val = sem("val")
        relu = sem("relu")
        absv = sem("absv")
        expn = sem("expn")
        logp = sem("logp")
        h_sum = sem("h_sum")
        h_hi = sem("h_hi")
        h_lo = sem("h_lo")
        x2_in = [sem(f"x2_in{i}") for i in range(4)]
        x2_part = sem("x2_part")
        t1_done = sem("t1_done")
        hT_ready = sem("hT_ready")
        wout_done = sem("wout_done")
        x1_ready = sem("x1_ready")
        st2 = sem("st2")
        ag2 = sem("ag2")
        ve2 = sem("ve2")
        rstd2 = sem("rstd2")
        nmr2 = sem("nmr2")
        wscl_ready = sem("wscl_ready")
        xc2_ready = sem("xc2_ready")
        t2_done = sem("t2_done")
        xTh_ready = sem("xTh_ready")
        xTl_ready = sem("xTl_ready")
        router_done = sem("router_done")
        lg_ready = sem("lg_ready")
        mx_ready = sem("mx_ready")
        mi_ready = sem("mi_ready")
        oh_ready = sem("oh_ready")
        gap_ready = sem("gap_ready")
        e_ready = sem("e_ready")
        wden_ready = sem("wden_ready")
        w1_ready = sem("w1_ready")
        w2_ready = sem("w2_ready")
        wt_ready = sem("wt_ready")
        w_ready = sem("w_ready")
        wh_ready = sem("wh_ready")
        wcat_ready = sem("wcat_ready")
        wT_done = sem("wT_done")
        wTs_ready = sem("wTs_ready")
        pb_done = sem("pb_done")
        moe_done = sem("moe_done")
        dve_part = sem("dve_part")
        act_part = sem("act_part")
        sum_a = sem("sum_a")
        sum_b = sem("sum_b")
        sum_8 = sem("sum_8")
        acc_ready = sem("acc_ready")
        out_ready = sem("out_ready")
        out_sent = [sem(f"out_sent{i}") for i in range(2)]

        block = ctx.enter_context(nc.Block())

        def loop(eng, a, b, step, body, peel=False):
            if peel or b - a <= step:
                for k in range(min(step, b - a)):
                    body(a, k)
                a += step
            if a >= b:
                return
            assert (b - a) % step == 0
            with eng.Fori(0, (b - a) // step, 1) as turn:
                for k in range(step):
                    body(turn * step + a, k)

        def wait_pos(eng, s, value, at_least_one):
            if at_least_one:
                eng.wait_ge(s, value)

        NW_IN = 4 + 3 + 12 + 1 + 1
        PARTS = ((0, CW // 2, H - CW // 2), (CW // 2, CW - CW // 2, 0))

        @block.sync
        def _(sp):
            for k, src in enumerate((gate_B_kernel, B_kernel, gate_A_kernel, A_kernel)):
                sp.dma_start(kraw[:, k], src).then_inc(weights_in, 16)
            sp.dma_start(we_raw, expert_w.rearrange("e d c -> d e c")).then_inc(weights_in, 16)
            sp.dma_start(rw_raw, router_w).then_inc(weights_in, 16)
            sp.dma_start(w_raw, W_out).then_inc(weights_in, 16)
            sp.wait_ge(zeroed, 1)
            for part in range(3):
                for r in range(R):
                    at = (part * R + r) * E
                    sp.dma_start(eb_raw[at:at + E, r], expert_b).then_inc(weights_in, 16)
            sp.dma_start(brf[0:1, :], b_out.rearrange("(o c) -> o c", o=1)).then_inc(weights_in, 16)
            rb_src = bass.AP(tensor=router_b.tensor, offset=0, ap=[[0, 128], [0, R], [1, E]])
            sp.dma_start(rb4[:, :, :], rb_src).then_inc(weights_in, 16)
            for b in range(NB):
                for ph, nh, h0 in PARTS:
                    for pw, nw, w0 in PARTS:
                        at = b * CW + ph
                        sp.dma_start(cx[at:at + nh, pw:pw + nw],
                                     x[b, h0:h0 + nh, w0:w0 + nw, :]).then_inc(corner_in, 16)
            sp.wait_ge(setup_v, S_TABLE)
            sp.dma_start(tbl, table).then_inc(table_out, 16)
            sp.wait_ge(setup_v, S_B3)
            for k in range(3):
                sp.dma_start(brow[k:k + 1, :], b3[0:1, k]).then_inc(brow_in, 16)
            sp.wait_ge(setup_v, S_CFIX)
            sp.dma_start(fixed, cfix[0:CR]).then_inc(fixed_out, 16)
            sp.wait_ge(table_out, 16)
            sp.wait_ge(fixed_out, 16)
            sp.wait_ge(zeroed, 3)

            parts = [0]
            for pair in range(PAIRS):
                n0, m0 = pair * Q, pair * C

                def ln_load(q, k):
                    if not (pair == 0 and isinstance(q, int) and q + k < 4):
                        sp.wait_ge(ln_hi, q + (n0 + k - 3))
                    sp.dma_start(xin[:, k % 4], xt[:, bass.ds((q + (n0 + k)) * R, R), :])\
                      .then_inc(x_in[k % 4], 16)

                if pair:
                    sp.wait_ge(acc_ready, n0)
                loop(sp, 0, 4, 4, ln_load)
                loop(sp, 4, Q, 4, ln_load)

                def circ_load(c, k):
                    slot, g = GRP * k, GRP * k
                    if not (pair == 0 and isinstance(c, int)):
                        sp.wait_ge(conv_done, c + (m0 + g - GRP))

                    def band(p0, w0, w1, wrap=0):
                        v0, v1 = W - w1, W - w0
                        diag = v0 + p0 - (W - 1) + wrap
                        src = bass.AP(tensor=tbl.tensor, offset=(c + g) * (DIAG * NT) + (MID + diag) * NT,
                                      ap=[[NT, SPAN], [DIAG * NT, GRP], [1, (v1 - v0) * NT]])
                        dst = circ[p0:p0 + SPAN, slot:slot + GRP, v0:v1, :].rearrange("p c w n -> p c (w n)")
                        sp.dma_start(dst, src).then_inc(circ_in[k], 16)

                    for p0 in range(0, W, SPAN):
                        band(p0, max(p0 - RAD, 0), min(p0 + SPAN + RAD, W))
                    band(0, W - RAD, W, W)
                    band(W - SPAN, 0, RAD, -W)

                circ_load(0, 0)
                circ_load(0, 1)
                with sp.Fori(1, C // 4, 1) as turn:
                    circ_load(turn * 4, 0)
                    circ_load(turn * 4, 1)

                def x2_load(q, k, first, last):
                    n = q + (n0 + k)
                    slot = k % 4
                    dst = xin[:, slot]
                    src = xt[:, bass.ds(n * R, R), :]
                    if not (first or last):
                        sp.dma_start(dst, src).then_inc(x2_in[slot], 16)
                        return
                    sp.dma_start(dst, src).then_inc(x2_part, 16)
                    parts[0] += 1
                    sp.wait_ge(x2_part, 16 * parts[0])
                    b = (n0 + q + k) // QI
                    rows = (0, R, b * CW + 2 * RAD) if first else (R - RAD, R, b * CW + RAD)
                    r0, r1, f0 = rows
                    sp.dma_start(xin[0:RAD + 1, slot, r0:r1],
                                 fixed[f0:f0 + r1 - r0, RAD:KS].rearrange("r w c -> w r c"))\
                      .then_inc(x2_part, 16)
                    parts[0] += 1
                    sp.wait_ge(x2_part, 16 * parts[0])
                    sp.dma_start(xin[W - RAD:W, slot, r0:r1],
                                 fixed[f0:f0 + r1 - r0, 0:RAD].rearrange("r w c -> w r c"))\
                      .then_inc(x2_in[slot], 16)

                def ahead(q, k, first=False, last=False):
                    sp.wait_ge(acc_ready, q + (n0 + k + 1))
                    x2_load(q, k + 4, first, last)

                def store(q, k):
                    n = q + (n0 + k)
                    sp.wait_ge(out_ready, n + 1)
                    sp.dma_start(ot[:, bass.ds(n * R, R), :], outs[:, k % 2]).then_inc(out_sent[k % 2], 16)

                def both(q, k):
                    ahead(q, k)
                    store(q, k)

                sp.wait_ge(ln_hi, n0 + Q)
                for q in range(4):
                    x2_load(0, q, q == 0, False)
                loop(sp, 0, QI - 8, 4, both)
                for q in range(QI - 8, QI):
                    ahead(0, q, q + 4 == QI, q + 4 == QI - 1)
                    store(0, q)
                loop(sp, QI, Q - 8, 4, both)
                for q in range(Q - 8, Q):
                    if q + 4 < Q:
                        ahead(0, q, False, q + 4 == Q - 1)
                    store(0, q)
            for k in range(2):
                sp.wait_ge(out_sent[k], 16 * PAIRS * Q // 2)

        @block.gpsimd
        def _(g):
            g.memset(eb_raw, 0.0).then_inc(zeroed, 1)
            g.memset(table, 0.0).then_inc(zeroed, 1)
            g.memset(circ[:, :, :, :], 0.0).then_inc(zeroed, 1)
            g.memset(brow[:, :], 0.0).then_inc(zeroed, 1)
            g.memset(ones3[:, :], 1.0)
            g.memset(onesf, 1.0)
            g.memset(mhalf[:, :], -0.5)
            g.memset(epst[:, 0], EPS1)
            g.memset(epst[:, 1], EPS2)
            for e in range(E):
                g.memset(iota8[:, :, e:e + 1], float(e))
            g.memset(w_abs, 0.0)
            g.memset(identf[:, :], 0.0)
            g.memset(mirror[:, :], 0.0)
            g.memset(ident[:, :], 0.0).then_inc(consts, 1)
            g.wait_ge(consts, 1)
            g.affine_select(out=mirror[:, :], in_=mirror[:, :], compare_op=ALU.not_equal, fill=1.0,
                            base=-127, pattern=[[1, 128]], channel_multiplier=1).then_inc(consts, 1)
            for m in (identf, ident):
                g.affine_select(out=m[:, :], in_=m[:, :], compare_op=ALU.not_equal, fill=1.0,
                                base=0, pattern=[[-1, 128]], channel_multiplier=1).then_inc(consts, 1)
            g.wait_ge(setup_v, S_CVE)
            g.tensor_tensor(crs[0:CR], cve[0:CR], mhalf[0:CR, 0:CW], ALU.pow).then_inc(setup_g, 1)

            for pair in range(PAIRS):
                n0, m0 = pair * Q, pair * C

                def ln_root(q, k):
                    n = q + (n0 + k)
                    g.wait_ge(ln_aggr, n + 1)
                    g.tensor_tensor(ve[:, k % 2], mv[:, k % 2, :, 1], epst[:, 0], ALU.add)\
                     .then_inc(ln_ve, 1)
                    g.wait_ge(ln_ve, n + 1)
                    g.tensor_tensor(rstd[:, k % 2], ve[:, k % 2], mhalf[:, 0:R], ALU.pow).then_inc(ln_rstd, 1)

                def ln_low(q, k):
                    n = q + (n0 + k)
                    g.wait_ge(ln_hi, n + 1)
                    at = (q + k) * R + ((q + k) // QI) * (2 * RAD) + RAD
                    view = XN[:, :, bass.ds(at, R), :]
                    g.tensor_tensor(view[:, :, :, 1], xc[:, k % 2].rearrange("p r c -> p c r"),
                                    view[:, :, :, 0], ALU.subtract).then_inc(ln_lo, 1)

                def ln_both(q, k):
                    ln_root(q, k + 1)
                    ln_low(q, k)

                if pair:
                    g.wait_ge(xc2_ready, n0)
                ln_root(0, 0)
                loop(g, 0, Q - 2, 2, ln_both)
                ln_both(0, Q - 2)
                ln_low(0, Q - 1)
                g.wait_ge(ln_lo, n0 + Q)
                xi = XN[:, :, :, :].rearrange("p c (b r) l -> p c b (r l)", b=PAIR).bitcast(i32)
                for b in range(PAIR):
                    g.tensor_copy(xi[:, :, b, 0:RAD], xi[:, :, b, H:H + RAD]).then_inc(halo, 1)
                    g.tensor_copy(xi[:, :, b, H + RAD:HP], xi[:, :, b, RAD:2 * RAD]).then_inc(halo, 1)

                def h_low(c, k):
                    m = c + (m0 + k)
                    g.wait_ge(h_hi, m + 1)
                    view = XN[:, bass.ds(c + k, 1), :, :].rearrange("p o (b r) l -> p (o b) r l", b=PAIR)
                    g.tensor_tensor(view[:, :, RAD:RAD + H, 1],
                                    t_hp[:, k % 2].rearrange("p (b r) -> p b r", b=PAIR),
                                    view[:, :, RAD:RAD + H, 0], ALU.subtract).then_inc(h_lo, 1)

                loop(g, 0, C, 2, h_low)

                def root2(q, k):
                    n = q + (n0 + k)
                    g.wait_ge(ag2, n + 1)
                    g.tensor_tensor(ve[:, k % 2], mv[:, k % 2, :, 1], epst[:, 1], ALU.add)\
                     .then_inc(ve2, 1)
                    g.wait_ge(ve2, n + 1)
                    g.tensor_tensor(rstd[:, k % 2], ve[:, k % 2], mhalf[:, 0:R], ALU.pow).then_inc(rstd2, 1)

                def spread(q, k):
                    n = q + (n0 + k)
                    s = k % 2
                    g.wait_ge(w2_ready, n + 1)
                    g.tensor_tensor(wt1[:, :, :], oh1[:, :, :],
                                    w1[:, :].unsqueeze(2).broadcast_to([128, R, E]), ALU.mult).then_inc(wt_ready, 1)
                    g.tensor_tensor(wt2[:, :, :], oh2[:, :, :],
                                    w2[:, :].unsqueeze(2).broadcast_to([128, R, E]), ALU.mult).then_inc(wt_ready, 1)
                    g.wait_ge(wt_ready, 2 * n + 2)
                    wait_pos(g, acc_ready, n - 1, not (isinstance(q, int) and n < 2))
                    g.tensor_tensor(wsel[:, s], wt1[:, :, :], wt2[:, :, :], ALU.add).then_inc(w_ready, 1)

                def spread_low(q, k):
                    n = q + (n0 + k)
                    g.wait_ge(wh_ready, n + 1)
                    g.tensor_tensor(wcat[:, 1], wscl[:, :], wcat[:, 0], ALU.subtract).then_inc(wcat_ready, 1)

                def sum_row(q, k, r):
                    n = q + (n0 + k)
                    yr = ys[:, r * 512:(r + 2) * 512] if r >= dve_rows(k) else ys[:, r * 512:(r + 1) * 512]
                    g.wait_ge(act_part, n * R + r + 1)
                    if r >= dve_rows(k):
                        g.tensor_tensor(yr[:, 0:512], yr[:, 0:512], yr[:, 512:1024], ALU.add).then_inc(sum_8, 1)
                        count = n // 2 if isinstance(n, int) else (q + n0) // 2 + k // 2
                        g.wait_ge(sum_8, count + 1)
                    g.tensor_tensor(yr[:, 0:256], yr[:, 0:256], yr[:, 256:512], ALU.add).then_inc(sum_a, 1)
                    g.wait_ge(sum_a, n * R + r + 1)
                    wait_pos(g, out_ready, n, not (isinstance(q, int) and n < 1))
                    g.tensor_tensor(ysum[:, r], yr[:, 0:128], yr[:, 128:256], ALU.add).then_inc(sum_b, 1)

                def final(q, k):
                    n = q + (n0 + k)
                    g.wait_ge(sum_b, R * n + R)
                    g.wait_ge(acc_ready, n + 1)
                    g.tensor_tensor(outs[:, k % 2], acc[:, k % 2], ysum[:, :, :], ALU.add).then_inc(out_ready, 1)

                def step(t, k, a3, a2, a1, a0):
                    if a0:
                        sum_row(t, k, 0)
                        sum_row(t, k, 1)
                    if a2:
                        root2(t, k + 2)
                    if a0:
                        sum_row(t, k, 2)
                    if a1:
                        spread(t, k + 1)
                    if a0:
                        sum_row(t, k, 3)
                        final(t, k)
                    if a1:
                        spread_low(t, k + 1)

                for k in (-3, -2, -1):
                    step(0, k, True, k > -3, k > -2, False)
                loop(g, 0, Q - 4, 4, lambda t, k: step(t, k, True, True, True, True), pair == 0)
                for k in range(Q - 4, Q):
                    step(0, k, k + 3 < Q, k + 2 < Q, k + 1 < Q, True)

        @block.scalar
        def _(a):
            a.add_instruction(mybir.InstLoadActFuncSet(
                name=nc.get_next_instruction_name(), act_func_set_id=LN_EXP_SET, ins=[], outs=[],
                engine=mybir.EngineType.Activation))

            def corner(src, dst, func, **kw):
                a.activation(dst, src, func, **kw).then_inc(setup_a, 1)

            a.wait_ge(setup_p, P_CXT)
            corner(PT[:, :, :].rearrange("p r w -> p (r w)")[:, 0:7 * CR],
                   cxT[:, 0:7].rearrange("p w r -> p (w r)"), ACT.Copy)
            corner(PX[:, :, :].rearrange("p r w -> p (r w)")[:, 0:6 * CR],
                   cxT[:, 7:13].rearrange("p w r -> p (w r)"), ACT.Copy)
            flat = [ccv[:, k].rearrange("p w r -> p (w r)") for k in range(NCV)]
            a.wait_ge(setup_v, S_CCONV)
            corner(flat[0], ctm[0], ACT.Exp, scale=-1.0)
            corner(flat[1], ctm[1], ACT.Exp, scale=-1.0)
            a.wait_ge(setup_v, S_CVAL)
            corner(ctm[2], ctm[4], ACT.Abs)
            corner(ctm[3], ctm[6], ACT.Exp)
            a.wait_ge(setup_a, A_ABS)
            corner(ctm[4], ctm[5], ACT.Exp, scale=-1.0)
            a.wait_ge(setup_a, A_EXPN)
            corner(ctm[5], ctm[7], ACT.Ln, bias=1.0)

            for pair in range(PAIRS):
                n0, m0 = pair * Q, pair * C

                def ln_high(q, k):
                    n = q + (n0 + k)
                    a.wait_ge(nmr_ready, n + 1)
                    wait_pos(a, ln_lo, n - 1, not (isinstance(q, int) and n < 2))
                    for r in range(DVE_LN, R):
                        ins = a.activation(xc[:, k % 2, r], xin[:, k % 4, r], ACT.Identity,
                                           scale=rstd[:, k % 2, r:r + 1], bias=nmr[:, k % 2, r:r + 1])
                    ins.then_inc(ln_xa, 1)
                    a.wait_ge(ln_xc, n + 1)
                    a.wait_ge(ln_xa, n + 1)
                    at = (q + k) * R + ((q + k) // QI) * (2 * RAD) + RAD
                    a.activation(XN[:, :, bass.ds(at, R), 0], xc[:, k % 2].rearrange("p r c -> p c r"),
                                 ACT.Copy).then_inc(ln_hi, 1)

                loop(a, 0, Q, 4, ln_high, pair == 0)

                def gate(c, k):
                    m = c + (m0 + k)
                    a.wait_ge(conv_done, m + 1)
                    wait_pos(a, gate_rec, m - 1, not (isinstance(c, int) and m < 2))
                    a.activation(t_eg[:, k % 2], PY[k % 4][:, 0:256], ACT.Exp,
                                 scale=sc[:, NSG:NSG + 1]).then_inc(gate_exp, 1)

                def softplus_log(c, k):
                    m = c + (m0 + k)
                    s = k % 2
                    a.wait_ge(val, m + 1)
                    wait_pos(a, h_sum, m - 1, not (isinstance(c, int) and m < 2))
                    a.activation(t_l[:, s], t_v[:, s], ACT.Abs).then_inc(absv, 1)
                    a.wait_ge(absv, m + 1)
                    a.activation(t_l[:, s], t_l[:, s], ACT.Exp, scale=-1.0).then_inc(expn, 1)
                    a.wait_ge(expn, m + 1)
                    a.activation(t_l[:, s], t_l[:, s], ACT.Ln, bias=1.0).then_inc(logp, 1)

                def conv_end(c, k):
                    gate(c, k + 1)
                    softplus_log(c, k)

                gate(0, 0)
                loop(a, 0, C - 4, 4, conv_end, pair == 0)
                for k in range(C - 4, C - 1):
                    conv_end(0, k)
                softplus_log(0, C - 1)

                def h_copy(q, k):
                    n = q + (n0 + k)
                    a.wait_ge(t1_done, n + 1)
                    wait_pos(a, wout_done, n, not (isinstance(q, int) and n < 1))
                    a.activation(hT[:, :, :], PT[:, :, :], ACT.Copy).then_inc(hT_ready, 1)

                def x_high(q, k):
                    n = q + (n0 + k)
                    a.wait_ge(t2_done, n + 1)
                    wait_pos(a, moe_done, (n - 1) * R, not (isinstance(q, int) and n < 2))
                    a.activation(xTh[:, k % 2], PX[:, :, :], ACT.Copy).then_inc(xTh_ready, 1)

                def w_copy(q, k):
                    n = q + (n0 + k)
                    a.wait_ge(wT_done, n + 1)
                    wait_pos(a, pb_done, n, not (isinstance(q, int) and n < 1))
                    a.activation(wTs[:, :], PWT, ACT.Copy).then_inc(wTs_ready, 1)

                def weigh(q, k, r):
                    n = q + (n0 + k)
                    a.wait_ge(moe_done, n * R + r + 1)
                    a.wait_ge(w_ready, n + 1)
                    wait_pos(a, sum_b, (n - 1) * R + r + 1, not (isinstance(q, int) and n < 1))
                    halves = (1, 0) if r >= dve_rows(k) else (1,)
                    for place, s in enumerate(halves):
                        for e in range(HALF):
                            at = r * 512 + (place * HALF + e) * C
                            ins = a.activation(ys[:, at:at + C], PY[2 * (r % 2) + s][:, e * C:(e + 1) * C],
                                               ACT.Copy, scale=wsel[:, k % 2, r, s * HALF + e:s * HALF + e + 1])
                    ins.then_inc(act_part, 1)

                def normalise(q, k):
                    n = q + (n0 + k)
                    a.wait_ge(nmr2, n + 1)
                    wait_pos(a, t2_done, n - 1, not (isinstance(q, int) and n < 2))
                    for r in range(R):
                        ins = a.activation(xc[:, k % 2, r], x1[:, k % 4, r], ACT.Identity,
                                           scale=rstd[:, k % 2, r:r + 1], bias=nmr[:, k % 2, r:r + 1])
                    ins.then_inc(xc2_ready, 1)

                def w_parts(q, k):
                    n = q + (n0 + k)
                    a.wait_ge(w_ready, n + 1)
                    wait_pos(a, wT_done, n, not (isinstance(q, int) and n < 1))
                    a.activation(wscl[:, :], wsel[:, k % 2].rearrange("p r e -> p (r e)"), ACT.Copy,
                                 scale=sc[:, KWE:KWE + 1]).then_inc(wscl_ready, 1)
                    a.wait_ge(wscl_ready, n + 1)
                    a.activation(wcat[:, 0:3:2], wscl[:, :].unsqueeze(1).broadcast_to([128, 2, R * E]),
                                 ACT.Copy).then_inc(wh_ready, 1)

                def gap_exp(q, k):
                    n = q + (n0 + k)
                    a.wait_ge(gap_ready, n + 1)
                    a.activation(eg2[:, :], gap[:, :], ACT.Exp).then_inc(e_ready, 1)

                def step(t, k, a3, a2, a1, a0):
                    if a0:
                        weigh(t, k, 0)
                        weigh(t, k, 1)
                    if a1:
                        x_high(t, k + 1)
                    if a0:
                        weigh(t, k, 2)
                    if a1:
                        gap_exp(t, k + 1)
                    if a0:
                        w_copy(t, k)
                        weigh(t, k, 3)
                    if a3:
                        h_copy(t, k + 3)
                    if a2:
                        normalise(t, k + 2)
                    if a1:
                        w_parts(t, k + 1)

                for k in (-3, -2, -1):
                    step(0, k, True, k > -3, k > -2, False)
                loop(a, 0, Q - 4, 4, lambda t, k: step(t, k, True, True, True, True), pair == 0)
                for k in range(Q - 4, Q):
                    step(0, k, k + 3 < Q, k + 2 < Q, k + 1 < Q, True)

        @block.vector
        def _(v):
            done = [0]

            def setup(ins):
                done[0] += 1
                ins.then_inc(setup_v, 1)
                v.wait_ge(setup_v, done[0])

            def after(name):
                assert done[0] == SETUP[name], (name, done[0])

            v.wait_ge(weights_in, 16 * NW_IN)
            v.wait_ge(consts, 4)
            v.wait_ge(zeroed, 4)
            for col, src in ((GB, kraw[:, 0]), (BB, kraw[:, 1])):
                setup(v.tensor_reduce(w_abs[:, col:col + 1], src.rearrange("p i j -> p (i j)"), AX, ALU.max,
                                      apply_absolute_value=True))
            setup(v.tensor_reduce(w_abs[:, EW:EW + 1], we_raw.rearrange("p e c -> p (e c)"), AX, ALU.max,
                                  apply_absolute_value=True))
            setup(v.tensor_reduce(w_abs[:, RW:RW + 1], rw_raw, AX, ALU.max, apply_absolute_value=True))
            setup(v.tensor_reduce(w_abs[0:96, EB:EB + 1], eb_raw[0:96].rearrange("p r c -> p (r c)"), AX,
                                  ALU.max, apply_absolute_value=True))
            after("ABS")
            v.wait_ge(setup_p, P_ABST)
            setup(v.tensor_reduce(colmax[0:NSC], PM[0:NSC, 0:128], AX, ALU.max))
            setup(v.tensor_scalar(diag5[0:NSC], identf[0:NSC, 0:NSC], colmax[0:NSC, 0:1], None, ALU.mult))
            after("DIAG")
            v.wait_ge(setup_p, P_MAX)
            setup(v.tensor_scalar(pw2[:, :], PM[:, 128:128 + NSC], 2.0 ** -60, None, ALU.max))
            setup(v.tensor_scalar(pw2[:, :].bitcast(i32), pw2[:, :].bitcast(i32), 0x7F800000, None,
                                  ALU.bitwise_and))
            setup(v.reciprocal(inv[:, :], pw2[:, :]))

            def scale(dst, src, *ops):
                (o1, v1), (o2, v2) = ops if len(ops) == 2 else (ops[0], (None, None))
                if o2 is None:
                    setup(v.tensor_scalar(sc[:, dst:dst + 1], src, v1, None, o1))
                else:
                    setup(v.tensor_scalar(sc[:, dst:dst + 1], src, v1, v2, o1, o2))

            WS = 1.0 / KSC
            scale(IKAP, pw2[:, BB:BB + 1], (ALU.mult, 1.0 / 32), (ALU.max, 1.0))
            setup(v.reciprocal(sc[:, KAP:KAP + 1], sc[:, IKAP:IKAP + 1]))
            scale(NSG, pw2[:, GB:GB + 1], (ALU.mult, -WS))
            scale(SBV, pw2[:, BB:BB + 1], (ALU.mult, WS))
            scale(ISE, inv[:, EW:EW + 1], (ALU.mult, 1.0 / WS))
            scale(SR, pw2[:, RW:RW + 1], (ALU.mult, WS))
            scale(SEB, pw2[:, EB:EB + 1], (ALU.mult, KSC ** -2))
            scale(KWE, sc[:, ISE:ISE + 1], (ALU.mult, KSC))
            for k, col in ((0, GB), (1, BB)):
                setup(v.tensor_scalar(ksc[:, k], kraw[:, k], inv[:, col:col + 1], KSC, ALU.mult, ALU.mult))
            for k in range(2):
                cell = table[:, MID - RAD:MID + RAD + 1, k * 2 * KS:(k + 1) * 2 * KS]
                cell = cell.rearrange("p j (i l) -> p i j l", l=2)
                setup(v.tensor_copy(cell[:, :, :, 0], ksc[:, k, :, ::-1]))
                setup(v.tensor_tensor(cell[:, :, :, 1], ksc[:, k, :, ::-1], cell[:, :, :, 0], ALU.subtract))
            after("TABLE")
            setup(v.tensor_scalar(we_sc, we_raw, inv[:, EW:EW + 1], KSC, ALU.mult, ALU.mult))
            setup(v.tensor_copy(weh[:, :, :], we_sc))
            setup(v.tensor_tensor(wel[:, :, :], we_sc, weh[:, :, :], ALU.subtract))
            setup(v.tensor_scalar(rw_sc, rw_raw, inv[:, RW:RW + 1], KSC, ALU.mult, ALU.mult))
            setup(v.tensor_copy(rwh[:, :], rw_sc))
            setup(v.tensor_tensor(rwl[:, :], rw_sc, rwh[:, :], ALU.subtract))
            setup(v.tensor_scalar(eb_sc[0:96], eb_raw[0:96], inv[0:96, EB:EB + 1], KSC, ALU.mult, ALU.mult))
            setup(v.tensor_copy(eb_hi[0:96], eb_sc[0:96]))
            setup(v.tensor_copy(bblk[0:64], eb_hi[0:64]))
            setup(v.tensor_tensor(bblk[64:96], eb_sc[64:96], eb_hi[64:96], ALU.subtract))
            setup(v.tensor_scalar(wf[:, :], w_raw, F0, None, ALU.mult))
            v.wait_ge(setup_p, P_COLSUM)
            setup(v.scalar_tensor_tensor(out=brd[0:1, 0:C], in0=PM[0:1, 256:256 + C], scalar=F0 * EPS_SCAN,
                                         in1=brf[0:1, :], op0=ALU.mult, op1=ALU.add))
            setup(v.tensor_scalar(brd[0:1, 0:C], brd[0:1, 0:C], sc[0:1, KAP:KAP + 1], None, ALU.mult))
            for k in range(3):
                setup(v.tensor_copy(b3[0:1, k], brd[0:1, 0:C]))
                if k < 2:
                    setup(v.tensor_tensor(brd[0:1, 0:C], brd[0:1, 0:C], b3[0:1, k], ALU.subtract))
            after("B3")

            v.wait_ge(corner_in, 16 * 4 * NB)
            for w in range(CW):
                ins = v.bn_stats(cst[0:CR, w], cx[0:CR, w])
            setup(ins)
            for w in range(CW):
                ins = v.bn_aggr(cmv[0:CR, w], cst[0:CR, w])
            setup(ins)
            setup(v.tensor_scalar(cve[0:CR], cmv[0:CR, :, 1], EPS1, None, ALU.add))
            after("CVE")
            v.wait_ge(setup_g, 1)
            for w in range(CW):
                ins = v.tensor_scalar(cxn[0:CR, w], cx[0:CR, w], cmv[0:CR, w, 0:1], crs[0:CR, w:w + 1],
                                      ALU.subtract, ALU.mult)
            setup(ins)
            after("CXN")
            v.wait_ge(setup_a, A_CXT)
            L = CR - 2 * RAD
            setup(v.memset(ccv, 0.0))
            for j in range(KS):
                for i in range(KS):
                    for k, kern in enumerate((0, 2, 1)):
                        into = ccv[:, k, :, RAD:RAD + L]
                        ins = v.scalar_tensor_tensor(
                            out=into, in0=cxT[:, 2 * RAD - j:2 * RAD - j + KS, 2 * RAD - i:2 * RAD - i + L],
                            scalar=kraw[:, kern, i, j:j + 1], in1=into, op0=ALU.mult, op1=ALU.add)
                        if k == NCV - 1:
                            setup(ins)
            after("CCONV")
            v.wait_ge(setup_a, A_GATES)
            for k in range(2):
                setup(v.tensor_scalar(ctm[k], ctm[k], 1.0, None, ALU.add))
                setup(v.reciprocal(ctm[k], ctm[k]))
            setup(v.tensor_tensor(ctm[2], ccv[:, 2].rearrange("p w r -> p (w r)"), ctm[0], ALU.mult))
            setup(v.memset(ctm[3], 0.0))
            ta = ctm[3].rearrange("p (w b r) -> p w b r", w=KS, b=NB)
            tg = ctm[1].rearrange("p (w b r) -> p w b r", w=KS, b=NB)
            for b in range(NB):
                ins = v.tensor_tensor(ta[:, :, b, RAD:RAD + KS], tg[:, :, b, RAD:RAD + KS],
                                      kraw[:, 3].rearrange("p i j -> p j i"), ALU.mult)
            setup(ins)
            after("CVAL")
            v.wait_ge(setup_a, A_LN)
            setup(v.scalar_tensor_tensor(out=ctm[0], in0=ctm[2], scalar=0.0, in1=ctm[7], op0=ALU.max,
                                         op1=ALU.add))
            setup(v.tensor_scalar(ctm[6], ctm[6], 1.0, None, ALU.add))
            setup(v.reciprocal(ctm[1], ctm[6]))
            setup(v.tensor_scalar(ctm[2], ctm[1], -1.0, 1.0, ALU.mult, ALU.add))
            power = ctm[1]
            free = [ctm[4], ctm[5]]
            terms = 1
            while terms < STEPS:
                setup(v.scalar_tensor_tensor(out=ctm[2], in0=power, scalar=1.0, in1=ctm[2], op0=ALU.add,
                                             op1=ALU.mult))
                terms *= 2
                if terms < STEPS:
                    nxt = free.pop(0)
                    setup(v.tensor_tensor(nxt, power, power, ALU.mult))
                    power = nxt
            setup(v.tensor_scalar(ctm[2], ctm[2], -F0, None, ALU.add))
            setup(v.scalar_tensor_tensor(out=ctm[3], in0=ctm[0], scalar=EPS_SCAN, in1=ctm[2], op0=ALU.add,
                                         op1=ALU.mult))
            after("CDELTA")
            v.wait_ge(setup_p, P_CW)
            for half, bank in ((0, PY[0]), (1, PY[1])):
                lo, hi = (0, 4) if half == 0 else (4, KS)
                setup(v.tensor_tensor(cfix[0:CR, lo:hi], cx[0:CR, RAD + lo:RAD + hi],
                                      bank[0:CR, 0:(hi - lo) * C].rearrange("p (w c) -> p w c", c=C), ALU.add))
            after("CFIX")

            for pair in range(PAIRS):
                n0, m0 = pair * Q, pair * C

                def ln_stat(q, k):
                    n = q + (n0 + k)
                    nd = n // 4 if isinstance(n, int) else (q + n0) // 4 + k // 4
                    v.wait_ge(x_in[k % 4], nd * 16 + 16)
                    for r in range(R):
                        ins = v.bn_stats(stats[:, k % 2, r], xin[:, k % 4, r])
                    ins.then_inc(ln_stats, 1)

                def ln_moments(q, k):
                    for r in range(R):
                        ins = v.bn_aggr(mv[:, k % 2, r], stats[:, k % 2, r])
                    ins.then_inc(ln_aggr, 1)

                def ln_apply(q, k):
                    n = q + (n0 + k)
                    v.wait_ge(ln_rstd, n + 1)
                    wait_pos(v, ln_lo, n - 1, not (isinstance(q, int) and n < 2))
                    v.scalar_tensor_tensor(out=nmr[:, k % 2], in0=mv[:, k % 2, :, 0], scalar=-1.0,
                                           in1=rstd[:, k % 2], op0=ALU.mult, op1=ALU.mult)\
                     .then_inc(nmr_ready, 1)
                    for r in range(DVE_LN):
                        ins = v.tensor_scalar(xc[:, k % 2, r], xin[:, k % 4, r], mv[:, k % 2, r, 0:1],
                                              rstd[:, k % 2, r:r + 1], ALU.subtract, ALU.mult)
                    ins.then_inc(ln_xc, 1)

                def ln_both(q, k):
                    ln_stat(q, k + 1)
                    v.wait_ge(ln_stats, q + (n0 + k + 2))
                    ln_apply(q, k)
                    ln_moments(q, k + 1)

                if pair == 0:
                    v.wait_ge(fixed_out, 16)
                    v.wait_ge(brow_in, 48)
                    v.wait_ge(table_out, 16)
                ln_stat(0, 0)
                v.wait_ge(ln_stats, n0 + 1)
                ln_moments(0, 0)
                loop(v, 0, Q - 4, 4, ln_both, pair == 0)
                for k in range(Q - 4, Q - 1):
                    ln_both(0, k)
                ln_apply(0, Q - 1)

                def value(c, k):
                    m = c + (m0 + k)
                    s = k % 2
                    v.wait_ge(gate_exp, m + 1)
                    v.tensor_scalar(t_eg[:, s], t_eg[:, s], 1.0, None, ALU.add).then_inc(gate_den, 1)
                    v.wait_ge(gate_den, m + 1)
                    v.reciprocal(t_rs[:, s], t_eg[:, s]).then_inc(gate_rec, 1)
                    v.wait_ge(gate_rec, m + 1)
                    wait_pos(v, absv, m - 1, not (isinstance(c, int) and m < 2))
                    v.scalar_tensor_tensor(out=t_v[:, s], in0=PY[k % 4][:, 256:512], scalar=sc[:, SBV:SBV + 1],
                                           in1=t_rs[:, s], op0=ALU.mult, op1=ALU.mult).then_inc(val, 1)
                    v.wait_ge(val, m + 1)
                    v.tensor_scalar(t_relu[:, s], t_v[:, s], sc[:, KAP:KAP + 1], 0.0, ALU.mult, ALU.max)\
                     .then_inc(relu, 1)

                def finish(c, k):
                    m = c + (m0 + k)
                    s = k % 2
                    v.wait_ge(logp, m + 1)
                    v.wait_ge(relu, m + 1)
                    wait_pos(v, h_lo, m - 1, not (isinstance(c, int) and m < 2))
                    v.scalar_tensor_tensor(out=t_hp[:, s], in0=t_l[:, s], scalar=sc[:, KAP:KAP + 1],
                                           in1=t_relu[:, s], op0=ALU.mult, op1=ALU.add).then_inc(h_sum, 1)
                    v.wait_ge(h_sum, m + 1)
                    view = XN[:, bass.ds(c + k, 1), :, :].rearrange("p o (b r) l -> p (o b) r l", b=PAIR)
                    v.tensor_copy(view[:, :, RAD:RAD + H, 0],
                                  t_hp[:, s].rearrange("p (b r) -> p b r", b=PAIR)).then_inc(h_hi, 1)

                def conv_end(c, k):
                    value(c, k + 1)
                    finish(c, k)

                value(0, 0)
                loop(v, 0, C - 4, 4, conv_end, pair == 0)
                for k in range(C - 4, C - 1):
                    conv_end(0, k)
                finish(0, C - 1)

                def residual(q, k):
                    n = q + (n0 + k)
                    nd = n // 4 if isinstance(n, int) else (q + n0) // 4 + k // 4
                    v.wait_ge(wout_done, n + 1)
                    v.wait_ge(x2_in[k % 4], nd * 16 + 16)
                    v.scalar_tensor_tensor(out=x1[:, k % 4], in0=PW[:, :, :], scalar=sc[:, IKAP:IKAP + 1],
                                           in1=xin[:, k % 4], op0=ALU.mult, op1=ALU.add).then_inc(x1_ready, 1)

                def stat(q, k, r):
                    if r == 0:
                        v.wait_ge(x1_ready, q + (n0 + k + 1))
                    ins = v.bn_stats(stats[:, k % 2, r], x1[:, k % 4, r])
                    if r == R - 1:
                        ins.then_inc(st2, 1)

                def moments(q, k):
                    for r in range(R):
                        ins = v.bn_aggr(mv[:, k % 2, r], stats[:, k % 2, r])
                    ins.then_inc(ag2, 1)

                def mean_root(q, k):
                    n = q + (n0 + k)
                    v.wait_ge(rstd2, n + 1)
                    wait_pos(v, xc2_ready, n - 1, not (isinstance(q, int) and n < 2))
                    v.scalar_tensor_tensor(out=nmr[:, k % 2], in0=mv[:, k % 2, :, 0], scalar=-1.0,
                                           in1=rstd[:, k % 2], op0=ALU.mult, op1=ALU.mult).then_inc(nmr2, 1)

                def x_low(q, k):
                    n = q + (n0 + k)
                    v.wait_ge(xTh_ready, n + 1)
                    v.tensor_tensor(xTl[:, k % 2], PX[:, :, :], xTh[:, k % 2], ALU.subtract)\
                     .then_inc(xTl_ready, 1)

                def route(q, k):
                    n = q + (n0 + k)
                    v.wait_ge(router_done, n + 1)
                    v.scalar_tensor_tensor(out=lg[:, :, :].rearrange("p r e -> p (r e)"), in0=PR,
                                           scalar=sc[:, SR:SR + 1],
                                           in1=rb4[:, :, :].rearrange("p r e -> p (r e)"),
                                           op0=ALU.mult, op1=ALU.add).then_inc(lg_ready, 1)

                def largest(q, k):
                    for r in range(R):
                        ins = v.max(mx[:, r], lg[:, r])
                    ins.then_inc(mx_ready, 1)

                def places(q, k):
                    n = q + (n0 + k)
                    v.wait_ge(mx_ready, n + 1)
                    v.tensor_tensor(gap[:, :], mx[:, :, 1], mx[:, :, 0], ALU.subtract).then_inc(gap_ready, 1)
                    for r in range(R):
                        ins = v.max_index(mi[:, r], mx[:, r], lg[:, r])
                    ins.then_inc(mi_ready, 1)

                def one_hot(q, k):
                    n = q + (n0 + k)
                    v.wait_ge(mi_ready, n + 1)
                    wait_pos(v, wt_ready, 2 * n, not (isinstance(q, int) and n < 1))
                    for o, j in ((oh1, 0), (oh2, 1)):
                        ins = v.tensor_tensor(o[:, :, :], iota8[:, :, :],
                                              mi[:, :, j:j + 1].broadcast_to([128, R, E]), ALU.is_equal)
                    ins.then_inc(oh_ready, 1)

                def denominator(q, k):
                    n = q + (n0 + k)
                    v.wait_ge(e_ready, n + 1)
                    v.tensor_scalar(wden[:, :], eg2[:, :], 1.0, sc[:, ISE:ISE + 1], ALU.add, ALU.mult)\
                     .then_inc(wden_ready, 1)

                def first_share(q, k):
                    v.wait_ge(wden_ready, q + (n0 + k + 1))
                    v.reciprocal(w1[:, :], wden[:, :]).then_inc(w1_ready, 1)

                def second_share(q, k):
                    v.wait_ge(w1_ready, q + (n0 + k + 1))
                    v.tensor_tensor(w2[:, :], eg2[:, :], w1[:, :], ALU.mult).then_inc(w2_ready, 1)

                def weigh(q, k, r, e):
                    n = q + (n0 + k)
                    if r >= dve_rows(k):
                        return
                    pair_sum = (dve_rows(0) + dve_rows(1)) * HALF
                    before = (q + (n0 + k - k % 2)) * (pair_sum // 2) \
                        + (dve_rows(0) * HALF if k % 2 else 0)
                    if e == 0:
                        v.wait_ge(moe_done, n * R + r + 1)
                        v.wait_ge(w_ready, n + 1)
                        if r == 0 and not (isinstance(q, int) and n < 2):
                            v.wait_ge(out_sent[k % 2], (n // 2 if isinstance(n, int)
                                                        else (q + n0) // 2 + k // 2) * 16)
                    else:
                        v.wait_ge(dve_part, before + (r * HALF + e))
                    py = PY[2 * (r % 2)]
                    v.scalar_tensor_tensor(out=acc[:, k % 2, r], in0=py[:, e * C:(e + 1) * C],
                                           scalar=wsel[:, k % 2, r, e:e + 1],
                                           in1=acc[:, k % 2, r] if e else x1[:, k % 4, r],
                                           op0=ALU.mult, op1=ALU.add).then_inc(dve_part, 1)

                def bias(q, k):
                    n = q + (n0 + k)
                    rows = dve_rows(k)
                    v.wait_ge(pb_done, n + 1)
                    if rows < R:
                        v.scalar_tensor_tensor(out=acc[:, k % 2, rows:R], in0=PW[:, rows:R],
                                               scalar=sc[:, SEB:SEB + 1], in1=x1[:, k % 4, rows:R],
                                               op0=ALU.mult, op1=ALU.add)
                    pair_sum = (dve_rows(0) + dve_rows(1)) * HALF
                    before = (q + (n0 + k - k % 2)) * (pair_sum // 2)
                    v.wait_ge(dve_part, before + (pair_sum if k % 2 else dve_rows(0) * HALF))
                    v.scalar_tensor_tensor(out=acc[:, k % 2, 0:rows], in0=PW[:, 0:rows],
                                           scalar=sc[:, SEB:SEB + 1], in1=acc[:, k % 2, 0:rows],
                                           op0=ALU.mult, op1=ALU.add).then_inc(acc_ready, 1)

                def step(t, k, a3, a2, a1, a0):
                    if a0:
                        weigh(t, k, 0, 0)
                        weigh(t, k, 0, 1)
                        weigh(t, k, 0, 2)
                        weigh(t, k, 0, 3)
                        weigh(t, k, 1, 0)
                        weigh(t, k, 1, 1)
                    if a2:
                        residual(t, k + 2)
                    if a0:
                        weigh(t, k, 1, 2)
                    if a2:
                        stat(t, k + 2, 0)
                        stat(t, k + 2, 1)
                    if a0:
                        weigh(t, k, 1, 3)
                    if a2:
                        stat(t, k + 2, 2)
                        stat(t, k + 2, 3)
                    if a1:
                        x_low(t, k + 1)
                    if a2:
                        v.wait_ge(st2, t + (n0 + k + 3))
                    if a0:
                        weigh(t, k, 2, 0)
                    if a2:
                        moments(t, k + 2)
                    if a0:
                        weigh(t, k, 2, 1)
                    if a1:
                        route(t, k + 1)
                        v.wait_ge(lg_ready, t + (n0 + k + 2))
                    if a0:
                        weigh(t, k, 2, 2)
                    if a1:
                        largest(t, k + 1)
                    if a0:
                        weigh(t, k, 2, 3)
                    if a1:
                        places(t, k + 1)
                    if a0:
                        weigh(t, k, 3, 0)
                    if a1:
                        one_hot(t, k + 1)
                        denominator(t, k + 1)
                    if a0:
                        weigh(t, k, 3, 1)
                    if a1:
                        first_share(t, k + 1)
                    if a0:
                        weigh(t, k, 3, 2)
                    if a1:
                        second_share(t, k + 1)
                    if a2:
                        mean_root(t, k + 2)
                    if a0:
                        weigh(t, k, 3, 3)
                        bias(t, k)

                for k in (-3, -2, -1):
                    step(0, k, True, k > -3, k > -2, False)
                loop(v, 0, Q - 4, 4, lambda t, k: step(t, k, True, True, True, True), pair == 0)
                for k in range(Q - 4, Q):
                    step(0, k, k + 3 < Q, k + 2 < Q, k + 1 < Q, True)

        @block.tensor
        def _(p):
            p.wait_ge(consts, 4)
            p.wait_ge(setup_v, S_ABS)
            p.transpose(PM[0:NSC, 0:128], w_abs, identf[:, :]).then_inc(setup_p, 1)
            p.wait_ge(setup_v, S_DIAG)
            p.matmul(PM[:, 128:128 + NSC], onesf[0:NSC, :], diag5[0:NSC], start=True, stop=True)\
             .then_inc(setup_p, 1)
            p.wait_ge(setup_v, S_DIAG + 1)
            p.matmul(PM[0:1, 256:256 + C], onesf[:, 0:1], w_raw, start=True, stop=True).then_inc(setup_p, 1)
            p.wait_ge(setup_v, S_CXN)
            for w in range(CW):
                bank, at = (PT, w) if w < 7 else (PX, w - 7)
                ins = p.transpose(bank[:, :, :].rearrange("p r w -> p (r w)")[:, at * CR:(at + 1) * CR],
                                  cxn[0:CR, w], identf[0:CR, 0:CR])
            ins.then_inc(setup_p, 1)
            p.wait_ge(setup_v, S_CDELTA)
            dh = ctm[3].rearrange("p (w r) -> p w r", w=KS)
            for w in range(KS):
                ins = p.matmul(PY[w // 4][0:CR, (w % 4) * C:(w % 4 + 1) * C], dh[:, w], w_raw, start=True,
                               stop=True)
            ins.then_inc(setup_p, 1)

            for pair in range(PAIRS):
                n0, m0 = pair * Q, pair * C

                def conv(c, k):
                    m = c + (m0 + k)
                    cg = (c + m0) // 4
                    p.wait_ge(circ_in[(k % 4) // GRP], (cg + (k // 4 + 1)) * (16 * 10))
                    wait_pos(p, val, m - 3, not (isinstance(c, int) and m < 4))
                    view = XN[:, bass.ds(c + k, 1), :, :].rearrange("p o (b r) l -> p (o b) r l", b=PAIR)
                    for cv in range(2):
                        into = PY[k % 4][:, cv * 256:(cv + 1) * 256].rearrange("p (b r) -> p b r", b=PAIR)
                        for i in range(KS):
                            for part, (wl, xl) in enumerate(((0, 0), (0, 1), (1, 0))):
                                ins = p.matmul(into, circ[:, k % 4, :, (cv * KS + i) * 2 + wl],
                                               view[:, :, 2 * RAD - i:2 * RAD - i + H, xl],
                                               start=(i == 0 and part == 0), stop=(i == KS - 1 and part == 2))
                    ins.then_inc(conv_done, 1)

                p.wait_ge(halo, 2 * PAIR * (pair + 1))
                if pair == 0:
                    p.wait_ge(setup_v, S_CFIX)
                else:
                    p.wait_ge(act_part, n0 * R)
                    p.wait_ge(dve_part, n0 // 2 * (dve_rows(0) + dve_rows(1)) * HALF)
                loop(p, 0, C, 4, conv, pair == 0)

                def turn_h(q, k):
                    n = q + (n0 + k)
                    wait_pos(p, hT_ready, n, not (isinstance(q, int) and n < 1))
                    at = (q + k) * R + ((q + k) // QI) * (2 * RAD) + RAD
                    for r in range(R):
                        for part in range(2):
                            src = XN[:, :, bass.ds(at + r, 1), part].rearrange("p c o -> p (c o)")
                            ins = p.matmul(PT[:, r], src, mirror[:, :], start=part == 0, stop=part == 1)
                    ins.then_inc(t1_done, 1)

                def project(q, k):
                    n = q + (n0 + k)
                    p.wait_ge(hT_ready, n + 1)
                    wait_pos(p, x1_ready, n, not (isinstance(q, int) and n < 1))
                    wait_pos(p, acc_ready, n - 2, not (isinstance(q, int) and n < 3))
                    for r in range(R):
                        p.matmul(PW[:, r], ones3[:, :], brow[:, :], start=True, stop=False)
                        ins = p.matmul(PW[:, r], hT[:, r], wf[:, :], start=False, stop=True)
                    ins.then_inc(wout_done, 1)

                def turn_x(q, k):
                    n = q + (n0 + k)
                    p.wait_ge(xc2_ready, n + 1)
                    wait_pos(p, xTl_ready, n, not (isinstance(q, int) and n < 1))
                    for r in range(R):
                        ins = p.transpose(PX[:, r], xc[:, k % 2, r], identf[:, :])
                    ins.then_inc(t2_done, 1)

                def router(q, k):
                    n = q + (n0 + k)
                    p.wait_ge(xTl_ready, n + 1)
                    wait_pos(p, wTs_ready, n - 1, not (isinstance(q, int) and n < 2))
                    for r in range(R):
                        into = PR[:, r * E:(r + 1) * E]
                        p.matmul(into, xTh[:, k % 2, r], rwh[:, :], start=True, stop=False)
                        p.matmul(into, xTh[:, k % 2, r], rwl[:, :], start=False, stop=False)
                        ins = p.matmul(into, xTl[:, k % 2, r], rwh[:, :], start=False, stop=True)
                    ins.then_inc(router_done, 1)

                def turn_w(q, k, ahead):
                    n = q + (n0 + k)
                    p.wait_ge(wcat_ready, n + 1)
                    p.wait_ge(lg_ready, n + 1 + ahead)
                    p.transpose(PWT, wcat[:, :, :].rearrange("p k e -> p (k e)"), ident[:, :]).then_inc(wT_done, 1)

                def bias(q, k, ahead):
                    n = q + (n0 + k)
                    p.wait_ge(wTs_ready, n + 1)
                    p.wait_ge(x1_ready, n + 1 + ahead)
                    p.matmul(PW[:, :, :], wTs[:, :], bblk[:, :, :], start=True, stop=True).then_inc(pb_done, 1)

                def experts(q, k, r):
                    n = q + (n0 + k)
                    n4 = n * R + r
                    if not (isinstance(q, int) and n4 < 2):
                        p.wait_ge(act_part, n4 - 1)
                        pair_sum = (dve_rows(0) + dve_rows(1)) * HALF
                        before = (q + (n0 + k - k % 2)) * (pair_sum // 2)
                        if r >= 2:
                            rows = (dve_rows(0) if k % 2 else 0) + min(r - 1, dve_rows(k))
                        elif k % 2:
                            rows = min(r + R - 1, dve_rows(0))
                        else:
                            rows = min(r + R - 1, dve_rows(1)) - dve_rows(1)
                        p.wait_ge(dve_part, before + rows * HALF)
                    b0, b1 = PY[2 * (r % 2)], PY[2 * (r % 2) + 1]
                    wh = [weh[:, s * HALF:(s + 1) * HALF].rearrange("p e c -> p (e c)") for s in range(2)]
                    wl = [wel[:, s * HALF:(s + 1) * HALF].rearrange("p e c -> p (e c)") for s in range(2)]
                    hi, lo = xTh[:, k % 2, r], xTl[:, k % 2, r]
                    for s, bank in ((0, b0), (1, b1)):
                        p.matmul(bank[:, :], hi, wh[s], start=True, stop=False)
                        p.matmul(bank[:, :], hi, wl[s], start=False, stop=False)
                        ins = p.matmul(bank[:, :], lo, wh[s], start=False, stop=True)
                    ins.then_inc(moe_done, 1)

                def step(t, k, a3, a2, a1, a0):
                    if a0:
                        experts(t, k, 1)
                    if a2:
                        project(t, k + 2)
                    if a1:
                        turn_x(t, k + 1)
                    if a0:
                        experts(t, k, 2)
                    if a1:
                        router(t, k + 1)
                    if a0:
                        turn_w(t, k, 1 if a1 else 0)
                        experts(t, k, 3)
                        bias(t, k, 2 if a2 else 1 if a1 else 0)
                    if a3:
                        turn_h(t, k + 3)
                    if a1:
                        experts(t, k + 1, 0)

                p.wait_ge(h_lo, m0 + C)
                for k in (-3, -2, -1):
                    step(0, k, True, k > -3, k > -2, False)
                loop(p, 0, Q - 4, 4, lambda t, k: step(t, k, True, True, True, True), pair == 0)
                for k in range(Q - 4, Q):
                    step(0, k, k + 3 < Q, k + 2 < Q, k + 1 < Q, True)


SETUP = {"ABS": 5, "DIAG": 7, "TABLE": 24, "B3": 42, "CVE": 45, "CXN": 46, "CCONV": 96, "CVAL": 103,
         "CDELTA": 114, "CFIX": 116}
S_ABS, S_DIAG, S_TABLE, S_B3, S_CVE, S_CXN, S_CCONV, S_CVAL, S_CDELTA, S_CFIX = SETUP.values()
P_ABST, P_MAX, P_COLSUM, P_CXT, P_CW = 1, 2, 3, 4, 5
A_CXT, A_GATES, A_ABS, A_EXPN, A_LN = 2, 4, 6, 7, 8

_INS = ["x", "L0_conv_A_kernel", "L0_conv_B_kernel", "L0_conv_gate_A_kernel", "L0_conv_gate_B_kernel",
        "L0_conv_W_out", "L0_conv_b_out", "L0_ffn_router_w", "L0_ffn_router_b", "L0_ffn_expert_w",
        "L0_ffn_expert_b"]


def kernel(**inputs):
    import numpy as _np
    import concourse.bacc as _bacc
    from concourse import mybir as _mybir
    from concourse.bass_utils import run_bass_kernel_spmd as _run

    nc = _bacc.Bacc("TRN2", target_bir_lowering=False, num_devices=1)
    arrays, args = {}, []
    for name in _INS:
        a = _np.ascontiguousarray(inputs[name])
        arrays[f"in_{name}_dram"] = a
        args.append(nc.dram_tensor(f"in_{name}_dram", a.shape, _mybir.dt.from_np(a.dtype),
                                   kind="ExternalInput").ap())
    args.append(nc.dram_tensor("out_dram", inputs["x"].shape, _mybir.dt.float32, kind="ExternalOutput").ap())
    metaformer_layer(nc, *args)
    r = _run(nc, [arrays], core_ids=[0])
    return r.results[0]["out_dram"]
```

```python
import concourse.bass as bass
from concourse import mybir
from contextlib import ExitStack


def metaformer_layer(nc, x, A_kernel, B_kernel, gate_A_kernel, gate_B_kernel, W_out, b_out,
                     router_w, router_b, expert_w, expert_b, out):
    f32, f16, bf16 = mybir.dt.float32, mybir.dt.float16, mybir.dt.bfloat16
    i32, u32 = mybir.dt.int32, mybir.dt.uint32
    ALU = mybir.AluOpType
    ACT = mybir.ActivationFunctionType
    AX = mybir.AxisListType.X

    NB, H, W, C = x.shape
    E = router_w.shape[1]
    KS = A_kernel.shape[1]
    RAD = KS // 2
    STEPS = 8
    PAIR = 2
    PAIRS = NB // PAIR
    R = 4
    QI = H // R
    Q = PAIR * QI
    HP = H + 2 * RAD
    NT = 2 * KS * 2
    SPAN = 16
    DIAG = 2 * (SPAN - 1 + RAD) + 1
    MID = SPAN - 1 + RAD
    GRP = 2
    KSC = 256.0
    EPS_SCAN, EPS1, EPS2 = 1e-6, 1e-6, 1e-5
    F0 = 1.0 - 2.0 ** -STEPS
    CW = 2 * KS - 1
    CR = NB * CW
    KR = KS * NB
    HALF = E // 2
    LN_EXP_SET = 6
    XS = 8
    DVE_LN = 1
    DVE_LO = 2

    def dve_rows(k):
        return R - 1

    xt = x.rearrange("b h w c -> w (b h) c")
    ot = out.rearrange("b h w c -> w (b h) c")

    ctx = ExitStack()
    with ctx:
        def sb(name, shape, dt):
            return ctx.enter_context(nc.sbuf_tensor(name, shape, dt))

        def pb(name, shape, dt):
            return ctx.enter_context(nc.psum_tensor(name, shape, dt))

        def sem(name):
            return ctx.enter_context(nc.semaphore(name))

        XN = sb("XN", [128, C, PAIR * HP, 2], f16)
        circ = sb("circ", [128, 2 * GRP, W, NT], f16)
        xin = sb("xin", [128, 4, R, C], f32)
        xc = sb("xc", [128, 2, R, C], f32)
        hT = sb("hT", [128, R, W], f32)
        x1 = xin
        xTh = sb("xTh", [128, 2, R, W], f16)
        xTl = sb("xTl", [128, 2, R, W], f16)
        ys = sb("ys", [128, 12 * 256], f32)
        ysum = sb("ysum", [128, R, C], f32)
        outs = sb("outs", [128, 2, R, C], f32)
        acc = outs
        weh = sb("weh", [128, E, C], f16)
        wel = sb("wel", [128, E, C], f16)
        wf = sb("wf", [128, C], f32)
        identf = sb("identf", [128, 128], f32)
        ident = sb("ident", [128, 128], f16)
        mirror = sb("mirror", [128, 128], f16)
        rwh = sb("rwh", [128, E], f16)
        rwl = sb("rwl", [128, E], f16)
        ones3 = sb("ones3", [128, 128], bf16)
        brow = sb("brow", [128, C], bf16)
        bblk = sb("bblk", [96, R, C], f16)
        rb4 = sb("rb4", [128, R, E], f32)
        iota8 = sb("iota8", [128, R, E], f32)
        mhalf = sb("mhalf", [128, 16], f32)
        epst = sb("epst", [128, R], f32)
        NSC = 5
        GB, BB, EW, RW, EB = range(NSC)
        pw2 = sb("pw2", [128, NSC], f32)
        inv = sb("inv", [128, NSC], f32)
        sc = sb("sc", [128, 12], f32)
        KAP, IKAP, NSG, SBV, ISE, SR, SEB, KWE = range(8)
        stats = sb("stats", [128, 2, R, 6], f32)
        mv = sb("mv", [128, 4, R, 2], f32)
        ve = sb("ve", [128, 2, R], f32)
        rstd = sb("rstd", [128, 2, R], f32)
        lg = sb("lg", [128, R, E], f32)
        mx = sb("mx", [128, R, 8], f32)
        mi = sb("mi", [128, R, 8], u32)
        oh1 = sb("oh1", [128, R, E], f32)
        oh2 = sb("oh2", [128, R, E], f32)
        gap = sb("gap", [128, R], f32)
        eg2 = sb("eg2", [128, R], f32)
        wden = sb("wden", [128, R], f32)
        w1 = sb("w1", [128, R], f32)
        w2 = sb("w2", [128, R], f32)
        wt1 = sb("wt1", [128, R, E], f32)
        wt2 = sb("wt2", [128, R, E], f32)
        wsel = sb("wsel", [128, 2, R, E], f32)
        nmr = sb("nmr", [128, 2, R], f32)
        wscl = sb("wscl", [128, R * E], f32)
        wcat = sb("wcat", [128, 3, R * E], f16)
        wTs = sb("wTs", [96, 128], f16)

        def ytmp(n):
            return ys[:, n * 512:(n + 1) * 512].rearrange("p (s n) -> p s n", s=2)

        t_eg, t_rs, t_v, t_relu, t_l, t_hp = [ytmp(n) for n in range(6)]

        xnf = XN[:, :, :, :].rearrange("p c r l -> p (c r l)").bitcast(f32)
        used = [0]

        def tmp(n):
            used[0] += n
            return xnf[:, used[0] - n:used[0]]

        kraw = tmp(4 * KS * KS).rearrange("p (k i j) -> p k i j", k=4, i=KS)
        ksc = tmp(2 * KS * KS).rearrange("p (k i j) -> p k i j", k=2, i=KS)
        table = tmp(DIAG * NT // 2).bitcast(f16).rearrange("p (d n) -> p d n", n=NT)
        we_raw = tmp(E * C).rearrange("p (e c) -> p e c", e=E)
        we_sc = tmp(E * C).rearrange("p (e c) -> p e c", e=E)
        rw_raw = tmp(E)
        rw_sc = tmp(E)
        w_raw = tmp(C)
        w_abs = tmp(NSC)
        eb_raw = tmp(R * C).rearrange("p (r c) -> p r c", r=R)
        eb_sc = tmp(R * C).rearrange("p (r c) -> p r c", r=R)
        eb_hi = tmp(R * C // 2).bitcast(f16).rearrange("p (r c) -> p r c", r=R)
        diag5 = tmp(NSC)
        colmax = tmp(1)
        onesf = tmp(128)
        brf = tmp(C)
        brd = tmp(2 * C)
        b3 = tmp(3 * C // 2).bitcast(bf16).rearrange("p (k c) -> p k c", k=3)
        cx = tmp(CW * C).rearrange("p (w c) -> p w c", w=CW)
        cxn = tmp(CW * C).rearrange("p (w c) -> p w c", w=CW)
        cst = tmp(CW * 6).rearrange("p (w s) -> p w s", w=CW)
        cmv = tmp(CW * 2).rearrange("p (w s) -> p w s", w=CW)
        cve = tmp(CW)
        crs = tmp(CW)
        cxT = tmp(CW * CR).rearrange("p (w r) -> p w r", w=CW)
        NCV = 3
        ccv = tmp(NCV * KS * KR).rearrange("p (k w r) -> p k w r", k=NCV, w=KS)
        ctm = [tmp(KS * KR) for _ in range(8)]
        prod = tmp(2 * KS * KR).rearrange("p (k w r) -> p k w r", k=2, w=KS)
        cx7 = tmp(KS * C).rearrange("p (w c) -> p w c", w=KS)
        cfix = tmp(KS * C).rearrange("p (w c) -> p w c", w=KS)

        PT = pb("PT", [128, R, W], f32)
        PX = pb("PX", [128, R, W], f32)
        PW = pb("PW", [128, R, C], f32)
        PM = pb("PM", [128, 512], f32)
        PY = [pb(f"PY{i}", [128, 512], f32) for i in range(4)]
        PR = PM[:, 0:R * E]
        PWT = PM[0:96, 256:256 + 64].bitcast(f16)

        tbl = nc.dram_tensor("circulant_table", [C, DIAG, NT], f16).ap()
        fixed = nc.dram_tensor("corner_rows", [KS, NB, KS, C], f32).ap()

        weights_in = sem("weights_in")
        corner_in = sem("corner_in")
        corner7_in = sem("corner7_in")
        taps_v = sem("taps_v")
        taps_a = sem("taps_a")
        taps_g = sem("taps_g")
        zeroed = sem("zeroed")
        consts = sem("consts")
        setup_v = sem("setup_v")
        setup_a = sem("setup_a")
        setup_p = sem("setup_p")
        setup_g = sem("setup_g")
        table_out = sem("table_out")
        brow_in = sem("brow_in")
        fixed_out = sem("fixed_out")
        x_in = [sem(f"x_in{i}") for i in range(XS)]
        circ_in = [sem(f"circ_in{i}") for i in range(2)]
        ln_stats = sem("ln_stats")
        ln_aggr = sem("ln_aggr")
        ln_ve = sem("ln_ve")
        ln_rstd = sem("ln_rstd")
        ln_xc = sem("ln_xc")
        ln_hi = sem("ln_hi")
        ln_lo = sem("ln_lo")
        halo = sem("halo")
        ln_lod = sem("ln_lod")
        nmr_ready = sem("nmr_ready")
        ln_xa = sem("ln_xa")
        conv_done = sem("conv_done")
        gate_exp = sem("gate_exp")
        gate_den = sem("gate_den")
        gate_rec = sem("gate_rec")
        val = sem("val")
        relu = sem("relu")
        absv = sem("absv")
        expn = sem("expn")
        logp = sem("logp")
        h_sum = sem("h_sum")
        h_hi = sem("h_hi")
        h_lo = sem("h_lo")
        x2_in = [sem(f"x2_in{i}") for i in range(4)]
        x2_part = sem("x2_part")
        t1_done = sem("t1_done")
        hT_ready = sem("hT_ready")
        wout_done = sem("wout_done")
        x1_ready = sem("x1_ready")
        st2 = sem("st2")
        ag2 = sem("ag2")
        ve2 = sem("ve2")
        rstd2 = sem("rstd2")
        nmr2 = sem("nmr2")
        wscl_ready = sem("wscl_ready")
        xc2_ready = sem("xc2_ready")
        t2_done = sem("t2_done")
        xTh_ready = sem("xTh_ready")
        xTl_ready = sem("xTl_ready")
        router_done = sem("router_done")
        lg_ready = sem("lg_ready")
        mx_ready = sem("mx_ready")
        mi_ready = sem("mi_ready")
        oh_ready = sem("oh_ready")
        gap_ready = sem("gap_ready")
        e_ready = sem("e_ready")
        wden_ready = sem("wden_ready")
        w1_ready = sem("w1_ready")
        w2_ready = sem("w2_ready")
        wt_ready = sem("wt_ready")
        w_ready = sem("w_ready")
        wh_ready = sem("wh_ready")
        wcat_ready = sem("wcat_ready")
        wT_done = sem("wT_done")
        wTs_ready = sem("wTs_ready")
        pb_done = sem("pb_done")
        moe_done = sem("moe_done")
        dve_part = sem("dve_part")
        act_part = sem("act_part")
        sum_a = sem("sum_a")
        sum_b = sem("sum_b")
        sum_8 = sem("sum_8")
        acc_ready = sem("acc_ready")
        out_ready = sem("out_ready")
        out_sent = [sem(f"out_sent{i}") for i in range(2)]

        block = ctx.enter_context(nc.Block())

        def loop(eng, a, b, step, body, peel=False):
            if peel or b - a <= step:
                for k in range(min(step, b - a)):
                    body(a, k)
                a += step
            if a >= b:
                return
            assert (b - a) % step == 0
            with eng.Fori(0, (b - a) // step, 1) as turn:
                for k in range(step):
                    body(turn * step + a, k)

        def xns(k):
            return xc[:, k % 2] if k % 4 < 2 else outs[:, k % 2]

        xsy = ys[:, 0:(XS - 4) * R * C].rearrange("p (s r c) -> p s r c", s=XS - 4, r=R)

        def xs(k):
            return xin[:, k % XS] if k % XS < 4 else xsy[:, k % XS - 4]

        def ln_loop(eng, h0, body):
            with eng.Fori(0, (QI - 8) // XS, 1) as turn:
                for k in range(4, 4 + XS):
                    body(turn * XS + h0, k)

        def row0(k, b):
            return k * R + b * 2 * RAD + RAD

        def wait_pos(eng, s, value, at_least_one):
            if at_least_one:
                eng.wait_ge(s, value)

        def corner_tap(kern, tap):
            j, i = tap // KS, tap % KS
            at = (2 * RAD - i) * NB
            return cxT[:, 2 * RAD - j:2 * RAD - j + KS, at:at + KR], kraw[:, kern, i, j:j + 1]

        NW_IN = 4 + 3 + 12 + 1 + 1
        PARTS7 = ((0, RAD, H - RAD), (RAD, RAD + 1, 0))
        PARTS = ((0, CW // 2, H - CW // 2), (CW // 2, CW - CW // 2, 0))

        @block.sync
        def _(sp):
            for k, src in enumerate((gate_B_kernel, B_kernel, gate_A_kernel, A_kernel)):
                sp.dma_start(kraw[:, k], src).then_inc(weights_in, 16)
            sp.dma_start(we_raw, expert_w.rearrange("e d c -> d e c")).then_inc(weights_in, 16)
            sp.dma_start(rw_raw, router_w).then_inc(weights_in, 16)
            sp.dma_start(w_raw, W_out).then_inc(weights_in, 16)
            sp.wait_ge(zeroed, 1)
            for part in range(3):
                for r in range(R):
                    at = (part * R + r) * E
                    sp.dma_start(eb_raw[at:at + E, r], expert_b).then_inc(weights_in, 16)
            sp.dma_start(brf[0:1, :], b_out.rearrange("(o c) -> o c", o=1)).then_inc(weights_in, 16)
            rb_src = bass.AP(tensor=router_b.tensor, offset=0, ap=[[0, 128], [0, R], [1, E]])
            sp.dma_start(rb4[:, :, :], rb_src).then_inc(weights_in, 16)
            for b in range(NB):
                for ph, nh, h0 in PARTS:
                    for pw, nw, w0 in PARTS:
                        at = b * CW + ph
                        sp.dma_start(cx[at:at + nh, pw:pw + nw],
                                     x[b, h0:h0 + nh, w0:w0 + nw, :]).then_inc(corner_in, 16)
            for ph, nh, h0 in PARTS7:
                for r in range(nh):
                    for pw, nw, w0 in PARTS7:
                        at = (ph + r) * NB
                        sp.dma_start(cx7[at:at + NB, pw:pw + nw],
                                     x[:, h0 + r, w0:w0 + nw, :]).then_inc(corner7_in, 16)
            for k in range(XS):
                sp.dma_start(xs(k), xt[:, k * R:(k + 1) * R, :]).then_inc(x_in[k], 16)
            sp.wait_ge(setup_v, S_TABLE)
            sp.dma_start(tbl, table).then_inc(table_out, 16)
            sp.wait_ge(setup_v, S_B3)
            for k in range(3):
                sp.dma_start(brow[k:k + 1, :], b3[0:1, k]).then_inc(brow_in, 16)
            sp.wait_ge(setup_v, S_CFIX)
            sp.dma_start(fixed.rearrange("r b w c -> (r b) w c"), cfix[0:KR]).then_inc(fixed_out, 16)
            sp.wait_ge(table_out, 16)
            sp.wait_ge(fixed_out, 16)
            sp.wait_ge(zeroed, 4)

            parts = [0]
            for pair in range(PAIRS):
                n0, m0 = pair * Q, pair * C

                def ln_load(q, k):
                    if not isinstance(q, int):
                        sp.wait_ge(ln_xa, q + (n0 + k - XS + 1))
                        sp.wait_ge(ln_xc, q + (n0 + k - XS + 1))
                    sp.dma_start(xs(k), xt[:, bass.ds((q + (n0 + k)) * R, R), :]).then_inc(x_in[k], 16)

                if pair:
                    sp.wait_ge(out_ready, n0)
                    for k in range(XS):
                        ln_load(0, k)
                loop(sp, XS, Q, XS, ln_load)

                def circ_load(c, k):
                    slot, g = GRP * k, GRP * k
                    if not (pair == 0 and isinstance(c, int)):
                        sp.wait_ge(conv_done, c + (m0 + g - GRP))

                    def band(p0, w0, w1, wrap=0):
                        v0, v1 = W - w1, W - w0
                        diag = v0 + p0 - (W - 1) + wrap
                        src = bass.AP(tensor=tbl.tensor, offset=(c + g) * (DIAG * NT) + (MID + diag) * NT,
                                      ap=[[NT, SPAN], [DIAG * NT, GRP], [1, (v1 - v0) * NT]])
                        dst = circ[p0:p0 + SPAN, slot:slot + GRP, v0:v1, :].rearrange("p c w n -> p c (w n)")
                        sp.dma_start(dst, src).then_inc(circ_in[k], 16)

                    for p0 in range(0, W, SPAN):
                        band(p0, max(p0 - RAD, 0), min(p0 + SPAN + RAD, W))
                    band(0, W - RAD, W, W)
                    band(W - SPAN, 0, RAD, -W)

                circ_load(0, 0)
                circ_load(0, 1)
                with sp.Fori(1, C // 4, 1) as turn:
                    circ_load(turn * 4, 0)
                    circ_load(turn * 4, 1)

                def x2_load(q, k, first, last):
                    n = q + (n0 + k)
                    slot = k % 4
                    dst = xin[:, slot]
                    src = xt[:, bass.ds(n * R, R), :]
                    if not (first or last):
                        sp.dma_start(dst, src).then_inc(x2_in[slot], 16)
                        return
                    sp.dma_start(dst, src).then_inc(x2_part, 16)
                    parts[0] += 1
                    sp.wait_ge(x2_part, 16 * parts[0])
                    b = (n0 + q + k) // QI
                    r0, r1, f0 = (0, R, RAD) if first else (R - RAD, R, 0)
                    sp.dma_start(xin[0:RAD + 1, slot, r0:r1],
                                 fixed[f0:f0 + r1 - r0, b, RAD:KS].rearrange("r w c -> w r c"))\
                      .then_inc(x2_part, 16)
                    parts[0] += 1
                    sp.wait_ge(x2_part, 16 * parts[0])
                    sp.dma_start(xin[W - RAD:W, slot, r0:r1],
                                 fixed[f0:f0 + r1 - r0, b, 0:RAD].rearrange("r w c -> w r c"))\
                      .then_inc(x2_in[slot], 16)

                def ahead(q, k, first=False, last=False):
                    sp.wait_ge(acc_ready, q + (n0 + k + 1))
                    x2_load(q, k + 4, first, last)

                def store(q, k):
                    n = q + (n0 + k)
                    sp.wait_ge(out_ready, n + 1)
                    sp.dma_start(ot[:, bass.ds(n * R, R), :], outs[:, k % 2]).then_inc(out_sent[k % 2], 16)

                def both(q, k):
                    ahead(q, k)
                    store(q, k)

                sp.wait_ge(ln_hi, n0 + Q)
                for q in range(4):
                    x2_load(0, q, q == 0, False)
                loop(sp, 0, QI - 8, 4, both)
                for q in range(QI - 8, QI):
                    ahead(0, q, q + 4 == QI, q + 4 == QI - 1)
                    store(0, q)
                loop(sp, QI, Q - 8, 4, both)
                for q in range(Q - 8, Q):
                    if q + 4 < Q:
                        ahead(0, q, False, q + 4 == Q - 1)
                    store(0, q)
            for k in range(2):
                sp.wait_ge(out_sent[k], 16 * PAIRS * Q // 2)

        @block.gpsimd
        def _(g):
            g.memset(eb_raw, 0.0).then_inc(zeroed, 1)
            g.memset(table, 0.0).then_inc(zeroed, 1)
            g.memset(brow[:, :], 0.0).then_inc(zeroed, 1)
            g.memset(ones3[:, :], 1.0)
            g.memset(onesf, 1.0)
            g.memset(mhalf[:, :], -0.5)
            g.memset(epst[:, :], EPS2)
            for e in range(E):
                g.memset(iota8[:, :, e:e + 1], float(e))
            g.memset(w_abs, 0.0)
            g.memset(identf[:, :], 0.0)
            g.memset(mirror[:, :], 0.0)
            g.memset(ident[:, :], 0.0).then_inc(consts, 1)
            g.wait_ge(consts, 1)
            g.affine_select(out=mirror[:, :], in_=mirror[:, :], compare_op=ALU.not_equal, fill=1.0,
                            base=-127, pattern=[[1, 128]], channel_multiplier=1).then_inc(consts, 1)
            for m in (identf, ident):
                g.affine_select(out=m[:, :], in_=m[:, :], compare_op=ALU.not_equal, fill=1.0,
                                base=0, pattern=[[-1, 128]], channel_multiplier=1).then_inc(consts, 1)
            g.memset(circ[:, :, :, :], 0.0).then_inc(zeroed, 1)
            g.wait_ge(setup_v, S_CVE)
            g.tensor_tensor(crs[0:CR], cve[0:CR], mhalf[0:CR, 0:CW], ALU.pow).then_inc(setup_g, 1)
            g.memset(ccv[:, 1], 0.0).then_inc(taps_g, 1)
            for tap in range(KS * KS):
                g.wait_ge(taps_a, tap + 1)
                g.wait_ge(taps_g, tap + 1)
                g.tensor_tensor(ccv[:, 1], ccv[:, 1], prod[:, tap % 2], ALU.add).then_inc(taps_g, 1)

            for pair in range(PAIRS):
                n0, m0 = pair * Q, pair * C

                def ln_root(q, k):
                    n = q + (n0 + k)
                    g.wait_ge(ln_ve, n + 1)
                    wait_pos(g, ln_xa, n - 1, not (isinstance(q, int) and n < 2))
                    wait_pos(g, ln_xc, n - 1, not (isinstance(q, int) and n < 2))
                    g.tensor_tensor(rstd[:, k % 2], ve[:, k % 2], mhalf[:, 0:R], ALU.pow).then_inc(ln_rstd, 1)

                def ln_low(q, k, b):
                    n = q + (n0 + k)
                    g.wait_ge(ln_hi, n + 1)
                    at = q * R + row0(k, b)
                    view = XN[:, :, bass.ds(at + DVE_LO, R - DVE_LO), :]
                    g.tensor_tensor(view[:, :, :, 1], xns(k)[:, DVE_LO:R].rearrange("p r c -> p c r"),
                                    view[:, :, :, 0], ALU.subtract).then_inc(ln_lo, 1)

                def ln_both(q, k, b):
                    ln_root(q, k + 2)
                    ln_low(q, k - 1, b)

                if pair:
                    g.wait_ge(xc2_ready, n0)
                ln_root(0, 0)
                ln_root(0, 1)
                for b in range(PAIR):
                    h0 = b * QI
                    for k in range(h0, h0 + 4):
                        ln_root(0, k + 2)
                        if k:
                            ln_low(0, k - 1, (k - 1) // QI)
                    ln_loop(g, h0, lambda q, k: ln_both(q, k, b))
                    for k in range(h0 + QI - 4, h0 + QI):
                        if k + 2 < Q:
                            ln_root(0, k + 2)
                        ln_low(0, k - 1, b)
                ln_low(0, Q - 1, PAIR - 1)

                def h_low(c, k):
                    m = c + (m0 + k)
                    g.wait_ge(h_hi, m + 1)
                    view = XN[:, bass.ds(c + k, 1), :, :].rearrange("p o (b r) l -> p (o b) r l", b=PAIR)
                    g.tensor_tensor(view[:, :, RAD:RAD + H, 1],
                                    t_hp[:, k % 2].rearrange("p (b r) -> p b r", b=PAIR),
                                    view[:, :, RAD:RAD + H, 0], ALU.subtract).then_inc(h_lo, 1)

                loop(g, 0, C, 2, h_low)

                def root2(q, k):
                    n = q + (n0 + k)
                    g.wait_ge(ag2, n + 1)
                    g.tensor_tensor(ve[:, k % 2], mv[:, k % 2, :, 1], epst[:, :], ALU.add)\
                     .then_inc(ve2, 1)
                    g.wait_ge(ve2, n + 1)
                    g.tensor_tensor(rstd[:, k % 2], ve[:, k % 2], mhalf[:, 0:R], ALU.pow).then_inc(rstd2, 1)

                def spread(q, k):
                    n = q + (n0 + k)
                    s = k % 2
                    g.wait_ge(w2_ready, n + 1)
                    g.tensor_tensor(wt1[:, :, :], oh1[:, :, :],
                                    w1[:, :].unsqueeze(2).broadcast_to([128, R, E]), ALU.mult).then_inc(wt_ready, 1)
                    g.tensor_tensor(wt2[:, :, :], oh2[:, :, :],
                                    w2[:, :].unsqueeze(2).broadcast_to([128, R, E]), ALU.mult).then_inc(wt_ready, 1)
                    g.wait_ge(wt_ready, 2 * n + 2)
                    wait_pos(g, acc_ready, n - 1, not (isinstance(q, int) and n < 2))
                    g.tensor_tensor(wsel[:, s], wt1[:, :, :], wt2[:, :, :], ALU.add).then_inc(w_ready, 1)

                def spread_low(q, k):
                    n = q + (n0 + k)
                    g.wait_ge(wh_ready, n + 1)
                    g.tensor_tensor(wcat[:, 1], wscl[:, :], wcat[:, 0], ALU.subtract).then_inc(wcat_ready, 1)

                def sum_row(q, k, r):
                    n = q + (n0 + k)
                    yr = ys[:, r * 512:(r + 2) * 512] if r >= dve_rows(k) else ys[:, r * 512:(r + 1) * 512]
                    g.wait_ge(act_part, n * R + r + 1)
                    if r >= dve_rows(k):
                        g.tensor_tensor(yr[:, 0:512], yr[:, 0:512], yr[:, 512:1024], ALU.add).then_inc(sum_8, 1)
                        g.wait_ge(sum_8, n + 1)
                    g.tensor_tensor(yr[:, 0:256], yr[:, 0:256], yr[:, 256:512], ALU.add).then_inc(sum_a, 1)
                    g.wait_ge(sum_a, n * R + r + 1)
                    wait_pos(g, out_ready, n, not (isinstance(q, int) and n < 1))
                    g.tensor_tensor(ysum[:, r], yr[:, 0:128], yr[:, 128:256], ALU.add).then_inc(sum_b, 1)

                def final(q, k):
                    n = q + (n0 + k)
                    g.wait_ge(sum_b, R * n + R)
                    g.wait_ge(acc_ready, n + 1)
                    g.tensor_tensor(outs[:, k % 2], acc[:, k % 2], ysum[:, :, :], ALU.add).then_inc(out_ready, 1)

                def step(t, k, a3, a2, a1, a0):
                    if a0:
                        sum_row(t, k, 0)
                        sum_row(t, k, 1)
                    if a2:
                        root2(t, k + 2)
                    if a0:
                        sum_row(t, k, 2)
                    if a1:
                        spread(t, k + 1)
                    if a0:
                        sum_row(t, k, 3)
                        final(t, k)
                    if a1:
                        spread_low(t, k + 1)

                for k in (-3, -2, -1):
                    step(0, k, True, k > -3, k > -2, False)
                loop(g, 0, Q - 4, 4, lambda t, k: step(t, k, True, True, True, True), pair == 0)
                for k in range(Q - 4, Q):
                    step(0, k, k + 3 < Q, k + 2 < Q, k + 1 < Q, True)

        @block.scalar
        def _(a):
            a.add_instruction(mybir.InstLoadActFuncSet(
                name=nc.get_next_instruction_name(), act_func_set_id=LN_EXP_SET, ins=[], outs=[],
                engine=mybir.EngineType.Activation))

            def corner(src, dst, func, **kw):
                a.activation(dst, src, func, **kw).then_inc(setup_a, 1)

            a.wait_ge(setup_p, P_CXT)
            for bank, w0, w1 in ((PT, 0, 7), (PX, 7, CW)):
                src = bank[:, :, :].rearrange("p r w -> p (r w)")[:, 0:(w1 - w0) * CR]
                corner(src.rearrange("p (w b r) -> p w b r", w=w1 - w0, b=NB),
                       cxT[:, w0:w1].rearrange("p w (r b) -> p w b r", b=NB), ACT.Copy)
            a.wait_ge(setup_a, A_CXT)
            for tap in range(KS * KS):
                if tap >= 2:
                    a.wait_ge(taps_g, tap)
                part, weight = corner_tap(2, tap)
                a.activation(prod[:, tap % 2], part, ACT.Copy, scale=weight).then_inc(taps_a, 1)
            flat = [ccv[:, k].rearrange("p w r -> p (w r)") for k in range(NCV)]
            a.wait_ge(taps_v, 2 * KS * KS)
            corner(flat[0], ctm[0], ACT.Exp, scale=-1.0)
            a.wait_ge(taps_g, KS * KS + 1)
            corner(flat[1], ctm[1], ACT.Exp, scale=-1.0)
            a.wait_ge(setup_v, S_CVAL)
            corner(ctm[2], ctm[4], ACT.Abs)
            corner(ctm[3], ctm[6], ACT.Exp)
            a.wait_ge(setup_a, A_ABS)
            corner(ctm[4], ctm[5], ACT.Exp, scale=-1.0)
            a.wait_ge(setup_a, A_EXPN)
            corner(ctm[5], ctm[7], ACT.Ln, bias=1.0)

            for pair in range(PAIRS):
                n0, m0 = pair * Q, pair * C

                def ln_scale(q, k):
                    n = q + (n0 + k)
                    a.wait_ge(nmr_ready, n + 1)
                    wait_pos(a, ln_lo, n - 3, not (isinstance(q, int) and n < 4))
                    wait_pos(a, ln_lod, n - 3, not (isinstance(q, int) and n < 4))
                    for r in range(DVE_LN, R):
                        ins = a.activation(xns(k)[:, r], xs(k)[:, r], ACT.Identity,
                                           scale=rstd[:, k % 2, r:r + 1], bias=nmr[:, k % 2, r:r + 1])
                    ins.then_inc(ln_xa, 1)

                def ln_high(q, k, b):
                    n = q + (n0 + k)
                    a.wait_ge(ln_xc, n + 1)
                    a.wait_ge(ln_xa, n + 1)
                    at = q * R + row0(k, b)
                    a.activation(XN[:, :, bass.ds(at, R), 0], xns(k).rearrange("p r c -> p c r"),
                                 ACT.Copy).then_inc(ln_hi, 1)

                def ln_step(q, k, b):
                    ln_scale(q, k)
                    ln_high(q, k - 1, b)

                if pair == 0:
                    a.wait_ge(fixed_out, 16)
                    a.wait_ge(brow_in, 48)
                    a.wait_ge(table_out, 16)
                else:
                    a.wait_ge(out_sent[0], 16 * n0 // 2)
                    a.wait_ge(out_sent[1], 16 * n0 // 2)
                for b in range(PAIR):
                    h0 = b * QI
                    ln_scale(0, h0)
                    if b:
                        ln_high(0, h0 - 1, b - 1)
                    for k in range(h0 + 1, h0 + 4):
                        ln_step(0, k, b)
                    ln_loop(a, h0, lambda q, k: ln_step(q, k, b))
                    for k in range(h0 + QI - 4, h0 + QI):
                        ln_step(0, k, b)
                ln_high(0, Q - 1, PAIR - 1)

                def gate(c, k):
                    m = c + (m0 + k)
                    a.wait_ge(conv_done, m + 1)
                    wait_pos(a, gate_rec, m - 1, not (isinstance(c, int) and m < 2))
                    a.activation(t_eg[:, k % 2], PY[k % 4][:, 0:256], ACT.Exp,
                                 scale=sc[:, NSG:NSG + 1]).then_inc(gate_exp, 1)

                def softplus_log(c, k):
                    m = c + (m0 + k)
                    s = k % 2
                    a.wait_ge(val, m + 1)
                    wait_pos(a, h_sum, m - 1, not (isinstance(c, int) and m < 2))
                    a.activation(t_l[:, s], t_v[:, s], ACT.Abs).then_inc(absv, 1)
                    a.wait_ge(absv, m + 1)
                    a.activation(t_l[:, s], t_l[:, s], ACT.Exp, scale=-1.0).then_inc(expn, 1)
                    a.wait_ge(expn, m + 1)
                    a.activation(t_l[:, s], t_l[:, s], ACT.Ln, bias=1.0).then_inc(logp, 1)

                def conv_end(c, k):
                    gate(c, k + 1)
                    softplus_log(c, k)

                gate(0, 0)
                loop(a, 0, C - 4, 4, conv_end, pair == 0)
                for k in range(C - 4, C - 1):
                    conv_end(0, k)
                softplus_log(0, C - 1)

                def h_copy(q, k):
                    n = q + (n0 + k)
                    a.wait_ge(t1_done, n + 1)
                    wait_pos(a, wout_done, n, not (isinstance(q, int) and n < 1))
                    a.activation(hT[:, :, :], PT[:, :, :], ACT.Copy).then_inc(hT_ready, 1)

                def x_high(q, k):
                    n = q + (n0 + k)
                    a.wait_ge(t2_done, n + 1)
                    wait_pos(a, moe_done, (n - 1) * R, not (isinstance(q, int) and n < 2))
                    a.activation(xTh[:, k % 2], PX[:, :, :], ACT.Copy).then_inc(xTh_ready, 1)

                def w_copy(q, k):
                    n = q + (n0 + k)
                    a.wait_ge(wT_done, n + 1)
                    wait_pos(a, pb_done, n, not (isinstance(q, int) and n < 1))
                    a.activation(wTs[:, :], PWT, ACT.Copy).then_inc(wTs_ready, 1)

                def weigh_half(k, r, place, s):
                    for e in range(HALF):
                        at = r * 512 + (place * HALF + e) * C
                        ins = a.activation(ys[:, at:at + C], PY[2 * (r % 2) + s][:, e * C:(e + 1) * C],
                                           ACT.Copy, scale=wsel[:, k % 2, r, s * HALF + e:s * HALF + e + 1])
                    return ins

                def weigh(q, k, r):
                    n = q + (n0 + k)
                    a.wait_ge(moe_done, n * R + r + 1)
                    a.wait_ge(w_ready, n + 1)
                    wait_pos(a, sum_b, (n - 1) * R + r + 1, not (isinstance(q, int) and n < 1))
                    ins = weigh_half(k, r, 0, 1)
                    if r < dve_rows(k):
                        ins.then_inc(act_part, 1)

                def weigh_rest(k, r):
                    if r >= dve_rows(k):
                        weigh_half(k, r, 1, 0).then_inc(act_part, 1)

                def normalise(q, k):
                    n = q + (n0 + k)
                    a.wait_ge(nmr2, n + 1)
                    wait_pos(a, t2_done, n - 1, not (isinstance(q, int) and n < 2))
                    for r in range(R):
                        ins = a.activation(xc[:, k % 2, r], x1[:, k % 4, r], ACT.Identity,
                                           scale=rstd[:, k % 2, r:r + 1], bias=nmr[:, k % 2, r:r + 1])
                    ins.then_inc(xc2_ready, 1)

                def w_parts(q, k):
                    n = q + (n0 + k)
                    a.wait_ge(w_ready, n + 1)
                    wait_pos(a, wT_done, n, not (isinstance(q, int) and n < 1))
                    a.activation(wscl[:, :], wsel[:, k % 2].rearrange("p r e -> p (r e)"), ACT.Copy,
                                 scale=sc[:, KWE:KWE + 1]).then_inc(wscl_ready, 1)
                    a.wait_ge(wscl_ready, n + 1)
                    a.activation(wcat[:, 0:3:2], wscl[:, :].unsqueeze(1).broadcast_to([128, 2, R * E]),
                                 ACT.Copy).then_inc(wh_ready, 1)

                def gap_exp(q, k):
                    n = q + (n0 + k)
                    a.wait_ge(gap_ready, n + 1)
                    a.activation(eg2[:, :], gap[:, :], ACT.Exp).then_inc(e_ready, 1)

                def step(t, k, a3, a2, a1, a0):
                    if a0:
                        weigh(t, k, 0)
                    if a1:
                        x_high(t, k + 1)
                    if a0:
                        weigh(t, k, 1)
                        weigh(t, k, 2)
                        weigh(t, k, 3)
                    if a1:
                        gap_exp(t, k + 1)
                    if a0:
                        w_copy(t, k)
                        weigh_rest(k, 3)
                    if a3:
                        h_copy(t, k + 3)
                    if a2:
                        normalise(t, k + 2)
                    if a1:
                        w_parts(t, k + 1)

                for k in (-3, -2, -1):
                    step(0, k, True, k > -3, k > -2, False)
                loop(a, 0, Q - 4, 4, lambda t, k: step(t, k, True, True, True, True), pair == 0)
                for k in range(Q - 4, Q):
                    step(0, k, k + 3 < Q, k + 2 < Q, k + 1 < Q, True)

        @block.vector
        def _(v):
            done = [0]

            def setup(ins):
                done[0] += 1
                ins.then_inc(setup_v, 1)
                v.wait_ge(setup_v, done[0])

            def after(name):
                assert done[0] == SETUP[name], (name, done[0])

            v.wait_ge(weights_in, 16 * NW_IN)
            v.wait_ge(consts, 4)
            v.wait_ge(zeroed, 3)
            for col, src in ((GB, kraw[:, 0]), (BB, kraw[:, 1])):
                setup(v.tensor_reduce(w_abs[:, col:col + 1], src.rearrange("p i j -> p (i j)"), AX, ALU.max,
                                      apply_absolute_value=True))
            setup(v.tensor_reduce(w_abs[:, EW:EW + 1], we_raw.rearrange("p e c -> p (e c)"), AX, ALU.max,
                                  apply_absolute_value=True))
            setup(v.tensor_reduce(w_abs[:, RW:RW + 1], rw_raw, AX, ALU.max, apply_absolute_value=True))
            setup(v.tensor_reduce(w_abs[0:96, EB:EB + 1], eb_raw[0:96].rearrange("p r c -> p (r c)"), AX,
                                  ALU.max, apply_absolute_value=True))
            after("ABS")
            v.wait_ge(setup_p, P_ABST)
            setup(v.tensor_reduce(colmax[0:NSC], PM[0:NSC, 0:128], AX, ALU.max))
            setup(v.tensor_scalar(diag5[0:NSC], identf[0:NSC, 0:NSC], colmax[0:NSC, 0:1], None, ALU.mult))
            after("DIAG")
            v.wait_ge(setup_p, P_MAX)
            setup(v.tensor_scalar(pw2[:, :], PM[:, 128:128 + NSC], 2.0 ** -60, None, ALU.max))
            setup(v.tensor_scalar(pw2[:, :].bitcast(i32), pw2[:, :].bitcast(i32), 0x7F800000, None,
                                  ALU.bitwise_and))
            setup(v.reciprocal(inv[:, :], pw2[:, :]))

            def scale(dst, src, *ops):
                (o1, v1), (o2, v2) = ops if len(ops) == 2 else (ops[0], (None, None))
                if o2 is None:
                    setup(v.tensor_scalar(sc[:, dst:dst + 1], src, v1, None, o1))
                else:
                    setup(v.tensor_scalar(sc[:, dst:dst + 1], src, v1, v2, o1, o2))

            WS = 1.0 / KSC
            scale(IKAP, pw2[:, BB:BB + 1], (ALU.mult, 1.0 / 32), (ALU.max, 1.0))
            setup(v.reciprocal(sc[:, KAP:KAP + 1], sc[:, IKAP:IKAP + 1]))
            scale(NSG, pw2[:, GB:GB + 1], (ALU.mult, -WS))
            scale(SBV, pw2[:, BB:BB + 1], (ALU.mult, WS))
            scale(ISE, inv[:, EW:EW + 1], (ALU.mult, 1.0 / WS))
            scale(SR, pw2[:, RW:RW + 1], (ALU.mult, WS))
            scale(SEB, pw2[:, EB:EB + 1], (ALU.mult, KSC ** -2))
            scale(KWE, sc[:, ISE:ISE + 1], (ALU.mult, KSC))
            for k, col in ((0, GB), (1, BB)):
                setup(v.tensor_scalar(ksc[:, k], kraw[:, k], inv[:, col:col + 1], KSC, ALU.mult, ALU.mult))
            for k in range(2):
                cell = table[:, MID - RAD:MID + RAD + 1, k * 2 * KS:(k + 1) * 2 * KS]
                cell = cell.rearrange("p j (i l) -> p i j l", l=2)
                setup(v.tensor_copy(cell[:, :, :, 0], ksc[:, k, :, ::-1]))
                setup(v.tensor_tensor(cell[:, :, :, 1], ksc[:, k, :, ::-1], cell[:, :, :, 0], ALU.subtract))
            after("TABLE")
            setup(v.tensor_scalar(we_sc, we_raw, inv[:, EW:EW + 1], KSC, ALU.mult, ALU.mult))
            setup(v.tensor_copy(weh[:, :, :], we_sc))
            setup(v.tensor_tensor(wel[:, :, :], we_sc, weh[:, :, :], ALU.subtract))
            setup(v.tensor_scalar(rw_sc, rw_raw, inv[:, RW:RW + 1], KSC, ALU.mult, ALU.mult))
            setup(v.tensor_copy(rwh[:, :], rw_sc))
            setup(v.tensor_tensor(rwl[:, :], rw_sc, rwh[:, :], ALU.subtract))
            setup(v.tensor_scalar(eb_sc[0:96], eb_raw[0:96], inv[0:96, EB:EB + 1], KSC, ALU.mult, ALU.mult))
            setup(v.tensor_copy(eb_hi[0:96], eb_sc[0:96]))
            setup(v.tensor_copy(bblk[0:64], eb_hi[0:64]))
            setup(v.tensor_tensor(bblk[64:96], eb_sc[64:96], eb_hi[64:96], ALU.subtract))
            setup(v.tensor_scalar(wf[:, :], w_raw, F0, None, ALU.mult))
            v.wait_ge(setup_p, P_COLSUM)
            setup(v.scalar_tensor_tensor(out=brd[0:1, 0:C], in0=PM[0:1, 256:256 + C], scalar=F0 * EPS_SCAN,
                                         in1=brf[0:1, :], op0=ALU.mult, op1=ALU.add))
            setup(v.tensor_scalar(brd[0:1, 0:C], brd[0:1, 0:C], sc[0:1, KAP:KAP + 1], None, ALU.mult))
            for k in range(3):
                setup(v.tensor_copy(b3[0:1, k], brd[0:1, 0:C]))
                if k < 2:
                    setup(v.tensor_tensor(brd[0:1, 0:C], brd[0:1, 0:C], b3[0:1, k], ALU.subtract))
            after("B3")

            v.wait_ge(corner_in, 16 * 4 * NB)
            for w in range(CW):
                ins = v.bn_stats(cst[0:CR, w], cx[0:CR, w])
            setup(ins)
            for w in range(CW):
                ins = v.bn_aggr(cmv[0:CR, w], cst[0:CR, w])
            setup(ins)
            setup(v.tensor_scalar(cve[0:CR], cmv[0:CR, :, 1], EPS1, None, ALU.add))
            after("CVE")
            v.wait_ge(setup_g, 1)
            for w in range(CW):
                ins = v.tensor_scalar(cxn[0:CR, w], cx[0:CR, w], cmv[0:CR, w, 0:1], crs[0:CR, w:w + 1],
                                      ALU.subtract, ALU.mult)
            setup(ins)
            after("CXN")
            v.wait_ge(setup_a, A_CXT)
            setup(v.memset(ccv[:, 0], 0.0))
            setup(v.memset(ccv[:, 2], 0.0))
            for tap in range(KS * KS):
                for place, (k, kern) in enumerate(((0, 0), (2, 1))):
                    if tap:
                        v.wait_ge(taps_v, 2 * tap + place - 1)
                    part, weight = corner_tap(kern, tap)
                    v.scalar_tensor_tensor(out=ccv[:, k], in0=part, scalar=weight, in1=ccv[:, k],
                                           op0=ALU.mult, op1=ALU.add).then_inc(taps_v, 1)
            v.wait_ge(taps_v, 2 * KS * KS)
            v.wait_ge(setup_a, A_GATES)
            for k in range(2):
                setup(v.tensor_scalar(ctm[k], ctm[k], 1.0, None, ALU.add))
                setup(v.reciprocal(ctm[k], ctm[k]))
            setup(v.tensor_tensor(ctm[2], ccv[:, 2].rearrange("p w r -> p (w r)"), ctm[0], ALU.mult))
            ta = ctm[3].rearrange("p (w r b) -> p w r b", w=KS, b=NB)
            tg = ctm[1].rearrange("p (w r b) -> p w r b", w=KS, b=NB)
            for b in range(NB):
                ins = v.tensor_tensor(ta[:, :, :, b], tg[:, :, :, b],
                                      kraw[:, 3].rearrange("p i j -> p j i"), ALU.mult)
            setup(ins)
            after("CVAL")
            v.wait_ge(setup_a, A_LN)
            setup(v.scalar_tensor_tensor(out=ctm[0], in0=ctm[2], scalar=0.0, in1=ctm[7], op0=ALU.max,
                                         op1=ALU.add))
            setup(v.tensor_scalar(ctm[6], ctm[6], 1.0, None, ALU.add))
            setup(v.reciprocal(ctm[1], ctm[6]))
            setup(v.tensor_scalar(ctm[2], ctm[1], -1.0, 1.0, ALU.mult, ALU.add))
            power = ctm[1]
            free = [ctm[4], ctm[5]]
            terms = 1
            while terms < STEPS:
                setup(v.scalar_tensor_tensor(out=ctm[2], in0=power, scalar=1.0, in1=ctm[2], op0=ALU.add,
                                             op1=ALU.mult))
                terms *= 2
                if terms < STEPS:
                    nxt = free.pop(0)
                    setup(v.tensor_tensor(nxt, power, power, ALU.mult))
                    power = nxt
            setup(v.tensor_scalar(ctm[2], ctm[2], -F0, None, ALU.add))
            setup(v.scalar_tensor_tensor(out=ctm[3], in0=ctm[0], scalar=EPS_SCAN, in1=ctm[2], op0=ALU.add,
                                         op1=ALU.mult))
            after("CDELTA")
            v.wait_ge(setup_p, P_CW)
            v.wait_ge(corner7_in, 16 * 2 * KS)
            for half, bank in ((0, PY[0]), (1, PY[1])):
                lo, hi = (0, 4) if half == 0 else (4, KS)
                setup(v.tensor_tensor(cfix[0:KR, lo:hi], cx7[0:KR, lo:hi],
                                      bank[0:KR, 0:(hi - lo) * C].rearrange("p (w c) -> p w c", c=C), ALU.add))
            after("CFIX")

            for pair in range(PAIRS):
                n0, m0 = pair * Q, pair * C

                def ln_stat(q, k):
                    n = q + (n0 + k)
                    v.wait_ge(x_in[k % XS], (q + (n0 + k - k % XS + XS)) * (16 // XS))
                    for r in range(R):
                        ins = v.bn_stats(stats[:, k % 2, r], xs(k)[:, r])
                    ins.then_inc(ln_stats, 1)

                def ln_moments(q, k):
                    for r in range(R):
                        ins = v.bn_aggr(mv[:, k % 4, r], stats[:, k % 2, r])
                    ins.then_inc(ln_aggr, 1)

                def ln_eps(q, k):
                    n = q + (n0 + k)
                    v.wait_ge(ln_aggr, n + 1)
                    wait_pos(v, ln_rstd, n - 1, not (isinstance(q, int) and n < 2))
                    v.tensor_scalar(ve[:, k % 2], mv[:, k % 4, :, 1], EPS1, None, ALU.add).then_inc(ln_ve, 1)

                def ln_apply(q, k, ahead):
                    n = q + (n0 + k)
                    v.wait_ge(ln_rstd, n + 1)
                    wait_pos(v, ln_xa, n - 1, not (isinstance(q, int) and n < 2))
                    v.scalar_tensor_tensor(out=nmr[:, k % 2], in0=mv[:, k % 4, :, 0], scalar=-1.0,
                                           in1=rstd[:, k % 2], op0=ALU.mult, op1=ALU.mult)\
                     .then_inc(nmr_ready, 1)
                    wait_pos(v, ln_lo, n - 3, not (isinstance(q, int) and n < 4))
                    wait_pos(v, ln_lod, n - 3, not (isinstance(q, int) and n < 4))
                    if ahead:
                        v.wait_ge(ln_stats, q + (n0 + k + 3))
                    for r in range(DVE_LN):
                        ins = v.tensor_scalar(xns(k)[:, r], xs(k)[:, r], mv[:, k % 4, r, 0:1],
                                              rstd[:, k % 2, r:r + 1], ALU.subtract, ALU.mult)
                    ins.then_inc(ln_xc, 1)

                def ln_low(q, k, b):
                    n = q + (n0 + k)
                    v.wait_ge(ln_hi, n + 1)
                    at = q * R + row0(k, b)
                    view = XN[:, :, bass.ds(at, DVE_LO), :]
                    v.tensor_tensor(view[:, :, :, 1], xns(k)[:, 0:DVE_LO].rearrange("p r c -> p c r"),
                                    view[:, :, :, 0], ALU.subtract).then_inc(ln_lod, 1)

                def ln_step(q, k, b, ahead, behind):
                    if ahead:
                        ln_stat(q, k + 2)
                    ln_apply(q, k, ahead)
                    if ahead:
                        ln_moments(q, k + 2)
                    if behind:
                        ln_low(q, k - 2, b)
                    if ahead:
                        ln_eps(q, k + 2)

                for k in range(2):
                    ln_stat(0, k)
                    v.wait_ge(ln_stats, n0 + k + 1)
                    ln_moments(0, k)
                    ln_eps(0, k)
                if pair:
                    v.wait_ge(out_sent[0], 16 * n0 // 2)
                    v.wait_ge(out_sent[1], 16 * n0 // 2)
                for b in range(PAIR):
                    h0 = b * QI
                    for k in range(h0, h0 + 4):
                        ln_step(0, k, (k - 2) // QI, True, k > 1)
                    ln_loop(v, h0, lambda q, k: ln_step(q, k, b, True, True))
                    for k in range(h0 + QI - 4, h0 + QI):
                        ln_step(0, k, b, k + 2 < Q, True)
                ln_low(0, Q - 2, PAIR - 1)
                ln_low(0, Q - 1, PAIR - 1)
                v.wait_ge(ln_lo, n0 + Q)
                v.wait_ge(ln_lod, n0 + Q)
                xi = XN[:, :, :, :].rearrange("p c (b r) l -> p c b (r l)", b=PAIR).bitcast(i32)
                for b in range(PAIR):
                    v.tensor_copy(xi[:, :, b, 0:RAD], xi[:, :, b, H:H + RAD]).then_inc(halo, 1)
                    v.tensor_copy(xi[:, :, b, H + RAD:HP], xi[:, :, b, RAD:2 * RAD]).then_inc(halo, 1)

                def value(c, k):
                    m = c + (m0 + k)
                    s = k % 2
                    v.wait_ge(gate_exp, m + 1)
                    v.tensor_scalar(t_eg[:, s], t_eg[:, s], 1.0, None, ALU.add).then_inc(gate_den, 1)
                    v.wait_ge(gate_den, m + 1)
                    v.reciprocal(t_rs[:, s], t_eg[:, s]).then_inc(gate_rec, 1)
                    v.wait_ge(gate_rec, m + 1)
                    wait_pos(v, absv, m - 1, not (isinstance(c, int) and m < 2))
                    v.scalar_tensor_tensor(out=t_v[:, s], in0=PY[k % 4][:, 256:512], scalar=sc[:, SBV:SBV + 1],
                                           in1=t_rs[:, s], op0=ALU.mult, op1=ALU.mult).then_inc(val, 1)
                    v.wait_ge(val, m + 1)
                    v.tensor_scalar(t_relu[:, s], t_v[:, s], sc[:, KAP:KAP + 1], 0.0, ALU.mult, ALU.max)\
                     .then_inc(relu, 1)

                def finish(c, k):
                    m = c + (m0 + k)
                    s = k % 2
                    v.wait_ge(logp, m + 1)
                    v.wait_ge(relu, m + 1)
                    wait_pos(v, h_lo, m - 1, not (isinstance(c, int) and m < 2))
                    v.scalar_tensor_tensor(out=t_hp[:, s], in0=t_l[:, s], scalar=sc[:, KAP:KAP + 1],
                                           in1=t_relu[:, s], op0=ALU.mult, op1=ALU.add).then_inc(h_sum, 1)
                    v.wait_ge(h_sum, m + 1)
                    view = XN[:, bass.ds(c + k, 1), :, :].rearrange("p o (b r) l -> p (o b) r l", b=PAIR)
                    v.tensor_copy(view[:, :, RAD:RAD + H, 0],
                                  t_hp[:, s].rearrange("p (b r) -> p b r", b=PAIR)).then_inc(h_hi, 1)

                def conv_end(c, k):
                    value(c, k + 1)
                    finish(c, k)

                value(0, 0)
                loop(v, 0, C - 4, 4, conv_end, pair == 0)
                for k in range(C - 4, C - 1):
                    conv_end(0, k)
                finish(0, C - 1)

                def residual(q, k):
                    n = q + (n0 + k)
                    v.wait_ge(wout_done, n + 1)
                    v.wait_ge(x2_in[k % 4], (q + (n0 + k - k % 4 + 4)) * 4)
                    v.scalar_tensor_tensor(out=x1[:, k % 4], in0=PW[:, :, :], scalar=sc[:, IKAP:IKAP + 1],
                                           in1=xin[:, k % 4], op0=ALU.mult, op1=ALU.add).then_inc(x1_ready, 1)

                def stat(q, k, r):
                    if r == 0:
                        v.wait_ge(x1_ready, q + (n0 + k + 1))
                    ins = v.bn_stats(stats[:, k % 2, r], x1[:, k % 4, r])
                    if r == R - 1:
                        ins.then_inc(st2, 1)

                def moments(q, k):
                    for r in range(R):
                        ins = v.bn_aggr(mv[:, k % 2, r], stats[:, k % 2, r])
                    ins.then_inc(ag2, 1)

                def mean_root(q, k):
                    n = q + (n0 + k)
                    v.wait_ge(rstd2, n + 1)
                    wait_pos(v, xc2_ready, n - 1, not (isinstance(q, int) and n < 2))
                    v.scalar_tensor_tensor(out=nmr[:, k % 2], in0=mv[:, k % 2, :, 0], scalar=-1.0,
                                           in1=rstd[:, k % 2], op0=ALU.mult, op1=ALU.mult).then_inc(nmr2, 1)

                def x_low(q, k):
                    n = q + (n0 + k)
                    v.wait_ge(xTh_ready, n + 1)
                    v.tensor_tensor(xTl[:, k % 2], PX[:, :, :], xTh[:, k % 2], ALU.subtract)\
                     .then_inc(xTl_ready, 1)

                def route(q, k):
                    n = q + (n0 + k)
                    v.wait_ge(router_done, n + 1)
                    v.scalar_tensor_tensor(out=lg[:, :, :].rearrange("p r e -> p (r e)"), in0=PR,
                                           scalar=sc[:, SR:SR + 1],
                                           in1=rb4[:, :, :].rearrange("p r e -> p (r e)"),
                                           op0=ALU.mult, op1=ALU.add).then_inc(lg_ready, 1)

                def largest(q, k):
                    for r in range(R):
                        ins = v.max(mx[:, r], lg[:, r])
                    ins.then_inc(mx_ready, 1)

                def places(q, k):
                    n = q + (n0 + k)
                    v.wait_ge(mx_ready, n + 1)
                    v.tensor_tensor(gap[:, :], mx[:, :, 1], mx[:, :, 0], ALU.subtract).then_inc(gap_ready, 1)
                    for r in range(R):
                        ins = v.max_index(mi[:, r], mx[:, r], lg[:, r])
                    ins.then_inc(mi_ready, 1)

                def one_hot(q, k):
                    n = q + (n0 + k)
                    v.wait_ge(mi_ready, n + 1)
                    wait_pos(v, wt_ready, 2 * n, not (isinstance(q, int) and n < 1))
                    for o, j in ((oh1, 0), (oh2, 1)):
                        ins = v.tensor_tensor(o[:, :, :], iota8[:, :, :],
                                              mi[:, :, j:j + 1].broadcast_to([128, R, E]), ALU.is_equal)
                    ins.then_inc(oh_ready, 1)

                def denominator(q, k):
                    n = q + (n0 + k)
                    v.wait_ge(e_ready, n + 1)
                    v.tensor_scalar(wden[:, :], eg2[:, :], 1.0, sc[:, ISE:ISE + 1], ALU.add, ALU.mult)\
                     .then_inc(wden_ready, 1)

                def first_share(q, k):
                    v.wait_ge(wden_ready, q + (n0 + k + 1))
                    v.reciprocal(w1[:, :], wden[:, :]).then_inc(w1_ready, 1)

                def second_share(q, k):
                    v.wait_ge(w1_ready, q + (n0 + k + 1))
                    v.tensor_tensor(w2[:, :], eg2[:, :], w1[:, :], ALU.mult).then_inc(w2_ready, 1)

                def weigh(q, k, r, e):
                    n = q + (n0 + k)
                    if r >= dve_rows(k):
                        return
                    pair_sum = (dve_rows(0) + dve_rows(1)) * HALF
                    before = (q + (n0 + k - k % 2)) * (pair_sum // 2) \
                        + (dve_rows(0) * HALF if k % 2 else 0)
                    if e == 0:
                        v.wait_ge(moe_done, n * R + r + 1)
                        v.wait_ge(w_ready, n + 1)
                        if r == 0 and not (isinstance(q, int) and n < 2):
                            v.wait_ge(out_sent[k % 2], (q + (n0 + k - k % 2)) * 8)
                    else:
                        v.wait_ge(dve_part, before + (r * HALF + e))
                    py = PY[2 * (r % 2)]
                    v.scalar_tensor_tensor(out=acc[:, k % 2, r], in0=py[:, e * C:(e + 1) * C],
                                           scalar=wsel[:, k % 2, r, e:e + 1],
                                           in1=acc[:, k % 2, r] if e else x1[:, k % 4, r],
                                           op0=ALU.mult, op1=ALU.add).then_inc(dve_part, 1)

                def bias(q, k):
                    n = q + (n0 + k)
                    rows = dve_rows(k)
                    v.wait_ge(pb_done, n + 1)
                    if rows < R:
                        v.scalar_tensor_tensor(out=acc[:, k % 2, rows:R], in0=PW[:, rows:R],
                                               scalar=sc[:, SEB:SEB + 1], in1=x1[:, k % 4, rows:R],
                                               op0=ALU.mult, op1=ALU.add)
                    pair_sum = (dve_rows(0) + dve_rows(1)) * HALF
                    before = (q + (n0 + k - k % 2)) * (pair_sum // 2)
                    v.wait_ge(dve_part, before + (pair_sum if k % 2 else dve_rows(0) * HALF))
                    v.scalar_tensor_tensor(out=acc[:, k % 2, 0:rows], in0=PW[:, 0:rows],
                                           scalar=sc[:, SEB:SEB + 1], in1=acc[:, k % 2, 0:rows],
                                           op0=ALU.mult, op1=ALU.add).then_inc(acc_ready, 1)

                def step(t, k, a3, a2, a1, a0):
                    if a0:
                        weigh(t, k, 0, 0)
                        weigh(t, k, 0, 1)
                        weigh(t, k, 0, 2)
                        weigh(t, k, 0, 3)
                        weigh(t, k, 1, 0)
                        weigh(t, k, 1, 1)
                    if a2:
                        residual(t, k + 2)
                    if a0:
                        weigh(t, k, 1, 2)
                    if a2:
                        stat(t, k + 2, 0)
                    if a1:
                        x_low(t, k + 1)
                    if a0:
                        weigh(t, k, 1, 3)
                    if a2:
                        stat(t, k + 2, 1)
                        stat(t, k + 2, 2)
                        stat(t, k + 2, 3)
                        v.wait_ge(st2, t + (n0 + k + 3))
                    if a0:
                        weigh(t, k, 2, 0)
                    if a2:
                        moments(t, k + 2)
                    if a0:
                        weigh(t, k, 2, 1)
                    if a1:
                        route(t, k + 1)
                        v.wait_ge(lg_ready, t + (n0 + k + 2))
                    if a0:
                        weigh(t, k, 2, 2)
                    if a1:
                        largest(t, k + 1)
                    if a0:
                        weigh(t, k, 2, 3)
                    if a1:
                        places(t, k + 1)
                    if a0:
                        weigh(t, k, 3, 0)
                    if a1:
                        one_hot(t, k + 1)
                        denominator(t, k + 1)
                    if a0:
                        weigh(t, k, 3, 1)
                    if a1:
                        first_share(t, k + 1)
                    if a0:
                        weigh(t, k, 3, 2)
                    if a1:
                        second_share(t, k + 1)
                    if a2:
                        mean_root(t, k + 2)
                    if a0:
                        weigh(t, k, 3, 3)
                        bias(t, k)

                for k in (-3, -2, -1):
                    step(0, k, True, k > -3, k > -2, False)
                loop(v, 0, Q - 4, 4, lambda t, k: step(t, k, True, True, True, True), pair == 0)
                for k in range(Q - 4, Q):
                    step(0, k, k + 3 < Q, k + 2 < Q, k + 1 < Q, True)

        @block.tensor
        def _(p):
            p.wait_ge(consts, 4)
            p.wait_ge(setup_v, S_ABS)
            p.transpose(PM[0:NSC, 0:128], w_abs, identf[:, :]).then_inc(setup_p, 1)
            p.wait_ge(setup_v, S_DIAG)
            p.matmul(PM[:, 128:128 + NSC], onesf[0:NSC, :], diag5[0:NSC], start=True, stop=True)\
             .then_inc(setup_p, 1)
            p.wait_ge(setup_v, S_DIAG + 1)
            p.matmul(PM[0:1, 256:256 + C], onesf[:, 0:1], w_raw, start=True, stop=True).then_inc(setup_p, 1)
            p.wait_ge(setup_v, S_CXN)
            for w in range(CW):
                bank, at = (PT, w) if w < 7 else (PX, w - 7)
                ins = p.transpose(bank[:, :, :].rearrange("p r w -> p (r w)")[:, at * CR:(at + 1) * CR],
                                  cxn[0:CR, w], identf[0:CR, 0:CR])
            ins.then_inc(setup_p, 1)
            p.wait_ge(setup_v, S_CDELTA)
            dh = ctm[3].rearrange("p (w r) -> p w r", w=KS)
            for w in range(KS):
                ins = p.matmul(PY[w // 4][0:KR, (w % 4) * C:(w % 4 + 1) * C], dh[:, w], w_raw, start=True,
                               stop=True)
            ins.then_inc(setup_p, 1)

            for pair in range(PAIRS):
                n0, m0 = pair * Q, pair * C

                def conv(c, k):
                    m = c + (m0 + k)
                    p.wait_ge(circ_in[(k % 4) // GRP], (c + (m0 + k - k % 4 + 4)) * (4 * 10))
                    wait_pos(p, val, m - 3, not (isinstance(c, int) and m < 4))
                    view = XN[:, bass.ds(c + k, 1), :, :].rearrange("p o (b r) l -> p (o b) r l", b=PAIR)
                    for cv in range(2):
                        into = PY[k % 4][:, cv * 256:(cv + 1) * 256].rearrange("p (b r) -> p b r", b=PAIR)
                        for i in range(KS):
                            for part, (wl, xl) in enumerate(((0, 0), (0, 1), (1, 0))):
                                ins = p.matmul(into, circ[:, k % 4, :, (cv * KS + i) * 2 + wl],
                                               view[:, :, 2 * RAD - i:2 * RAD - i + H, xl],
                                               start=(i == 0 and part == 0), stop=(i == KS - 1 and part == 2))
                    ins.then_inc(conv_done, 1)

                p.wait_ge(halo, 2 * PAIR * (pair + 1))
                if pair == 0:
                    p.wait_ge(setup_v, S_CFIX)
                else:
                    p.wait_ge(act_part, n0 * R)
                    p.wait_ge(dve_part, n0 // 2 * (dve_rows(0) + dve_rows(1)) * HALF)
                loop(p, 0, C, 4, conv, pair == 0)

                def turn_h(q, k):
                    n = q + (n0 + k)
                    wait_pos(p, hT_ready, n, not (isinstance(q, int) and n < 1))
                    at = (q + k) * R + ((q + k) // QI) * (2 * RAD) + RAD
                    for r in range(R):
                        for part in range(2):
                            src = XN[:, :, bass.ds(at + r, 1), part].rearrange("p c o -> p (c o)")
                            ins = p.matmul(PT[:, r], src, mirror[:, :], start=part == 0, stop=part == 1)
                    ins.then_inc(t1_done, 1)

                def project(q, k):
                    n = q + (n0 + k)
                    p.wait_ge(hT_ready, n + 1)
                    wait_pos(p, x1_ready, n, not (isinstance(q, int) and n < 1))
                    wait_pos(p, acc_ready, n - 2, not (isinstance(q, int) and n < 3))
                    for r in range(R):
                        p.matmul(PW[:, r], ones3[:, :], brow[:, :], start=True, stop=False)
                        ins = p.matmul(PW[:, r], hT[:, r], wf[:, :], start=False, stop=True)
                    ins.then_inc(wout_done, 1)

                def turn_x(q, k):
                    n = q + (n0 + k)
                    p.wait_ge(xc2_ready, n + 1)
                    wait_pos(p, xTl_ready, n, not (isinstance(q, int) and n < 1))
                    for r in range(R):
                        ins = p.transpose(PX[:, r], xc[:, k % 2, r], identf[:, :])
                    ins.then_inc(t2_done, 1)

                def router(q, k):
                    n = q + (n0 + k)
                    p.wait_ge(xTl_ready, n + 1)
                    wait_pos(p, wTs_ready, n - 1, not (isinstance(q, int) and n < 2))
                    for r in range(R):
                        into = PR[:, r * E:(r + 1) * E]
                        p.matmul(into, xTh[:, k % 2, r], rwh[:, :], start=True, stop=False)
                        p.matmul(into, xTh[:, k % 2, r], rwl[:, :], start=False, stop=False)
                        ins = p.matmul(into, xTl[:, k % 2, r], rwh[:, :], start=False, stop=True)
                    ins.then_inc(router_done, 1)

                def turn_w(q, k, ahead):
                    n = q + (n0 + k)
                    p.wait_ge(wcat_ready, n + 1)
                    p.wait_ge(lg_ready, n + 1 + ahead)
                    p.transpose(PWT, wcat[:, :, :].rearrange("p k e -> p (k e)"), ident[:, :]).then_inc(wT_done, 1)

                def bias(q, k, ahead):
                    n = q + (n0 + k)
                    p.wait_ge(wTs_ready, n + 1)
                    p.wait_ge(x1_ready, n + 1 + ahead)
                    p.matmul(PW[:, :, :], wTs[:, :], bblk[:, :, :], start=True, stop=True).then_inc(pb_done, 1)

                def experts(q, k, r):
                    n = q + (n0 + k)
                    n4 = n * R + r
                    if not (isinstance(q, int) and n4 < 2):
                        p.wait_ge(act_part, n4 - 1)
                        pair_sum = (dve_rows(0) + dve_rows(1)) * HALF
                        before = (q + (n0 + k - k % 2)) * (pair_sum // 2)
                        if r >= 2:
                            rows = (dve_rows(0) if k % 2 else 0) + min(r - 1, dve_rows(k))
                        elif k % 2:
                            rows = min(r + R - 1, dve_rows(0))
                        else:
                            rows = min(r + R - 1, dve_rows(1)) - dve_rows(1)
                        p.wait_ge(dve_part, before + rows * HALF)
                    b0, b1 = PY[2 * (r % 2)], PY[2 * (r % 2) + 1]
                    wh = [weh[:, s * HALF:(s + 1) * HALF].rearrange("p e c -> p (e c)") for s in range(2)]
                    wl = [wel[:, s * HALF:(s + 1) * HALF].rearrange("p e c -> p (e c)") for s in range(2)]
                    hi, lo = xTh[:, k % 2, r], xTl[:, k % 2, r]
                    for s, bank in ((0, b0), (1, b1)):
                        p.matmul(bank[:, :], hi, wh[s], start=True, stop=False)
                        p.matmul(bank[:, :], hi, wl[s], start=False, stop=False)
                        ins = p.matmul(bank[:, :], lo, wh[s], start=False, stop=True)
                    ins.then_inc(moe_done, 1)

                def step(t, k, a3, a2, a1, a0):
                    if a0:
                        experts(t, k, 1)
                    if a2:
                        project(t, k + 2)
                    if a1:
                        turn_x(t, k + 1)
                    if a0:
                        experts(t, k, 2)
                    if a1:
                        router(t, k + 1)
                    if a0:
                        experts(t, k, 3)
                        turn_w(t, k, 1 if a1 else 0)
                    if a3:
                        turn_h(t, k + 3)
                    if a0:
                        bias(t, k, 2 if a2 else 1 if a1 else 0)
                    if a1:
                        experts(t, k + 1, 0)

                p.wait_ge(h_lo, m0 + C)
                for k in (-3, -2, -1):
                    step(0, k, True, k > -3, k > -2, False)
                loop(p, 0, Q - 4, 4, lambda t, k: step(t, k, True, True, True, True), pair == 0)
                for k in range(Q - 4, Q):
                    step(0, k, k + 3 < Q, k + 2 < Q, k + 1 < Q, True)


SETUP = {"ABS": 5, "DIAG": 7, "TABLE": 24, "B3": 42, "CVE": 45, "CXN": 46, "CVAL": 54, "CDELTA": 65,
         "CFIX": 67}
S_ABS, S_DIAG, S_TABLE, S_B3, S_CVE, S_CXN, S_CVAL, S_CDELTA, S_CFIX = SETUP.values()
P_ABST, P_MAX, P_COLSUM, P_CXT, P_CW = 1, 2, 3, 4, 5
A_CXT, A_GATES, A_ABS, A_EXPN, A_LN = 2, 4, 6, 7, 8

_INS = ["x", "L0_conv_A_kernel", "L0_conv_B_kernel", "L0_conv_gate_A_kernel", "L0_conv_gate_B_kernel",
        "L0_conv_W_out", "L0_conv_b_out", "L0_ffn_router_w", "L0_ffn_router_b", "L0_ffn_expert_w",
        "L0_ffn_expert_b"]


def kernel(**inputs):
    import numpy as _np
    import concourse.bacc as _bacc
    from concourse import mybir as _mybir
    from concourse.bass_utils import run_bass_kernel_spmd as _run

    nc = _bacc.Bacc("TRN2", target_bir_lowering=False, num_devices=1)
    arrays, args = {}, []
    for name in _INS:
        a = _np.ascontiguousarray(inputs[name])
        arrays[f"in_{name}_dram"] = a
        args.append(nc.dram_tensor(f"in_{name}_dram", a.shape, _mybir.dt.from_np(a.dtype),
                                   kind="ExternalInput").ap())
    args.append(nc.dram_tensor("out_dram", inputs["x"].shape, _mybir.dt.float32, kind="ExternalOutput").ap())
    metaformer_layer(nc, *args)
    r = _run(nc, [arrays], core_ids=[0])
    return r.results[0]["out_dram"]
```
